# Optimizing a Trainium2 kernel written in Bass

```python
import numpy as np
import jax
import jax.numpy as jnp

def _softmax(x, axis=-1):
    return jax.nn.softmax(x, axis=axis)

def _gelu(x):
    return jax.nn.gelu(x, approximate=True)

def _silu(x):
    return jax.nn.silu(x)

def _sigmoid(x):
    return jax.nn.sigmoid(x)

def _layernorm(x, axis=-1, eps=1e-05):
    m = jnp.mean(x, axis=axis, keepdims=True)
    v = jnp.var(x, axis=axis, keepdims=True)
    return (x - m) / jnp.sqrt(v + eps)

def _scatter_add(tgt, idx, src, axis=0):
    return tgt.at[idx].add(src)

def _segment_sum(src, seg, n):
    return jax.ops.segment_sum(src, seg, n)
kernel_name = 'mk_flamingo_gated_d2_seqx_r4_903bdc'

def setup_inputs(seed: int=0):
    np.random.seed(seed)
    _w = jnp.asarray

    def _rec_inputs():
        import jax
        import jax.numpy as jnp
        _rk = jax.random.key(seed)
        x = -0.000125 + 0.9999 * jax.random.normal(jax.random.fold_in(_rk, 1), (4, 512, 512), jnp.float32)
        _lenS = 512 - jax.random.randint(jax.random.fold_in(_rk, 7), (4,), 0, max(1, 512 // 4) + 1, jnp.int32)
        _lenS2 = 64 - jax.random.randint(jax.random.fold_in(_rk, 8), (4,), 0, max(1, 64 // 4) + 1, jnp.int32)
        _ctx_2048P = jax.random.normal(jax.random.fold_in(_rk, 11), (4, 16, 512), jnp.float32)
        _ctx_2048c = jax.random.dirichlet(jax.random.fold_in(_rk, 511), 0.3 * jnp.ones((16,), jnp.float32), (4, 64))
        _ctx_2048t = jnp.einsum('bsk,bkd->bsd', _ctx_2048c, _ctx_2048P)
        _ctx_2048t = _ctx_2048t * jax.lax.rsqrt(jnp.mean(jnp.square(_ctx_2048t)) + 1e-12) * 0.953939
        ctx_2048 = 0.00222621 + 0.99962 * (_ctx_2048t + 0.3 * jax.random.normal(jax.random.fold_in(_rk, 611), (4, 64, 512), jnp.float32))
        itok_Sx4_0_63 = jax.random.randint(jax.random.fold_in(_rk, 12), (512, 4), 0, 64, jnp.int32)
        _g = jax.random.normal(jax.random.fold_in(_rk, 9001), (2, 2), jnp.float32)
        _g = jnp.sign(_g) * jnp.maximum(jnp.abs(_g), 1.0) + (_g == 0) * 1.0
        g_xattn = _g[0]
        g_ffn = _g[1]
        return (x, ctx_2048, itok_Sx4_0_63, g_xattn, g_ffn)
    x, ctx_2048, itok_Sx4_0_63, g_xattn, g_ffn = _rec_inputs()

    def _L0_xattn_setup():
        import math
        import jax, jax.numpy as jnp
        import numpy as np
        B, S, D, N, K, TOPK = (4, 1024, 512, 64, 4, 2)
        key = jax.random.key(seed)
        k0, k1, k2, k3, k4 = jax.random.split(key, 5)
        token_states = jax.random.normal(k0, (B, S, D), dtype=jnp.float32)
        set_states = jax.random.normal(k1, (B, N, D), dtype=jnp.float32)
        desc_router = jax.random.normal(k2, (N, D), dtype=jnp.float32)
        token_to_sets = jax.random.randint(k3, (S, K), 0, N)
        bound = 1.0 / math.sqrt(D)
        W_q = jax.random.uniform(k4, (D, D), jnp.float32, -bound, bound)
        b_q = jnp.zeros((D,), jnp.float32)
        return {'token_states': token_states, 'set_states': set_states, 'desc_router': desc_router, 'W_q': W_q, 'b_q': b_q, 'token_to_sets': token_to_sets}
    _L0_xattn_all = _L0_xattn_setup()
    _L0_xattn_in = {k: v for k, v in _L0_xattn_all.items() if k in ('desc_router', 'W_q', 'b_q')}
    del _L0_xattn_all

    def _L0_ffn_setup():
        import jax, jax.numpy as jnp
        import numpy as np
        E = 32
        K = 6
        H = 512
        I = 256
        T = 512
        CAP = 192
        SCALE = 1.5
        SWIGLU_LIMIT = 10.0
        key = jax.random.key(seed)
        ks = jax.random.split(key, 9)

        def s(k, shape, fan):
            return jax.random.normal(k, shape, jnp.float32) * fan ** (-0.5)
        return {'x': jax.random.normal(ks[0], (1, T, H), jnp.float32), 'gate_w': s(ks[1], (E, H), H), 'bias': jax.random.normal(ks[2], (E,), jnp.float32) * 0.01, 'w_gate': s(ks[3], (E, I, H), H), 'w_up': s(ks[4], (E, I, H), H), 'w_down': s(ks[5], (E, H, I), I), 'sg': s(ks[6], (I, H), H), 'su': s(ks[7], (I, H), H), 'sd': s(ks[8], (H, I), I)}
    _L0_ffn_all = _L0_ffn_setup()
    _L0_ffn_in = {k: v for k, v in _L0_ffn_all.items() if k in ('gate_w', 'bias', 'w_gate', 'w_up', 'w_down', 'sg', 'su', 'sd')}
    del _L0_ffn_all

    def _L1_xattn_setup():
        import math
        import jax, jax.numpy as jnp
        import numpy as np
        HEADS = 16
        MASKED_BIAS = -10000.0

        def _mha(q, k, v):
            B, Sq, D = q.shape
            Sk = k.shape[-2]
            hd = D // HEADS
            qh = q.reshape(B, Sq, HEADS, hd).transpose(0, 2, 1, 3)
            kh = k.reshape(B, Sk, HEADS, hd).transpose(0, 2, 1, 3)
            vh = v.reshape(B, Sk, HEADS, hd).transpose(0, 2, 1, 3)
            scores = jnp.einsum('bhqd,bhkd->bhqk', qh, kh) / math.sqrt(hd)
            qi = jnp.arange(Sq)[:, None] + (Sk - Sq)
            ki = jnp.arange(Sk)[None, :]
            causal = ki <= qi
            scores = jnp.where(causal[None, None], scores, jnp.asarray(MASKED_BIAS, scores.dtype))
            attn = jax.nn.softmax(scores, axis=-1)
            out = jnp.einsum('bhqk,bhkd->bhqd', attn, vh)
            return out.transpose(0, 2, 1, 3).reshape(B, Sq, D)
        key = jax.random.key(seed)
        kq, kk, kv = jax.random.split(key, 3)
        B, S, D = (4, 256, 512)
        q = jax.random.normal(kq, (B, S, D), dtype=jnp.float32)
        k = jax.random.normal(kk, (B, S, D), dtype=jnp.float32)
        v = jax.random.normal(kv, (B, S, D), dtype=jnp.float32)
        return {'q': q, 'k': k, 'v': v}
    _L1_xattn_all = _L1_xattn_setup()
    _L1_xattn_in = {k: v for k, v in _L1_xattn_all.items() if k in ()}
    del _L1_xattn_all

    def _L1_ffn_setup():
        import jax, jax.numpy as jnp
        import numpy as np
        B, S, H, I, E, TOP_K, NS = (2, 512, 512, 352, 8, 2, 2)
        SI = I * NS
        INIT = 0.02
        key = jax.random.key(seed)
        ks = jax.random.split(key, 9)
        f32 = jnp.float32
        return {'hidden_states': jax.random.normal(ks[0], (B, S, H), f32), 'router_w': jax.random.normal(ks[1], (E, H), f32) * INIT, 'gate_w': jax.random.normal(ks[2], (E, H, I), f32) * INIT, 'up_w': jax.random.normal(ks[3], (E, H, I), f32) * INIT, 'down_w': jax.random.normal(ks[4], (E, I, H), f32) * INIT, 's_gate_w': jax.random.normal(ks[5], (H, SI), f32) * INIT, 's_gate_b': jnp.zeros((SI,), f32), 's_up_w': jax.random.normal(ks[6], (H, SI), f32) * INIT, 's_up_b': jnp.zeros((SI,), f32), 's_down_w': jax.random.normal(ks[7], (SI, H), f32) * INIT, 's_down_b': jnp.zeros((H,), f32)}
    _L1_ffn_all = _L1_ffn_setup()
    _L1_ffn_in = {k: v for k, v in _L1_ffn_all.items() if k in ('router_w', 'gate_w', 'up_w', 'down_w', 's_gate_w', 's_gate_b', 's_up_w', 's_up_b', 's_down_w', 's_down_b')}
    del _L1_ffn_all
    return {'x': x, 'ctx_2048': ctx_2048, 'itok_Sx4_0_63': itok_Sx4_0_63, 'g_xattn': g_xattn, 'g_ffn': g_ffn, 'L0_xattn_desc_router': _L0_xattn_in['desc_router'], 'L0_xattn_W_q': _L0_xattn_in['W_q'], 'L0_xattn_b_q': _L0_xattn_in['b_q'], 'L0_ffn_gate_w': _L0_ffn_in['gate_w'], 'L0_ffn_bias': _L0_ffn_in['bias'], 'L0_ffn_w_gate': _L0_ffn_in['w_gate'], 'L0_ffn_w_up': _L0_ffn_in['w_up'], 'L0_ffn_w_down': _L0_ffn_in['w_down'], 'L0_ffn_sg': _L0_ffn_in['sg'], 'L0_ffn_su': _L0_ffn_in['su'], 'L0_ffn_sd': _L0_ffn_in['sd'], 'L1_ffn_router_w': _L1_ffn_in['router_w'], 'L1_ffn_gate_w': _L1_ffn_in['gate_w'], 'L1_ffn_up_w': _L1_ffn_in['up_w'], 'L1_ffn_down_w': _L1_ffn_in['down_w'], 'L1_ffn_s_gate_w': _L1_ffn_in['s_gate_w'], 'L1_ffn_s_gate_b': _L1_ffn_in['s_gate_b'], 'L1_ffn_s_up_w': _L1_ffn_in['s_up_w'], 'L1_ffn_s_up_b': _L1_ffn_in['s_up_b'], 'L1_ffn_s_down_w': _L1_ffn_in['s_down_w'], 'L1_ffn_s_down_b': _L1_ffn_in['s_down_b']}

def reference(x, ctx_2048, itok_Sx4_0_63, g_xattn, g_ffn, L0_xattn_desc_router, L0_xattn_W_q, L0_xattn_b_q, L0_ffn_gate_w, L0_ffn_bias, L0_ffn_w_gate, L0_ffn_w_up, L0_ffn_w_down, L0_ffn_sg, L0_ffn_su, L0_ffn_sd, L1_ffn_router_w, L1_ffn_gate_w, L1_ffn_up_w, L1_ffn_down_w, L1_ffn_s_gate_w, L1_ffn_s_gate_b, L1_ffn_s_up_w, L1_ffn_s_up_b, L1_ffn_s_down_w, L1_ffn_s_down_b):
    import jax
    import jax.numpy as jnp

    def _L0_xattn_ref(token_states, set_states, desc_router, W_q, b_q, token_to_sets):
        import math
        import jax, jax.numpy as jnp
        import numpy as np
        B, S, D, N, K, TOPK = (4, 1024, 512, 64, 4, 2)
        batch, seq_len, d = token_states.shape
        num_sets = set_states.shape[1]
        scale = 1.0 / math.sqrt(d)
        q = jnp.einsum('bsd,ed->bse', token_states, W_q) + b_q
        scores = jnp.einsum('bse,ne->bsn', q, desc_router) * scale
        valid = token_to_sets >= 0
        mask = ((token_to_sets[:, :, None] == jnp.arange(num_sets)[None, None, :]) & valid[:, :, None]).any(axis=1)
        neg_inf = jnp.array(-jnp.inf, scores.dtype)
        scores = jnp.where(mask[None, :, :], scores, neg_inf)
        topk_vals, topk_idx = jax.lax.top_k(scores, TOPK)
        b_i = jnp.arange(batch)[:, None, None]
        s_i = jnp.arange(seq_len)[None, :, None]
        scores = jnp.full_like(scores, neg_inf).at[b_i, s_i, topk_idx].set(topk_vals)
        weights = jax.nn.softmax(scores, axis=-1)
        return jnp.einsum('bsn,bnd->bsd', weights, set_states)

    def _L0_ffn_ref(x, gate_w, bias, w_gate, w_up, w_down, sg, su, sd):
        import jax, jax.numpy as jnp
        import numpy as np
        E = 32
        K = 6
        H = 512
        I = 256
        T = 512
        CAP = 192
        SCALE = 1.5
        SWIGLU_LIMIT = 10.0
        B, S, Hd = x.shape
        h = x.reshape(-1, Hd)
        logits = h @ gate_w.T
        scores = jnp.sqrt(jax.nn.softplus(logits))
        _, topk_idx = jax.lax.top_k(scores + bias[None, :], K)
        topk_w = jnp.take_along_axis(scores, topk_idx, axis=1)
        topk_w = topk_w / jnp.sum(topk_w, axis=-1, keepdims=True)
        topk_w = topk_w * SCALE
        eid = topk_idx.reshape(-1)
        onehot = jax.nn.one_hot(eid, E, dtype=jnp.int32)
        pos = jnp.cumsum(onehot, axis=0) - 1
        pos = jnp.take_along_axis(pos, eid[:, None], axis=1)[:, 0]
        valid = pos < CAP
        pos = jnp.where(valid, pos, CAP)
        h_rep = jnp.repeat(h, K, axis=0)
        xb = jnp.zeros((E, CAP + 1, Hd), x.dtype).at[eid, pos].set(h_rep)
        g = jnp.einsum('ech,eih->eci', xb, w_gate)
        u = jnp.einsum('ech,eih->eci', xb, w_up)
        inter = jax.nn.silu(g) * u
        yb = jnp.einsum('eci,ehi->ech', inter, w_down)
        w_slot = jnp.where(valid, topk_w.reshape(-1), 0.0)
        y = yb[eid, pos] * w_slot[:, None]
        routed = y.reshape(-1, K, Hd).sum(axis=1)
        si = jax.nn.silu(h @ sg.T) * (h @ su.T)
        si = jnp.clip(si, -SWIGLU_LIMIT, SWIGLU_LIMIT)
        shared = si @ sd.T
        return (routed + shared).reshape(B, S, Hd)

    def _L1_xattn_ref(q, k, v):
        import math
        import jax, jax.numpy as jnp
        import numpy as np
        HEADS = 16
        MASKED_BIAS = -10000.0

        def _mha(q, k, v):
            B, Sq, D = q.shape
            Sk = k.shape[-2]
            hd = D // HEADS
            qh = q.reshape(B, Sq, HEADS, hd).transpose(0, 2, 1, 3)
            kh = k.reshape(B, Sk, HEADS, hd).transpose(0, 2, 1, 3)
            vh = v.reshape(B, Sk, HEADS, hd).transpose(0, 2, 1, 3)
            scores = jnp.einsum('bhqd,bhkd->bhqk', qh, kh) / math.sqrt(hd)
            qi = jnp.arange(Sq)[:, None] + (Sk - Sq)
            ki = jnp.arange(Sk)[None, :]
            causal = ki <= qi
            scores = jnp.where(causal[None, None], scores, jnp.asarray(MASKED_BIAS, scores.dtype))
            attn = jax.nn.softmax(scores, axis=-1)
            out = jnp.einsum('bhqk,bhkd->bhqd', attn, vh)
            return out.transpose(0, 2, 1, 3).reshape(B, Sq, D)
        return _mha(q, k, v)

    def _L1_ffn_ref(hidden_states, router_w, gate_w, up_w, down_w, s_gate_w, s_gate_b, s_up_w, s_up_b, s_down_w, s_down_b):
        import jax, jax.numpy as jnp
        import numpy as np
        B, S, H, I, E, TOP_K, NS = (2, 512, 512, 352, 8, 2, 2)
        SI = I * NS
        INIT = 0.02
        b, s, h = hidden_states.shape
        x = hidden_states.reshape(-1, h)
        T = x.shape[0]
        num_experts = router_w.shape[0]
        logits = x @ router_w.T
        probs = jax.nn.softmax(logits.astype(jnp.float32), axis=-1)
        topk_w, topk_idx = jax.lax.top_k(probs, TOP_K)
        topk_w = topk_w / jnp.sum(topk_w, axis=-1, keepdims=True)
        combine = jnp.zeros((T, num_experts), probs.dtype)
        combine = combine.at[jnp.arange(T)[:, None], topk_idx].add(topk_w)

        def expert_step(acc, ws):
            gw, uw, dw, ce = ws
            out = jax.nn.silu(x @ gw) * (x @ uw) @ dw
            return (acc + ce[:, None].astype(out.dtype) * out, None)
        moe_out, _ = jax.lax.scan(expert_step, jnp.zeros_like(x), (gate_w, up_w, down_w, combine.T))
        shared = jax.nn.silu(x @ s_gate_w + s_gate_b) * (x @ s_up_w + s_up_b) @ s_down_w + s_down_b
        return (moe_out + shared).reshape(b, s, h)
    x = x + jnp.tanh(g_xattn[0]) * _L0_xattn_ref(_layernorm(x, axis=-1), ctx_2048, L0_xattn_desc_router, L0_xattn_W_q, L0_xattn_b_q, itok_Sx4_0_63)
    x = x + jnp.tanh(g_ffn[0]) * _L0_ffn_ref(_layernorm(x, axis=-1), L0_ffn_gate_w, L0_ffn_bias, L0_ffn_w_gate, L0_ffn_w_up, L0_ffn_w_down, L0_ffn_sg, L0_ffn_su, L0_ffn_sd)
    x = x + jnp.tanh(g_xattn[1]) * _L1_xattn_ref(_layernorm(x, axis=-1), ctx_2048, ctx_2048)
    x = x + jnp.tanh(g_ffn[1]) * _L1_ffn_ref(_layernorm(x, axis=-1), L1_ffn_router_w, L1_ffn_gate_w, L1_ffn_up_w, L1_ffn_down_w, L1_ffn_s_gate_w, L1_ffn_s_gate_b, L1_ffn_s_up_w, L1_ffn_s_up_b, L1_ffn_s_down_w, L1_ffn_s_down_b)
    return x

_drawn_inputs = setup_inputs


def setup_inputs(seed=0):
    import zlib

    import numpy as np

    out = dict(_drawn_inputs(seed))
    spreads = {'g_ffn': (-1.0, 0.6),
     'L0_xattn_b_q': (0.0, 0.1),
     'L1_ffn_s_gate_b': (0.0, 0.8),
     'L1_ffn_s_up_b': (0.0, 0.8),
     'L1_ffn_s_down_b': (0.0, 0.1)}
    factors = {'L1_ffn_router_w': 3.234,
     'L1_ffn_gate_w': 2.865,
     'L1_ffn_up_w': 2.816,
     'L1_ffn_down_w': 2.805}
    for name, (base, spread) in spreads.items():
        noise = np.random.default_rng([zlib.crc32(name.encode()), seed]).standard_normal(out[name].shape)
        drawn = base * np.exp(spread * noise) if base else spread * noise
        out[name] = jnp.asarray(drawn.astype(out[name].dtype))
    for name, factor in factors.items():
        out[name] = (out[name] * factor).astype(out[name].dtype)
    return out
```

```python
import numpy as np
import concourse.bass as bass
from concourse import mybir
from contextlib import ExitStack

F32 = mybir.dt.float32
I32 = mybir.dt.int32
U32 = mybir.dt.uint32
ALU = mybir.AluOpType
ACT = mybir.ActivationFunctionType
AX = mybir.AxisListType

T = 16
D = 512
E0, K0, I0, CAP = 32, 6, 256, 192
HALF = CAP // 2
E1, K1, I1, SI = 8, 2, 352, 704
NT = 39
WE0 = 3072
WE1 = 4352
ROWS = 2176
TRASH0 = E0 * CAP

C_ID, C_U, C_ONE, C_IOTA, C_TOK, C_TR, C_CM, C_CA, C_I39 = 0, 128, 256, 384, 448, 464, 560, 624, 688
C_INV = 688 + NT * 8
NCONST = C_INV + 128


def constants():
    c = np.zeros((128, NCONST), np.float32)
    p = np.arange(128)
    c[:, C_ID:C_ID + 128] = np.eye(128)
    c[:, C_U:C_U + 128] = (p[:, None] < p[None, :])
    c[:, C_ONE:C_ONE + 128] = 1.0
    c[:, C_IOTA:C_IOTA + 64] = np.arange(64)
    c[:, C_TOK:C_TOK + T] = p[:, None] + 128 * np.arange(T)
    c[:, C_TR:C_TR + T * K0] = TRASH0 + p[:, None] + 128 * np.arange(T * K0)
    allowed = np.arange(64)[None, :] <= (p[:, None] - 64)
    c[:, C_CM:C_CM + 64] = allowed * (32.0 ** -0.5)
    c[:, C_CA:C_CA + 64] = np.where(allowed, 0.0, -10000.0)
    c[:, C_I39:C_I39 + NT * 8] = np.repeat(np.arange(NT), 8)
    c[:, C_INV:C_INV + 128] = 1.0 / 64
    l0 = np.zeros((TRASH0, 2), np.float32)
    l0[:, 0] = 2048 + np.arange(TRASH0) % HALF
    l1 = np.zeros((NT * 128, 2), np.float32)
    l1[:, 0] = 2048 + np.arange(NT * 128) % 128
    return c, l0, l1


class Engine:

    def __init__(self, sem, chain=False):
        self.sem, self.count, self.todo, self.chain = sem, 0, [], chain

    def op(self, fn, *waits, sig=True):
        if self.chain and self.count:
            waits = (*waits, (self.sem, self.count))
        if sig:
            self.count += 1
        self.todo.append((fn, waits, (self.sem, 1) if sig else None))
        return (self.sem, self.count)

    def play(self, eng):
        seen = {}
        for fn, waits, sig in self.todo:
            for w in waits:
                if w is None:
                    continue
                s, v = w
                if seen.get(s.name, 0) < v:
                    eng.wait_ge(s, v)
                    seen[s.name] = v
            ins = fn(eng)
            if sig:
                ins.then_inc(*sig)


class Landing:

    def __init__(self, sem):
        self.sem, self.count = sem, 0

    def dma(self, q, fn, *waits):
        self.count += 16
        q.todo.append((fn, waits, (self.sem, 16)))
        return (self.sem, self.count)


def program(nc, a, out):
    with ExitStack() as ctx:
        big = ctx.enter_context(nc.sbuf_tensor("big", [128, 53120], F32))
        PB = [ctx.enter_context(nc.psum_tensor(f"pb{i}", [128, 512], F32)) for i in range(8)]

        def sem(name):
            return ctx.enter_context(nc.semaphore(name))

        def land(name):
            return Landing(sem(name))

        pe, act, dve, pool, sp = (Engine(sem(n), n in ("s_act", "s_dve")) for n in ("s_pe", "s_act", "s_dve", "s_pool", "s_sp"))
        HN = nc.dram_tensor("hn_rows", [ROWS, D], F32, kind="Internal").ap()
        HN2 = nc.dram_tensor("hn2_rows", [ROWS, D], F32, kind="Internal").ap()
        ACC = nc.dram_tensor("acc_rows", [ROWS, D], F32, kind="Internal").ap()
        ACC2 = nc.dram_tensor("acc2_rows", [ROWS, D], F32, kind="Internal").ap()
        LIST0 = nc.dram_tensor("list0_rows", [TRASH0 + T * K0 * 128, 2], F32, kind="Internal").ap()
        LIST1 = nc.dram_tensor("list1_rows", [NT * 128, 2], F32, kind="Internal").ap()

        def S(off, *shape, p0=0, p1=128):
            n = int(np.prod(shape))
            v = big[p0:p1, off:off + n]
            if len(shape) == 2:
                v = v.rearrange("p (a b) -> p a b", a=shape[0])
            if len(shape) == 3:
                v = v.rearrange("p (a b c) -> p a b c", a=shape[0], b=shape[1])
            return v

        X = S(17408, T, D)
        WR = [S(WE0 * i, WE0) for i in range(2)]
        SW0 = S(6144, WE0)
        WQ = S(9216, 4, D)
        OH = 11264
        TMP = 14336
        INT0 = [S(25600 + 1024 * i, 2, D) for i in range(2)]
        G = [S(27648 + 512 * i, D, p1=HALF) for i in range(4)]
        XT = [S(29696 + 768 * i, 4, CAP) for i in range(2)]
        IN0 = [S(31232 + 384 * i, 2, CAP) for i in range(2)]
        SL0 = [S(32000 + 384 * i, 2, CAP) for i in range(2)]
        YS = [S(32768 + 512 * i, D, p1=HALF) for i in range(4)]
        INT1 = [25600 + 3072 * i for i in range(2)]
        SWD = S(31744, 6, D)
        W1 = S(0, E1 * WE1)
        at = [E1 * WE1]

        def take(*shape, p1=128):
            o = at[0]
            at[0] += int(np.prod(shape))
            return S(o, *shape, p1=p1)

        CON = take(NCONST)
        CTX = take(4, D)
        hoff = at[0]
        HT = take(4, T * 128)
        SGU = take(2, 4, SI)
        goff = at[0] - 2 * 4 * SI
        MV = take(T, 2)
        RS = take(T)
        TG = take(4)
        GVAL = take(4)
        IDS = take(64)
        WSL = take(64)
        MX = take(T, 8)
        MI = take(T, 8).bitcast(U32)
        RW1 = take(4, E1)
        SMALL = at[0]
        assert at[0] + 400 <= 53120, at[0]
        ident = CON[:, C_ID:C_ID + 128]

        g = [goff]

        def take0(*shape, p1=128):
            o = g[0]
            g[0] += int(np.prod(shape))
            assert g[0] <= goff + 5632
            return S(o, *shape, p1=p1)

        XN = [take0(D) for _ in range(3)]
        HTA = [take0(4, 128) for _ in range(2)]
        SC = take0(T, 64)
        WT = take0(D, p1=64)
        DT = take0(4, 64)
        MSB = take0(4, 64)
        CB = take0(64)
        BQ = take0(4)
        ITI = take0(4, 4).bitcast(I32)
        ITF = take0(4, 4)
        NEG = take0(4, 64)
        RW0 = take0(4, E0)
        ST = take0(6)

        block = ctx.enter_context(nc.Block())
        l_con, l_w, l_x = land("l_con"), land("l_w"), [land(f"l_x{i}") for i in range(4)]
        l_xn = [land(f"l_xn{i}") for i in range(3)]
        l_init = land("l_init")

        def load(l, q, dst, src, *waits):
            return l.dma(q, lambda e: e.dma_start(dst, src), *waits)

        l_it = land("l_it")
        for b in range(4):
            tx = load(l_x[b], sp, X[:, 4 * b:4 * b + 4, :], a["x"][b].rearrange("(t p) d -> p t d", p=128))
        load(l_con, act, CON, a["con"])
        load(l_w, act, WQ, a["wq"].rearrange("(k p) d -> p k d", p=128))
        load(l_w, act, DT, a["descT"].rearrange("(k p) n -> p k n", p=128))
        load(l_w, act, BQ, a["bq"])
        load(l_con, act, GVAL, a["g"])
        t_w = load(l_w, act, RW0, a["rw0"].rearrange("(k p) n -> p k n", p=128))
        load(l_con, act, CTX[0:64], a["ctx"].rearrange("b s d -> s b d"))
        t_con = load(l_con, act, CTX[64:128], a["ctx"].rearrange("b s d -> s b d"))
        t_it = load(l_it, sp, ITI, a["itok"].rearrange("(t p) k -> p t k", p=128))
        load(l_init, sp, LIST0[0:TRASH0, :].rearrange("(a b) c -> a (b c)", a=64), a["l0"].rearrange("(a b) c -> a (b c)", a=64))
        load(l_init, sp, LIST1.rearrange("(a b) c -> a (b c)", a=39), a["l1"].rearrange("(a b) c -> a (b c)", a=39))
        for tab in (HN, HN2, ACC, ACC2):
            t_init = load(l_init, sp, tab[2048:ROWS, :], a["zero"])

        t_tg = act.op(lambda e: e.activation(TG, GVAL, ACT.Tanh), t_con)

        def mrows(e):
            for m in range(4):
                for k in range(4):
                    i = e.matmul(PB[6][:, m * 64:(m + 1) * 64], WQ[:, k, m * 128:(m + 1) * 128], DT[:, k, :],
                                 start=(k == 0), stop=(k == 3))
            return i
        t_m = pe.op(mrows, t_w)
        t_msb = dve.op(lambda e: e.tensor_copy(MSB.rearrange("p a b -> p (a b)"), PB[6][:, 0:256]), t_m)
        BQB = S(TMP, 4, 128)
        t_bq = dve.op(lambda e: e.tensor_copy(BQB, BQ.unsqueeze(2).broadcast_to([128, 4, 128])), t_w)

        def cbrow(e):
            for k in range(4):
                i = e.matmul(PB[7][:, 0:64], BQB[:, k, :], DT[:, k, :], start=(k == 0), stop=(k == 3))
            return i
        t_cb = pe.op(cbrow, t_bq, t_w)
        QS = float(D) ** -0.5
        t_cb = dve.op(lambda e: e.tensor_scalar(CB, PB[7][:, 0:64], QS, None, ALU.mult), t_cb)
        t = dve.op(lambda e: e.tensor_copy(ITF, ITI), t_it)
        TM = S(TMP + 512, 4, 64)
        io4 = CON[:, C_IOTA:C_IOTA + 64].unsqueeze(1).broadcast_to([128, 4, 64])
        for k in range(4):
            dst = NEG if k == 0 else TM
            t = dve.op(lambda e, k=k, dst=dst: e.tensor_tensor(dst, io4, ITF[:, :, k:k + 1].broadcast_to([128, 4, 64]), ALU.is_equal), t, t_con)
            if k:
                t = dve.op(lambda e: e.tensor_tensor(NEG, NEG, TM, ALU.max), t)
        t_neg = dve.op(lambda e: e.tensor_scalar(NEG, NEG, 1.0, 1e30, ALU.subtract, ALU.mult), t)

        def ln_stats(b, src_t):
            for i in range(4 * b, 4 * b + 4):
                t = dve.op(lambda e, i=i: e.bn_stats(ST, X[:, i, :]), *src_t)
                t = dve.op(lambda e, i=i: e.bn_aggr(MV[:, i, :], ST), t)
            t = dve.op(lambda e: e.tensor_scalar(RS[:, 4 * b:4 * b + 4], MV[:, 4 * b:4 * b + 4, 1], 1e-5, None, ALU.add), t)
            t = act.op(lambda e: e.activation(RS[:, 4 * b:4 * b + 4], RS[:, 4 * b:4 * b + 4], ACT.Sqrt), t)
            return dve.op(lambda e: e.reciprocal(RS[:, 4 * b:4 * b + 4], RS[:, 4 * b:4 * b + 4]), t)

        def norm(i, dst, *waits):
            return dve.op(lambda e: e.tensor_scalar(dst, X[:, i, :], MV[:, i, 0:1], RS[:, i:i + 1], ALU.subtract, ALU.mult), *waits)

        def flip(i, src, ps, *waits):
            def f(e):
                for k in range(4):
                    r = e.transpose(ps[:, k * 128:(k + 1) * 128], src[:, k * 128:(k + 1) * 128], ident)
                return r
            return pe.op(f, t_con, *waits)

        ht_free = [None, None]
        ps_free = [t_msb, t_cb]
        pst_free = [None, None]
        xn_free = [None] * 3
        t_sc = [None] * 16
        pend = None

        def scores(i, t_ht):
            def f(e):
                for k in range(4):
                    r = e.matmul(PB[6 + i % 2][:, 0:64], HTA[i % 2][:, k, :], MSB[:, k, :], start=(k == 0), stop=(k == 3))
                return r
            t = pe.op(f, t_ht, t_msb, ps_free[i % 2])
            ht_free[i % 2] = t
            t = dve.op(lambda e: e.scalar_tensor_tensor(out=SC[:, i, :], in0=PB[6 + i % 2][:, 0:64], scalar=QS, in1=CB, op0=ALU.mult, op1=ALU.add), t, t_cb)
            ps_free[i % 2] = t
            t_sc[i] = t

        for b in range(4):
            t_rs = ln_stats(b, [(l_x[b].sem, 16)])
            for i in range(4 * b, 4 * b + 4):
                t_n = norm(i, XN[i % 3], t_rs, xn_free[i % 3])
                t_f = flip(i, XN[i % 3], PB[i % 2], t_n, pst_free[i % 2])
                xn_free[i % 3] = t_f
                t_h = act.op(lambda e, i=i: e.activation(HTA[i % 2].rearrange("p a b -> p (a b)"), PB[i % 2][:, :], ACT.Copy), t_f, ht_free[i % 2])
                pst_free[i % 2] = t_h
                if pend:
                    scores(*pend)
                pend = (i, t_h)
        scores(*pend)

        P12 = take0(4, 2)
        wt_free = None
        pmx_free = [pst_free[0], pst_free[1]]
        t_x1 = [None] * 16
        WTS = S(OH, 4, 64)
        WTS2 = S(OH + 256, 4, 64)
        IDF = S(OH + 512, 4, 8)
        t_wt = None
        for b in range(4):
            s = slice(4 * b, 4 * b + 4)
            t = dve.op(lambda e, s=s: e.tensor_tensor(SC[:, s, :], SC[:, s, :], NEG, ALU.add), t_neg, t_sc[4 * b + 3])
            for i in range(4 * b, 4 * b + 4):
                t2 = dve.op(lambda e, i=i: e.max(MX[:, i, :], SC[:, i, :]), t)
                t3 = dve.op(lambda e, i=i: e.max_index(MI[:, i, :], MX[:, i, :], SC[:, i, :]), t2)
            t = dve.op(lambda e, s=s: e.tensor_tensor(P12[:, :, 0:1], MX[:, s, 1:2], MX[:, s, 0:1], ALU.subtract), t2)
            t = act.op(lambda e: e.activation(P12[:, :, 1:2], P12[:, :, 0:1], ACT.Exp), t)
            t = dve.op(lambda e: e.tensor_scalar(P12[:, :, 0:1], P12[:, :, 1:2], 1.0, None, ALU.add), t)
            t = dve.op(lambda e: e.reciprocal(P12[:, :, 0:1], P12[:, :, 0:1]), t)
            t = dve.op(lambda e: e.tensor_tensor(P12[:, :, 1:2], P12[:, :, 1:2], P12[:, :, 0:1], ALU.mult), t)
            tp = t
            ti = dve.op(lambda e, s=s: e.tensor_copy(IDF, MI[:, s, :]), t3)
            for j, dst in ((0, WTS), (1, WTS2)):
                t = dve.op(lambda e, j=j, dst=dst: e.tensor_tensor(dst, io4, IDF[:, :, j:j + 1].broadcast_to([128, 4, 64]), ALU.is_equal), ti, t_wt)
                t = dve.op(lambda e, j=j, dst=dst: e.tensor_tensor(dst, dst, P12[:, :, j:j + 1].broadcast_to([128, 4, 64]), ALU.mult), t, tp)
            t = dve.op(lambda e: e.tensor_tensor(WTS, WTS, WTS2, ALU.add), t)

            def fw(e):
                for j in range(4):
                    r = e.transpose(PB[5][0:64, j * 128:(j + 1) * 128], WTS[:, j, :], ident)
                return r
            t_wt = pe.op(fw, t, wt_free)
            t = act.op(lambda e: e.activation(WT, PB[5][0:64, :], ACT.Copy), t_wt, t_x1[4 * b - 1] if b else None)
            wt_free = t
            for i in range(4 * b, 4 * b + 4):
                tm = pe.op(lambda e, i=i, b=b: e.matmul(PB[i % 2][:, :], WT[:, (i % 4) * 128:(i % 4 + 1) * 128], CTX[0:64, b, :], start=True, stop=True),
                           t, pmx_free[i % 2])
                t_x1[i] = dve.op(lambda e, i=i: e.scalar_tensor_tensor(out=X[:, i, :], in0=PB[i % 2][:, :], scalar=TG[:, 0:1], in1=X[:, i, :], op0=ALU.mult, op1=ALU.add), tm, t_tg)
                pmx_free[i % 2] = t_x1[i]

        def ln_rows(table, rw, ne, xn, xn_free, t_src, t_rw, ps_t, psl, extra=None):
            pst = list(ps_t)
            t_hn, pend = None, None
            done = []
            for b in range(4):
                t_rs = ln_stats(b, t_src(b))
                for i in range(4 * b, 4 * b + 4):
                    t_n = norm(i, xn[i % 3], t_rs, *xn_free[i % 3])
                    t_f = flip(i, xn[i % 3], PB[i % 2], t_n, pst[i % 2])
                    t_d = load(l_xn[i % 3], sp, table[i * 128:(i + 1) * 128, :], xn[i % 3], t_n)
                    xn_free[i % 3] = [t_f, t_d]
                    src = PB[i % 2][:, :].rearrange("p (k t) -> p k t", k=4)
                    t_h = act.op(lambda e, i=i, src=src: e.activation(HT[:, :, i * 128:(i + 1) * 128], src, ACT.Copy), t_f, extra)
                    pst[i % 2] = t_h

                    def lg(e, i=i):
                        for k in range(4):
                            r = e.matmul(psl[:, i * ne:(i + 1) * ne], HT[:, k, i * 128:(i + 1) * 128], rw[:, k, :], start=(k == 0), stop=(k == 3))
                        return r
                    if pend:
                        pend()
                    done.append(None)

                    def pend(lg=lg, t_h=t_h, i=i):
                        done[i] = pe.op(lg, t_h, t_rw)
            pend()
            rows = [(l.sem, l.count) for l in l_xn]
            return done, t_h, rows

        done0, t_ht, t_rows0 = ln_rows(HN, RW0, E0, XN, [[x] for x in xn_free], lambda b: [t_x1[4 * b + 3]], t_w,
                                       [pmx_free[0], pmx_free[1]], PB[6], None)

        l_sc = land("l_sc0")

        def route(ne, kk, sel, val, wscale, factor, t_sel, oh, tmp, lists, psa, psb, small, layer):
            n = T * ne
            OHv = S(oh, T, kk * ne).rearrange("p t (k e) -> p t k e", k=kk)
            TMv = S(tmp, T, kk * ne).rearrange("p t (k e) -> p t k e", k=kk)
            o = [small]

            def tk(*sh):
                q = o[0]
                o[0] += int(np.prod(sh))
                return S(q, *sh)
            IDX, WK, REC, DEN, ADR, VA = tk(T, 8), tk(T, kk), tk(T, kk, 2), tk(T, 1), tk(T, kk), tk(T, kk)
            ADI = tk(T, kk).bitcast(I32)
            MS, CA, CC = tk(T, ne), tk(T, ne), tk(T, ne)
            for i in range(T):
                t = dve.op(lambda e, i=i: e.max(MX[:, i, :], sel[:, i, :]), t_sel)
                t = dve.op(lambda e, i=i: e.max_index(MI[:, i, :], MX[:, i, :], sel[:, i, :]), t)
            t = dve.op(lambda e: e.tensor_copy(IDX, MI), t)
            sh = [128, T, kk, ne]
            iob = CON[:, C_IOTA:C_IOTA + ne].unsqueeze(1).unsqueeze(1).broadcast_to(sh)
            t_oh = dve.op(lambda e: e.tensor_tensor(OHv, iob, IDX[:, :, 0:kk].unsqueeze(3).broadcast_to(sh), ALU.is_equal), t)
            t_ms = dve.op(lambda e: e.tensor_reduce(MS, OHv.rearrange("p t k e -> p t e k"), AX.X, ALU.add), t_oh)

            def cnt(e):
                e.matmul(psa[:, 0:n], CON[:, C_U:C_U + 128], MS.rearrange("p t e -> p (t e)"), start=True, stop=True)
                return e.matmul(psb[:, 0:n], CON[:, C_ONE:C_ONE + 128], MS.rearrange("p t e -> p (t e)"), start=True, stop=True)
            t_cnt = pe.op(cnt, t_ms, t_con, t_sel)
            t = dve.op(lambda e: e.tensor_tensor(TMv, OHv, val.unsqueeze(2).broadcast_to(sh), ALU.mult), t_oh)
            t = dve.op(lambda e: e.tensor_reduce(WK, TMv, AX.X, ALU.add), t)
            t = dve.op(lambda e: e.tensor_reduce(DEN, WK, AX.X, ALU.add), t)
            t = dve.op(lambda e: e.reciprocal(DEN, DEN), t)
            t = dve.op(lambda e: e.tensor_scalar(DEN, DEN, wscale, factor, ALU.mult, ALU.mult), t, t_tg)
            t = dve.op(lambda e: e.tensor_tensor(REC[:, :, :, 1], WK, DEN.broadcast_to([128, T, kk]), ALU.mult), t)
            t_rec = dve.op(lambda e: e.tensor_copy(REC[:, :, :, 0], CON[:, C_TOK:C_TOK + T].unsqueeze(2).broadcast_to([128, T, kk])), t)
            t = dve.op(lambda e: e.tensor_copy(CA.rearrange("p t e -> p (t e)"), psb[:, 0:n]), t_cnt)
            cur, oth = CA, CC
            for st in (1, 2, 4, 8):
                t2 = dve.op(lambda e, st=st, cur=cur, oth=oth: e.tensor_copy(oth[:, 0:st, :], cur[:, 0:st, :]), t)
                t = dve.op(lambda e, st=st, cur=cur, oth=oth: e.tensor_tensor(oth[:, st:T, :], cur[:, st:T, :], cur[:, 0:T - st, :], ALU.add), t)
                t = (t if t[1] > t2[1] else t2)
                cur, oth = oth, cur
            t_base = None
            if layer == 1:
                NB, NC, NI = tk(8), tk(8), tk(8).bitcast(I32)
                CMP, ETF, ETI = tk(NT, 8), tk(NT), tk(NT).bitcast(I32)
                t3 = dve.op(lambda e: e.tensor_scalar(NB, cur[:, T - 1, :], 127.0, None, ALU.add), t)
                t3 = dve.op(lambda e: e.tensor_copy(NI, NB), t3)
                t3 = dve.op(lambda e: e.tensor_scalar(NI, NI, 7, None, ALU.logical_shift_right), t3)
                t3 = dve.op(lambda e: e.tensor_copy(NB, NI), t3)
                c2, o2 = NB, NC
                NTL = tk(8)
                t3 = dve.op(lambda e: e.tensor_copy(NTL, NB), t3)
                for st in (1, 2, 4):
                    t3 = dve.op(lambda e, st=st, c2=c2, o2=o2: e.tensor_copy(o2[:, 0:st], c2[:, 0:st]), t3)
                    t3 = dve.op(lambda e, st=st, c2=c2, o2=o2: e.tensor_tensor(o2[:, st:8], c2[:, st:8], c2[:, 0:8 - st], ALU.add), t3)
                    c2, o2 = o2, c2
                t4 = dve.op(lambda e: e.tensor_tensor(CMP, CON[:, C_I39:C_I39 + NT * 8].rearrange("p (a b) -> p a b", b=8),
                                                     c2.unsqueeze(1).broadcast_to([128, NT, 8]), ALU.is_ge), t3)
                t4 = dve.op(lambda e: e.tensor_reduce(ETF, CMP[:, :, 0:7], AX.X, ALU.add), t4)
                t4 = dve.op(lambda e: e.tensor_scalar(ETF, ETF, float(WE1), None, ALU.mult), t4)
                t_et = dve.op(lambda e: e.tensor_copy(ETI, ETF), t4)
                t3 = dve.op(lambda e: e.tensor_tensor(NTL, c2, NTL, ALU.subtract), t3)
                t_base = dve.op(lambda e: e.tensor_scalar(NTL, NTL, 128.0, None, ALU.mult), t3)
            t = dve.op(lambda e: e.tensor_tensor(oth.rearrange("p t e -> p (t e)"), cur.rearrange("p t e -> p (t e)"), psb[:, 0:n], ALU.subtract), t)
            t = dve.op(lambda e: e.tensor_tensor(oth.rearrange("p t e -> p (t e)"), oth.rearrange("p t e -> p (t e)"), psa[:, 0:n], ALU.add), t)
            if layer == 1:
                t = dve.op(lambda e: e.tensor_tensor(oth, oth, NTL.unsqueeze(1).broadcast_to([128, T, 8]), ALU.add), t, t_base)
            t = dve.op(lambda e: e.tensor_tensor(TMv, OHv, oth.unsqueeze(2).broadcast_to(sh), ALU.mult), t)
            t = dve.op(lambda e: e.tensor_reduce(ADR, TMv, AX.X, ALU.add), t)
            if layer == 0:
                t2 = dve.op(lambda e: e.tensor_scalar(VA, ADR, float(CAP), None, ALU.is_lt), t)
                t = dve.op(lambda e: e.scalar_tensor_tensor(out=ADR, in0=IDX[:, :, 0:kk], scalar=float(CAP), in1=ADR, op0=ALU.mult, op1=ALU.add), t2)
                tr = CON[:, C_TR:C_TR + T * kk].rearrange("p (t k) -> p t k", k=kk)
                t = dve.op(lambda e: e.tensor_tensor(ADR, ADR, tr, ALU.subtract), t)
                t = dve.op(lambda e: e.tensor_tensor(ADR, ADR, VA, ALU.mult), t)
                t = dve.op(lambda e: e.tensor_tensor(ADR, ADR, tr, ALU.add), t)
            t = dve.op(lambda e: e.tensor_copy(ADI, ADR), t)
            for i in range(T):
                for k in range(kk):
                    t_s = l_sc.dma(pool, lambda e, i=i, k=k: e.indirect_dma_start(
                        lists, bass.IndirectOffsetOnAxis(ap=ADI[:, i, k:k + 1], axis=0), REC[:, i, k, :], None), t, t_rec, t_init)
            if layer == 1:
                return t_s, ETI, t_et
            return t_s

        LG, EA, UU, LN_, BS = (S(27648 + 512 * i, 512) for i in range(5))
        BIA = S(27648 + 2560, 32)
        t_bia = load(land("l_bia"), act, BIA, a["bias"])
        tl = done0[15]
        t_shd0 = (dve.sem, dve.count)
        t = act.op(lambda e: e.activation(EA, PB[6][:, :], ACT.Abs), tl, t_shd0)
        t_e = act.op(lambda e: e.activation(EA, EA, ACT.Exp, scale=-1.0), t)
        t = dve.op(lambda e: e.tensor_scalar(UU, EA, 1.0, None, ALU.add), t_e)
        t_l = act.op(lambda e: e.activation(LN_, UU, ACT.Ln), t)
        t = dve.op(lambda e: e.tensor_scalar(LG, PB[6][:, :], 0.0, None, ALU.max), tl)
        t = dve.op(lambda e: e.scalar_tensor_tensor(out=UU, in0=UU, scalar=-1.0, in1=EA, op0=ALU.add, op1=ALU.subtract), t, t_l)
        t = dve.op(lambda e: e.tensor_tensor(LG, LG, UU, ALU.subtract), t)
        t = dve.op(lambda e: e.tensor_tensor(LG, LG, LN_, ALU.add), t)
        t_lg0 = act.op(lambda e: e.activation(LG, LG, ACT.Sqrt), t)
        LGv = LG.rearrange("p (t e) -> p t e", e=E0)
        BSv = BS.rearrange("p (t e) -> p t e", e=E0)
        t = dve.op(lambda e: e.tensor_tensor(BSv, LGv, BIA.unsqueeze(1).broadcast_to([128, T, E0]), ALU.add), t_lg0, t_bia)
        t_list0 = route(E0, K0, BSv, LGv, TG[:, 2:3], 1.5, t, OH, TMP, LIST0, PB[6], PB[7], 27648 + 2592, 0)

        l_sw = land("l_sw0")
        t_sw = load(l_sw, sp, SW0, a["sw0"], t_wt)
        l_acc = [land(f"l_acc{i}") for i in range(3)]
        ACCB = [XN[i] for i in range(3)]
        acc_free = [list(x) for x in [[(l_xn[i].sem, l_xn[i].count)] for i in range(3)]]

        def rows_out(i, ps, gate, table, t, buf, free, gsrc=None):
            tt_ = dve.op(lambda e: e.scalar_tensor_tensor(out=buf, in0=ps[:, :], scalar=gate, in1=X[:, i, :], op0=ALU.mult, op1=ALU.add), t, *free)
            td = load(l_acc[i % 3], sp, table[i * 128:(i + 1) * 128, :], buf, tt_)
            return tt_, td

        ps_g = [None, None]
        int_free = [None, None]
        py = [None, None]
        SSH = [S(OH - 2048 + 512 * i, 512) for i in range(2)]
        ss_free = [t_m, t_m]
        pend = None

        def down0(c, tint):
            nonlocal_t = None
            for j in range(4):
                i = 4 * c + j

                def f(e, j=j, i=i):
                    for k in range(2):
                        r = e.matmul(PB[4 + i % 2][:, :], INT0[c % 2][:, k, j * 128:(j + 1) * 128], SW0[:, 2048 + k * 512:2560 + k * 512], start=(k == 0), stop=(k == 1))
                    return r
                t = pe.op(f, tint, py[i % 2])
                nonlocal_t = t
                tt_, td = rows_out(i, PB[4 + i % 2], TG[:, 2:3], ACC, t, ACCB[i % 3], acc_free[i % 3])
                py[i % 2] = tt_
                acc_free[i % 3] = [td]
            int_free[c % 2] = nonlocal_t

        py = [wt_free, wt_free]
        psx = [t_ht, t_ht]
        u = 0
        for c in range(4):
            tl_ = None
            for m in range(2):
                pg, pu = PB[2 * (u % 2)], PB[2 * (u % 2) + 1]

                def f(e, m=m, c=c, pg=pg, pu=pu):
                    for ps, base in ((pg, 0), (pu, 1024)):
                        for k in range(4):
                            r = e.matmul(ps[:, :], SW0[:, base + k * 256 + m * 128:base + k * 256 + (m + 1) * 128], HT[:, k, c * 512:(c + 1) * 512], start=(k == 0), stop=(k == 3))
                    return r
                t = pe.op(f, t_sw, t_ht, psx[u % 2])
                ts = act.op(lambda e, u=u, pg=pg: e.activation(SSH[u % 2], pg[:, :], ACT.Silu), t, ss_free[u % 2])
                td = dve.op(lambda e, u=u, pu=pu, m=m, c=c: e.tensor_tensor(INT0[c % 2][:, m, :], SSH[u % 2], pu[:, :], ALU.mult), ts, int_free[c % 2])
                psx[u % 2] = td
                ss_free[u % 2] = td
                tl_ = dve.op(lambda e, m=m, c=c: e.tensor_scalar(INT0[c % 2][:, m, :], INT0[c % 2][:, m, :], 10.0, -10.0, ALU.min, ALU.max), td)
                u += 1
            if pend:
                down0(*pend)
            pend = (c, tl_)
        down0(*pend)
        t_acc_rows = [(l.sem, l.count) for l in l_acc]
        t_sh0 = (pe.sem, pe.count)
        t_shd = (dve.sem, dve.count)

        LB = S(TMP, HALF, 2, p1=64)
        l_lb = land("l_lb")
        t_lb = load(l_lb, sp, LB.rearrange("p a b -> p (a b)"), LIST0[0:TRASH0, :].rearrange("(a b) c -> a (b c)", a=64), t_list0)

        def fl(e):
            e.transpose(PB[6][0:HALF, 0:64], LB[:, :, 0], ident[0:64, 0:64])
            return e.transpose(PB[6][0:HALF, 64:128], LB[:, :, 1], ident[0:64, 0:64])
        t_fl = pe.op(fl, t_lb, t_list0)
        IDI = IDS.bitcast(I32)
        t_ids = dve.op(lambda e: e.tensor_copy(IDI[0:HALF, :], PB[6][0:HALF, 0:64]), t_fl)
        t_wsl = dve.op(lambda e: e.tensor_copy(WSL[0:HALF, :], PB[6][0:HALF, 64:128]), t_fl)

        l_wr = [land(f"l_wr{i}") for i in range(2)]
        l_g = [land(f"l_g{i}") for i in range(4)]
        l_add = land("l_add")
        wr_free = [t_sh0, t_sh0]
        g_free = [t_shd] * 4
        ys_free = [t_shd] * 4
        in_free = [t_shd, t_shd]
        t_add = None
        pxt, pgu, pyy = [t_shd] * 2, [t_shd] * 2, [t_shd, t_wsl]
        xt_free = [None, None]
        st = {}

        def fetch(e_):
            t_wr = load(l_wr[e_ % 2], sp, WR[e_ % 2], a["we0"][e_], wr_free[e_ % 2])
            tg_ = []
            for h in range(2):
                s = (2 * e_ + h) % 4
                tg_.append(l_g[s].dma(pool, lambda e, s=s, h=h: e.indirect_dma_start(
                    G[s], None, HN, bass.IndirectOffsetOnAxis(ap=IDI[0:HALF, 2 * e_ + h:2 * e_ + h + 1], axis=0)),
                    t_ids, g_free[s], *t_rows0, t_init))
            st[e_] = [t_wr, tg_]

        def turn(e_):
            t_wr, tg_ = st[e_]
            tc = []
            for h in range(2):
                s = (2 * e_ + h) % 4

                def f(e, s=s, h=h):
                    for k in range(4):
                        r = e.transpose(PB[h][:, k * HALF:(k + 1) * HALF], G[s][:, k * 128:(k + 1) * 128], ident[0:HALF, 0:HALF])
                    return r
                t = pe.op(f, tg_[h], pxt[h])
                g_free[s] = t
                src = PB[h][:, 0:4 * HALF].rearrange("p (k t) -> p k t", k=4)
                dst = XT[e_ % 2][:, :, h * HALF:(h + 1) * HALF]
                if h == 0:
                    t = act.op(lambda e, src=src, dst=dst: e.activation(dst, src, ACT.Copy), t, xt_free[e_ % 2])
                else:
                    t = dve.op(lambda e, src=src, dst=dst: e.tensor_copy(dst, src), t, xt_free[e_ % 2])
                pxt[h] = t
                tc.append(t)
            st[e_].append(tc)

        def up(e_):
            t_wr, tg_, tc = st[e_]
            pg, pu = PB[2 + 2 * (e_ % 2)], PB[3 + 2 * (e_ % 2)]

            def f(e):
                for ps, base in ((pg, 0), (pu, 1024)):
                    for m in range(2):
                        for k in range(4):
                            r = e.matmul(ps[:, m * CAP:(m + 1) * CAP], WR[e_ % 2][:, base + k * 256 + m * 128:base + k * 256 + (m + 1) * 128], XT[e_ % 2][:, k, :], start=(k == 0), stop=(k == 3))
                return r
            t = pe.op(f, t_wr, *tc, pgu[e_ % 2])
            xt_free[e_ % 2] = t
            sl, inn = SL0[e_ % 2].rearrange("p a b -> p (a b)"), IN0[e_ % 2].rearrange("p a b -> p (a b)")
            ts = act.op(lambda e: e.activation(sl, pg[:, 0:2 * CAP], ACT.Silu), t, pgu[e_ % 2])
            td = dve.op(lambda e: e.tensor_tensor(inn, sl, pu[:, 0:2 * CAP], ALU.mult), ts, in_free[e_ % 2])
            pgu[e_ % 2] = td
            st[e_].append(td)

        def down(e_):
            nonlocal t_add
            td = st[e_][3]
            for h in range(2):
                s = (2 * e_ + h) % 4

                def f(e, h=h):
                    for k in range(2):
                        r = e.matmul(PB[6 + h][0:HALF, :], IN0[e_ % 2][:, k, h * HALF:(h + 1) * HALF], WR[e_ % 2][:, 2048 + k * 512:2560 + k * 512], start=(k == 0), stop=(k == 1))
                    return r
                t = pe.op(f, td, pyy[h])
                wsc = WSL[0:HALF, 2 * e_ + h:2 * e_ + h + 1]
                if h == 0:
                    ty = act.op(lambda e, s=s, wsc=wsc: e.activation(YS[s], PB[6][0:HALF, :], ACT.Copy, scale=wsc), t, ys_free[s], t_wsl)
                else:
                    ty = dve.op(lambda e, s=s, wsc=wsc: e.tensor_scalar(YS[s], PB[7][0:HALF, :], wsc, None, ALU.mult), t, ys_free[s], t_wsl)
                pyy[h] = ty
                t_add = l_add.dma(pool, lambda e, s=s, h=h: e.indirect_dma_start(
                    ACC, bass.IndirectOffsetOnAxis(ap=IDI[0:HALF, 2 * e_ + h:2 * e_ + h + 1], axis=0), YS[s], None, compute_op=ALU.add),
                    ty, t_add, t_ids, *t_acc_rows, t_init)
                ys_free[s] = t_add
            wr_free[e_ % 2] = t
            in_free[e_ % 2] = t

        fetch(0)
        fetch(1)
        turn(0)
        for e_ in range(E0):
            up(e_)
            if e_ + 1 < E0:
                turn(e_ + 1)
            down(e_)
            if e_ + 2 < E0:
                fetch(e_ + 2)
        t_end0 = (pe.sem, pe.count)
        t_end0d = (dve.sem, dve.count)
        t_end0a = (act.sem, act.count)

        l_w1 = land("l_w1")
        load(l_w1, sp, S(0, 4, WE1), a["we1"][0:4].rearrange("e p n -> p e n"), t_end0, t_end0d, t_end0a)
        l_s1 = land("l_s1")
        t_rw1 = load(l_s1, sp, RW1, a["rw1"].rearrange("(k p) n -> p k n", p=128))
        l_xb = [land(f"l_xb{i}") for i in range(4)]
        for b in range(4):
            load(l_xb[b], sp, X[:, 4 * b:4 * b + 4, :], ACC[b * 512:(b + 1) * 512, :].rearrange("(t p) d -> p t d", p=128), t_add, t_end0)

        XC = [S(25600 + 512 * i, 512) for i in range(3)]
        CXT = S(25600 + 1536, 4, 4, 64)
        PP = S(25600 + 2560, 16, 64)
        PTt = S(25600 + 3584, 8, 128)
        HC = S(25600 + 4608, 4, 128)
        MN = S(25600 + 5120, 512)
        SMX = S(25600 + 5632, 16)
        SSM = S(25600 + 5648, 16)
        t_prev = None
        for b in range(4):
            def fc(e, b=b):
                for k in range(4):
                    r = e.transpose(PB[b % 2][:, k * 64:(k + 1) * 64], CTX[0:64, b, k * 128:(k + 1) * 128], ident[0:64, 0:64])
                return r
            t = pe.op(fc, t_end0d, t_end0a, t_prev)
            t_cx = act.op(lambda e, b=b: e.activation(CXT[:, b, :, :].rearrange("p k s -> p (k s)"), PB[b % 2][:, 0:256], ACT.Copy), t, t_add)
            t_prev = t_cx
        mask_m = CON[:, C_CM:C_CM + 64].unsqueeze(1).broadcast_to([128, 8, 64])
        mask_a = CON[:, C_CA:C_CA + 64].unsqueeze(1).broadcast_to([128, 8, 64])
        t_last = None
        t_x3 = [None] * 4
        for b in range(4):
            tb = (l_xb[b].sem, 16)
            i3 = 4 * b + 3
            t_rs = ln_stats(b, [tb, t_end0d])
            t_n = norm(i3, XC[b % 2], t_rs, t_last, t_end0)
            t_f = flip(i3, XC[b % 2], PB[2], t_n, t_last, t_end0a)
            t_h = act.op(lambda e: e.activation(HC.rearrange("p a b -> p (a b)"), PB[2][:, :], ACT.Copy), t_f)

            def fs(e, b=b):
                for h in range(16):
                    p0 = 32 * (h % 4)
                    bank = 4 + (h % 4)
                    r = e.matmul(PB[bank][:, (h // 4) * 64:(h // 4 + 1) * 64], HC[p0:p0 + 32, h // 4, :], CXT[p0:p0 + 32, b, h // 4, :],
                                 start=True, stop=True, tile_position=(p0, 0))
                return r
            t_s = pe.op(fs, t_h, t_cx, t_last)
            ppv = PP.rearrange("p (g r) s -> p r g s", r=4)
            for r in range(4):
                src = PB[4 + r][:, 0:256].rearrange("p (g s) -> p g s", s=64)
                t = dve.op(lambda e, r=r, src=src: e.tensor_tensor(ppv[:, r, :, :], src, mask_m[:, 0:4, :], ALU.mult), t_s)
                t = dve.op(lambda e, r=r: e.tensor_tensor(ppv[:, r, :, :], ppv[:, r, :, :], mask_a[:, 0:4, :], ALU.add), t)
            t = dve.op(lambda e: e.tensor_reduce(SMX, PP, AX.X, ALU.max), t)
            t = dve.op(lambda e: e.tensor_tensor(PP, PP, SMX.unsqueeze(2).broadcast_to([128, 16, 64]), ALU.subtract), t)
            t = act.op(lambda e: e.activation(PP.rearrange("p a b -> p (a b)"), PP.rearrange("p a b -> p (a b)"), ACT.Exp), t)
            t = dve.op(lambda e: e.tensor_reduce(SSM, PP, AX.X, ALU.add), t)
            t = dve.op(lambda e: e.reciprocal(SSM, SSM), t)
            t = dve.op(lambda e: e.tensor_tensor(PP, PP, SSM.unsqueeze(2).broadcast_to([128, 16, 64]), ALU.mult), t)

            def fp(e):
                for j in range(8):
                    r = e.transpose(PB[4 + j // 4][:, (j % 4) * 128:(j % 4 + 1) * 128], PP[:, 2 * j:2 * j + 2, :].rearrange("p a b -> p (a b)"), ident)
                return r
            t = pe.op(fp, t)
            for j in range(2):
                t_pt = act.op(lambda e, j=j: e.activation(PTt[:, 4 * j:4 * j + 4, :].rearrange("p a b -> p (a b)"), PB[4 + j][:, :], ACT.Copy), t)

            def fo(e, b=b):
                for h in range(16):
                    p0 = 64 * (h % 2)
                    r = e.matmul(PB[6 + h % 2][:, h * 32:(h + 1) * 32], PTt[p0:p0 + 64, h // 2, :], CTX[p0:p0 + 64, b, h * 32:(h + 1) * 32],
                                 start=True, stop=True, tile_position=(p0, 0))
                return r
            t_o = pe.op(fo, t_pt)
            t_mm = pe.op(lambda e, b=b: e.matmul(PB[3][:, :], CON[0:64, C_INV:C_INV + 128], CTX[0:64, b, :], start=True, stop=True), t_last)
            for q in range(2):
                ov = PB[6 + q][:, :].rearrange("p (a c d) -> p a c d", c=2, d=32)[:, :, q, :]
                xv = X[:, i3, :].rearrange("p (a c d) -> p a c d", c=2, d=32)[:, :, q, :]
                t = dve.op(lambda e, ov=ov, xv=xv: e.scalar_tensor_tensor(out=xv, in0=ov, scalar=TG[:, 1:2], in1=xv, op0=ALU.mult, op1=ALU.add), t_o, t_n)
            t = dve.op(lambda e: e.tensor_scalar(MN, PB[3][:, :], TG[:, 1:2], None, ALU.mult), t_mm)
            for j in range(3):
                t_last = dve.op(lambda e, i=4 * b + j: e.tensor_tensor(X[:, i, :], X[:, i, :], MN, ALU.add), t)
            t_x3[b] = t_last

        t_cend = (act.sem, act.count)
        done1, t_ht1, t_rows1 = ln_rows(HN2, RW1, E1, XC, [[t_last], [t_last], [t_last]], lambda b: [t_x3[b]], t_rw1,
                                        [t_last, t_last], PB[6], None)
        l_sgu = land("l_sgu")
        t_sgu = load(l_sgu, sp, SGU[:, 0, :, :], a["sg1"].rearrange("(k p) n -> p k n", p=128), t_shd, *t_acc_rows, t_x3[3])
        t_sgu = load(l_sgu, sp, SGU[:, 1, :, :], a["su1"].rearrange("(k p) n -> p k n", p=128))
        l_swd = land("l_swd")
        t_lnend = (pe.sem, pe.count)
        t_swd = load(l_swd, sp, SWD, a["sd1"].rearrange("(k p) n -> p k n", p=128), t_x3[3], *t_rows1, t_lnend)
        SMO = [SMALL]

        def tks(*sh):
            q = SMO[0]
            SMO[0] += int(np.prod(sh))
            return S(q, *sh)
        SB1 = tks(12)
        t_sb = load(l_s1, sp, SB1, a["sb1"])
        t_s1 = t_sb

        PR = S(25600 + 5760, T, E1)
        PRM, PRS = tks(T), tks(T)
        lgv = PB[6][:, 0:T * E1].rearrange("p (t e) -> p t e", e=E1)
        t = dve.op(lambda e: e.tensor_reduce(PRM, lgv, AX.X, ALU.max), done1[15], *t_rows1)
        t = dve.op(lambda e: e.tensor_tensor(PR, lgv, PRM.unsqueeze(2).broadcast_to([128, T, E1]), ALU.subtract), t)
        t = act.op(lambda e: e.activation(PR.rearrange("p a b -> p (a b)"), PR.rearrange("p a b -> p (a b)"), ACT.Exp), t)
        t = dve.op(lambda e: e.tensor_reduce(PRS, PR, AX.X, ALU.add), t)
        t = dve.op(lambda e: e.reciprocal(PRS, PRS), t)
        t = dve.op(lambda e: e.tensor_tensor(PR, PR, PRS.unsqueeze(2).broadcast_to([128, T, E1]), ALU.mult), t)
        l_sc = land("l_sc1")
        R1 = 4 * 4352 + 8192
        t_list1, ETI, t_et = route(E1, K1, PR, PR, TG[:, 3:4], 1.0, t, R1, R1 + 256, LIST1, PB[6], PB[7], R1 + 512, 1)
        ETK = tks(NT).bitcast(I32)
        t_etk = dve.op(lambda e: e.tensor_copy(ETK, ETI), t_et)

        LB1 = S(SMO[0], 256, p1=NT)
        SMO[0] += 256
        t_lb1 = load(l_lb, sp, LB1, LIST1.rearrange("(a b) c -> a (b c)", a=NT), t_list1)
        LB1v = LB1.rearrange("p (a b) -> p a b", b=2)

        def fl1(e):
            e.transpose(PB[6][:, 0:NT], LB1v[:, :, 0], ident[0:NT, 0:NT])
            return e.transpose(PB[6][:, 64:64 + NT], LB1v[:, :, 1], ident[0:NT, 0:NT])
        t_fl1 = pe.op(fl1, t_lb1, t_etk)
        t_ids1 = dve.op(lambda e: e.tensor_copy(IDI[:, 0:NT], PB[6][:, 0:NT]), t_fl1)
        t_wsl1 = dve.op(lambda e: e.tensor_copy(WSL[:, 0:NT], PB[6][:, 64:64 + NT]), t_fl1)

        NM = 6
        SS1 = [S(hoff - 2048 + 512 * i, 512) for i in range(2)]
        AC1 = [S(hoff - 1024 + 512 * i, 512) for i in range(2)]
        I1v = [S(o, NM, D) for o in INT1]
        for q in range(2):
            t_one = dve.op(lambda e, q=q: e.memset(I1v[q][64:65, 5, :], 1.0), t_list1, t_wsl1)
        ps_free = [t_wsl1] * 2
        ss_free = [t_x3[3], t_x3[3]]
        int_free = [t_one, t_one]
        ac_free = [[t_x3[3]], [t_x3[3]]]
        py = [t_wsl1] * 2
        pend = None

        def down1(c, tint):
            for j in range(4):
                i = 4 * c + j

                def f(e, j=j, i=i):
                    for k in range(6):
                        kp = 128 if k < 5 else 65
                        r = e.matmul(PB[4 + i % 2][:, :], I1v[c % 2][0:kp, k, j * 128:(j + 1) * 128], SWD[0:kp, k, :], start=(k == 0), stop=(k == 5))
                    return r
                t = pe.op(f, tint, py[i % 2], t_swd)
                tt_ = dve.op(lambda e, i=i: e.scalar_tensor_tensor(out=AC1[i % 2], in0=PB[4 + i % 2][:, :], scalar=TG[:, 3:4], in1=X[:, i, :], op0=ALU.mult, op1=ALU.add), t, *ac_free[i % 2])
                td = load(l_acc[i % 2], sp, ACC2[i * 128:(i + 1) * 128, :], AC1[i % 2], tt_)
                py[i % 2] = tt_
                ac_free[i % 2] = [td]
            int_free[c % 2] = t
            return tt_

        u = 0
        for c in range(4):
            for m in range(NM):
                w = 128 if m < 5 else 64
                pg, pu = PB[2 * (u % 2)], PB[2 * (u % 2) + 1]

                def f(e, m=m, c=c, pg=pg, pu=pu, w=w):
                    for q, ps in ((0, pg), (1, pu)):
                        for k in range(4):
                            r = e.matmul(ps[0:w, :], SGU[:, q, k, m * 128:m * 128 + w], HT[:, k, c * 512:(c + 1) * 512], start=(k == 0), stop=(k == 3))
                    return r
                t = pe.op(f, t_sgu, t_ht1, ps_free[u % 2])
                ts = act.op(lambda e, u=u, pg=pg, w=w, m=m: e.activation(SS1[u % 2][0:w, :], pg[0:w, :], ACT.Silu, bias=SB1[0:w, m:m + 1]), t, ss_free[u % 2], t_s1)
                td = dve.op(lambda e, u=u, pu=pu, m=m, c=c, w=w: e.scalar_tensor_tensor(out=I1v[c % 2][0:w, m, :], in0=pu[0:w, :], scalar=SB1[0:w, 6 + m:7 + m], in1=SS1[u % 2][0:w, :], op0=ALU.add, op1=ALU.mult), ts, int_free[c % 2], t_s1)
                ps_free[u % 2] = td
                ss_free[u % 2] = td
                u += 1
            if pend:
                down1(*pend)
            pend = (c, td)
        down1(*pend)
        t_sh1 = (pe.sem, pe.count)
        t_sh1d = (dve.sem, dve.count)
        t_acc2 = [(l.sem, l.count) for l in l_acc[0:2]]
        t_w1 = load(l_w1, sp, S(4 * WE1, 4, WE1), a["we1"][4:8].rearrange("e p n -> p e n"), t_sh1, t_sh1d)

        G1 = [S(hoff + 512 * i, 512) for i in range(2)]
        XT1 = [S(hoff + 1024 + 512 * i, 4, 128) for i in range(2)]
        SL1 = [S(hoff + 2048 + 352 * i, I1) for i in range(2)]
        IN1 = [S(hoff + 2752 + 352 * i, I1) for i in range(2)]
        NT1 = [S(hoff + 3456 + 384 * i, 3, 128) for i in range(2)]
        YS1 = [S(hoff + 4224 + 512 * i, 512) for i in range(3)]
        g_free = [t_sh1] * 2
        xt_free = [t_sh1] * 2
        sl_free = [t_sh1] * 2
        inn_free = [t_sh1] * 2
        nt_free = [t_sh1] * 2
        ys_free = [t_sh1] * 3
        p_xt, p_it = t_sh1d, t_sh1d
        p_gu = [t_sh1d] * 2
        p_y = [t_sh1d] * 2
        st = {}
        t_add = None

        def fetch1(n):
            st[n] = [l_g[n % 2].dma(pool, lambda e: e.indirect_dma_start(
                G1[n % 2], None, HN2, bass.IndirectOffsetOnAxis(ap=IDI[:, n:n + 1], axis=0)), t_ids1, g_free[n % 2], *t_rows1)]

        def turn1(n):
            nonlocal p_xt

            def f(e):
                for k in range(4):
                    r = e.transpose(PB[0][:, k * 128:(k + 1) * 128], G1[n % 2][:, k * 128:(k + 1) * 128], ident)
                return r
            t = pe.op(f, st[n][0], p_xt)
            g_free[n % 2] = t
            p_xt = act.op(lambda e: e.activation(XT1[n % 2].rearrange("p a b -> p (a b)"), PB[0][:, :], ACT.Copy), t, xt_free[n % 2])
            st[n].append(p_xt)

        def up1(n, reg):
            pg, pu = PB[2 + 2 * (n % 2)], PB[3 + 2 * (n % 2)]

            def f(e):
                r0 = e.value_load(ETK[0:1, n:n + 1], min_val=0, max_val=7 * WE1)
                regs[n] = r0
                for q, ps in ((0, pg), (1, pu)):
                    for k in range(4):
                        r = e.matmul(ps[:, 0:I1], XT1[n % 2][:, k, :], W1[:, bass.ds(r0 + (q * 4 + k) * I1, I1)], start=(k == 0), stop=(k == 3))
                return r
            t = pe.op(f, st[n][1], p_gu[n % 2], t_w1, t_etk)
            xt_free[n % 2] = t
            ts = act.op(lambda e: e.activation(SL1[n % 2], pg[:, 0:I1], ACT.Silu), t, sl_free[n % 2])
            td = dve.op(lambda e: e.tensor_tensor(IN1[n % 2], SL1[n % 2], pu[:, 0:I1], ALU.mult), ts, inn_free[n % 2])
            sl_free[n % 2] = td
            p_gu[n % 2] = td
            st[n].append(td)

        def flip1(n):
            nonlocal p_it

            def f(e):
                for k in range(3):
                    w = 128 if k < 2 else 96
                    r = e.transpose(PB[1][0:w, k * 128:(k + 1) * 128], IN1[n % 2][:, k * 128:k * 128 + w], ident)
                return r
            t = pe.op(f, st[n][2], p_it)
            inn_free[n % 2] = t
            dve.op(lambda e: e.tensor_copy(NT1[n % 2][:, 0:2, :].rearrange("p a b -> p (a b)"), PB[1][:, 0:256]), t, nt_free[n % 2])
            p_it = dve.op(lambda e: e.tensor_copy(NT1[n % 2][0:96, 2, :], PB[1][0:96, 256:384]), t, nt_free[n % 2])
            st[n].append(p_it)

        def down_1(n):
            nonlocal t_add

            def f(e):
                r0 = regs[n]
                for k in range(3):
                    w = 128 if k < 2 else 96
                    r = e.matmul(PB[6 + n % 2][:, :], NT1[n % 2][0:w, k, :], W1[0:w, bass.ds(r0 + 8 * I1 + k * 512, 512)], start=(k == 0), stop=(k == 2))
                return r
            t = pe.op(f, st[n][3], p_y[n % 2])
            nt_free[n % 2] = t
            ty = act.op(lambda e: e.activation(YS1[n % 3], PB[6 + n % 2][:, :], ACT.Copy, scale=WSL[:, n:n + 1]), t, ys_free[n % 3], t_wsl1)
            p_y[n % 2] = ty
            t_add = l_add.dma(pool, lambda e: e.indirect_dma_start(
                ACC2, bass.IndirectOffsetOnAxis(ap=IDI[:, n:n + 1], axis=0), YS1[n % 3], None, compute_op=ALU.add), ty, t_add, *t_acc2)
            ys_free[n % 3] = t_add

        regs = {}
        fetch1(0)
        fetch1(1)
        turn1(0)
        for n in range(NT):
            up1(n, None)
            if n + 1 < NT:
                turn1(n + 1)
            if n + 2 < NT:
                fetch1(n + 2)
            if n:
                down_1(n - 1)
            flip1(n)
        down_1(NT - 1)

        l_out = land("l_out")
        t_out = load(l_out, sp, out.rearrange("b s d -> (b s) d"), ACC2[0:2048, :], t_add)
        sp.op(lambda e: e.wait_ge(l_out.sem, l_out.count) or e, sig=False)

        @block.tensor
        def _(e):
            pe.play(e)

        @block.vector
        def _(e):
            dve.play(e)

        @block.scalar
        def _(e):
            act.play(e)

        @block.gpsimd
        def _(e):
            pool.play(e)

        @block.sync
        def _(e):
            sp.play(e)


def kernel(**inp):
    import concourse.bacc as bacc
    from concourse.bass_utils import run_bass_kernel_spmd as run
    v = {k: np.asarray(x) for k, x in inp.items()}

    def cols(w):
        c, n = w.shape[-2:]
        t = -(-c // 128)
        w = np.concatenate([w, np.zeros(w.shape[:-2] + (t * 128 - c, n), w.dtype)], axis=-2)
        w = w.reshape(w.shape[:-2] + (t, 128, n))
        w = np.swapaxes(w, -3, -2)
        return w.reshape(w.shape[:-2] + (t * n,))

    sw = np.swapaxes
    we0 = np.concatenate([cols(sw(v["L0_ffn_w_gate"], 1, 2)), cols(sw(v["L0_ffn_w_up"], 1, 2)), cols(sw(v["L0_ffn_w_down"], 1, 2))], axis=-1)
    sw0 = np.concatenate([cols(v["L0_ffn_sg"].T), cols(v["L0_ffn_su"].T), cols(v["L0_ffn_sd"].T)], axis=-1)
    we1 = np.concatenate([cols(v["L1_ffn_gate_w"]), cols(v["L1_ffn_up_w"]), cols(v["L1_ffn_down_w"])], axis=-1)
    sd1 = np.zeros((768, D), np.float32)
    sd1[0:SI] = v["L1_ffn_s_down_w"]
    sd1[SI] = v["L1_ffn_s_down_b"]
    sb1 = np.zeros((2, 768), np.float32)
    sb1[0, 0:SI] = v["L1_ffn_s_gate_b"]
    sb1[1, 0:SI] = v["L1_ffn_s_up_b"]
    con, l0, l1 = constants()
    arrays = {
        "x": v["x"], "ctx": v["ctx_2048"], "itok": v["itok_Sx4_0_63"],
        "g": np.broadcast_to(np.concatenate([v["g_xattn"], v["g_ffn"]])[None, :], (128, 4)),
        "descT": v["L0_xattn_desc_router"].T, "wq": v["L0_xattn_W_q"],
        "bq": v["L0_xattn_b_q"].reshape(4, 128).T,
        "rw0": v["L0_ffn_gate_w"].T, "bias": np.broadcast_to(v["L0_ffn_bias"][None, :], (128, E0)),
        "we0": we0, "sw0": sw0, "rw1": v["L1_ffn_router_w"].T, "we1": we1,
        "sg1": v["L1_ffn_s_gate_w"], "su1": v["L1_ffn_s_up_w"], "sd1": sd1,
        "sb1": sb1.reshape(2, 6, 128).transpose(2, 0, 1).reshape(128, 12),
        "con": con, "l0": l0, "l1": l1, "zero": np.zeros((128, D), np.float32),
    }
    nc = bacc.Bacc("TRN2", target_bir_lowering=False, num_devices=1)
    given, aps = {}, {}
    for name, x in arrays.items():
        x = np.ascontiguousarray(x)
        given[f"in_{name}"] = x
        aps[name] = nc.dram_tensor(f"in_{name}", x.shape, mybir.dt.from_np(x.dtype), kind="ExternalInput").ap()
    o = nc.dram_tensor("out_0", (4, 512, 512), F32, kind="ExternalOutput").ap()
    program(nc, aps, o)
    r = run(nc, [given], core_ids=[0])
    return r.results[0]["out_0"]
```

```python
import numpy as np
import concourse.bass as bass
from concourse import mybir
from contextlib import ExitStack

F32 = mybir.dt.float32
I32 = mybir.dt.int32
U32 = mybir.dt.uint32
ALU = mybir.AluOpType
ACT = mybir.ActivationFunctionType
AX = mybir.AxisListType

T = 16
D = 512
E0, K0, I0, CAP = 32, 6, 256, 192
HALF = CAP // 2
E1, K1, I1, SI = 8, 2, 352, 704
NT = 39
WE0 = 3072
WE1 = 4352
ROWS = 2048 + 192
TRASH0 = E0 * CAP

C_ID, C_U, C_ONE, C_IOTA, C_TOK, C_TR, C_CM, C_CA, C_I39 = 0, 128, 256, 384, 448, 464, 560, 624, 688
C_INV = 688 + NT * 8
NCONST = C_INV + 128


def constants():
    c = np.zeros((128, NCONST), np.float32)
    p = np.arange(128)
    c[:, C_ID:C_ID + 128] = np.eye(128)
    c[:, C_U:C_U + 128] = (p[:, None] < p[None, :])
    c[:, C_ONE:C_ONE + 128] = 1.0
    c[:, C_IOTA:C_IOTA + 64] = np.arange(64)
    c[:, C_TOK:C_TOK + T] = p[:, None] + 128 * np.arange(T)
    c[:, C_TR:C_TR + T * K0] = TRASH0 + p[:, None] + 128 * np.arange(T * K0)
    allowed = np.arange(64)[None, :] <= (p[:, None] - 64)
    c[:, C_CM:C_CM + 64] = allowed * (32.0 ** -0.5)
    c[:, C_CA:C_CA + 64] = np.where(allowed, 0.0, -10000.0)
    c[:, C_I39:C_I39 + NT * 8] = np.repeat(np.arange(NT), 8)
    c[:, C_INV:C_INV + 128] = 1.0 / 64
    l0 = np.zeros((TRASH0, 2), np.float32)
    l0[:, 0] = 2048 + np.arange(TRASH0) % CAP
    l1 = np.zeros(((E1 * 16 + 1) * 128, 2), np.float32)
    l1[:, 0] = 2048 + np.arange(len(l1)) % 128
    return c, l0, l1


class Engine:

    def __init__(self, sem, chain=False):
        self.sem, self.count, self.todo, self.chain = sem, 0, [], chain

    def op(self, fn, *waits, sig=True):
        if self.chain and self.count:
            waits = (*waits, (self.sem, self.count))
        if sig:
            self.count += 1
        self.todo.append((fn, waits, (self.sem, 1) if sig else None))
        return (self.sem, self.count)

    def play(self, eng):
        seen = {}
        for fn, waits, sig in self.todo:
            for w in waits:
                if w is None:
                    continue
                s, v = w
                if seen.get(s.name, 0) < v:
                    eng.wait_ge(s, v)
                    seen[s.name] = v
            ins = fn(eng)
            if sig:
                ins.then_inc(*sig)


class Landing:

    def __init__(self, sem):
        self.sem, self.count = sem, 0

    def dma(self, q, fn, *waits):
        self.count += 16
        q.todo.append((fn, waits, (self.sem, 16)))
        return (self.sem, self.count)


def program(nc, a, out):
    with ExitStack() as ctx:
        big = ctx.enter_context(nc.sbuf_tensor("big", [128, 53120], F32))
        PB = [ctx.enter_context(nc.psum_tensor(f"pb{i}", [128, 512], F32)) for i in range(8)]

        def sem(name):
            return ctx.enter_context(nc.semaphore(name))

        def land(name):
            return Landing(sem(name))

        pe, act, dve, pool, sp = (Engine(sem(n), n in ("s_act", "s_dve")) for n in ("s_pe", "s_act", "s_dve", "s_pool", "s_sp"))
        HN = nc.dram_tensor("hn_rows", [ROWS, D], F32, kind="Internal").ap()
        HN2 = nc.dram_tensor("hn2_rows", [ROWS, D], F32, kind="Internal").ap()
        ACC = nc.dram_tensor("acc_rows", [ROWS, D], F32, kind="Internal").ap()
        ACC2 = nc.dram_tensor("acc2_rows", [ROWS, D], F32, kind="Internal").ap()
        LIST0 = nc.dram_tensor("list0_rows", [TRASH0 + T * K0 * 128, 2], F32, kind="Internal").ap()
        LIST1 = nc.dram_tensor("list1_rows", [(E1 * 16 + 1) * 128, 2], F32, kind="Internal").ap()

        def S(off, *shape, p0=0, p1=128):
            n = int(np.prod(shape))
            v = big[p0:p1, off:off + n]
            if len(shape) == 2:
                v = v.rearrange("p (a b) -> p a b", a=shape[0])
            if len(shape) == 3:
                v = v.rearrange("p (a b c) -> p a b c", a=shape[0], b=shape[1])
            return v

        REST = E1 * WE1
        W1 = S(0, REST)

        def taker(start, end):
            at = [start]

            def take(*shape, p1=128):
                o = at[0]
                at[0] += int(np.prod(shape))
                assert at[0] <= end, (at[0], end)
                return S(o, *shape, p1=p1)
            take.at = at
            return take

        keep = taker(REST, 53120)
        CON = keep(NCONST)
        CTX = keep(4, D)
        TG, GVAL, IDS, WSL = keep(4), keep(4), keep(64), keep(64)
        ident = CON[:, C_ID:C_ID + 128]
        RING = keep.at[0]
        ring = taker(RING, 53120)
        WR = [ring(WE0) for _ in range(4)]
        YS = [ring(D, p1=HALF) for _ in range(4)]
        SW0 = WR[2]
        early = taker(RING + 3 * WE0, RING + 4 * WE0)
        WQ, DT, BQB = early(4, D), early(4, 64), early(4, 128)
        one = taker(0, REST)
        X = one(T, D)
        MSB, NCB, RW0, BIA = one(4, 64), one(4, 64), one(4, E0), one(E0)
        BQ, CB, ITF, CC = one(4), one(64), one(4, 4), one(4, 5 * E0)
        ITI = one(4, 4).bitcast(I32)
        CH = []
        for b in range(4):
            c = {"XN": [one(D), one(D)], "HT": one(4, 512), "SC": one(4, 64)}
            r = one.at[0]
            one.at[0] += 1536
            c["WTS"], c["WTS2"], c["WT"] = S(r, 4, 64), S(r + 256, 4, 64), S(r + 512, D, p1=64)
            c["TT"] = S(r + 1024, D, p1=64)
            c["OH"], c["TM"] = S(r, 4, K0 * E0), S(r + 768, 4, K0 * E0)
            c["INT"], c["SS"] = S(r, 2, D), S(r + 1024, D)
            for n in ("LG", "EA", "UU", "LN", "BS", "MS"):
                c[n] = one(4, E0)
            c["ST"], c["MV"], c["RS"], c["R2"] = one(4, 6), one(4, 2), one(4), one(4)
            c["MX"], c["MI"] = one(4, 8), one(4, 8).bitcast(U32)
            c["P12"], c["IDF"] = one(4, 2), one(4, 8)
            c["WK"], c["DEN"], c["ADR"], c["VA"] = one(4, K0), one(4, 1), one(4, K0), one(4, K0)
            c["REC"], c["ADI"] = one(4, K0, 2), one(4, K0).bitcast(I32)
            CH.append(c)
        two = taker(0, T * D)
        G = [two(D, p1=HALF) for _ in range(4)]
        XT = [two(4, CAP) for _ in range(2)]
        IN0 = [two(2, CAP) for _ in range(2)]
        SL0 = [two(2, CAP) for _ in range(2)]
        LB = two(HALF, 2, p1=64)

        block = ctx.enter_context(nc.Block())
        l_con, l_w, l_x = land("l_con"), land("l_w"), [land(f"l_x{i}") for i in range(4)]
        l_init = land("l_init")

        def load(l, q, dst, src, *waits):
            return l.dma(q, lambda e: e.dma_start(dst, src), *waits)

        def merge(*chains):
            live, n = list(chains), 0
            while live:
                for ch in list(live):
                    if n >= ch[0] and next(ch[1], None) is None:
                        live.remove(ch)
                n += 1

        l_it = land("l_it")
        t_con = load(land("l_con0"), act, CON, a["con"])
        load(l_w, act, WQ, a["wq"].rearrange("(k p) d -> p k d", p=128))
        for b in range(4):
            load(l_x[b], sp, X[:, 4 * b:4 * b + 4, :], a["x"][b].rearrange("(t p) d -> p t d", p=128))
        load(l_w, act, DT, a["descT"])
        t_w = load(l_w, act, BQ, a["bq"])
        t_gv = load(land("l_gv"), act, GVAL, a["g"])
        t_it = load(l_it, act, ITI, a["itok"].rearrange("(t p) k -> p t k", p=128))
        load(l_con, act, CTX[0:64], a["ctx"].rearrange("b s d -> s b d"))
        t_ctx = load(l_con, act, CTX[64:128], a["ctx"].rearrange("b s d -> s b d"))
        l_r0 = land("l_r0")
        load(l_r0, act, RW0, a["rw0"])
        t_r0 = load(l_r0, act, BIA, a["bias"])
        t_sw = load(land("l_sw0"), sp, SW0, a["sw0"])
        load(l_init, sp, LIST0[0:TRASH0, :].rearrange("(a b) c -> a (b c)", a=64), a["l0"].rearrange("(a b) c -> a (b c)", a=64))
        load(l_init, sp, LIST1.rearrange("(a b) c -> a (b c)", a=E1 * 16 + 1), a["l1"].rearrange("(a b) c -> a (b c)", a=E1 * 16 + 1))
        for tab in (HN, HN2, ACC, ACC2):
            t_init = load(l_init, sp, tab[2048:ROWS, :], a["zero"])
        l_wr = [land(f"l_wr{i}") for i in range(4)]
        st = {}
        for e_ in range(2):
            st[e_] = [load(l_wr[e_], sp, WR[e_], a["we0"][e_])]

        t_tg = act.op(lambda e: e.activation(TG, GVAL, ACT.Tanh), t_gv)
        QS = float(D) ** -0.5
        io4 = CON[:, C_IOTA:C_IOTA + 64].unsqueeze(1).broadcast_to([128, 4, 64])
        tk = {}

        def matrix():
            def mrows(e):
                for m in range(4):
                    for k in range(4):
                        i = e.matmul(PB[6][:, m * 64:(m + 1) * 64], WQ[:, k, m * 128:(m + 1) * 128], DT[:, k, :],
                                     start=(k == 0), stop=(k == 3))
                return i
            t_m = pe.op(mrows, t_w)
            t_bq = dve.op(lambda e: e.tensor_copy(BQB, BQ.unsqueeze(2).broadcast_to([128, 4, 128])), t_w)

            def cbrow(e):
                for k in range(4):
                    i = e.matmul(PB[7][:, 0:64], BQB[:, k, :], DT[:, k, :], start=(k == 0), stop=(k == 3))
                return i
            t_cb = pe.op(cbrow, t_bq, t_w)
            tk["early"] = t_cb
            yield 1
            tk["msb"] = act.op(lambda e: e.activation(MSB.rearrange("p a b -> p (a b)"), PB[6][:, 0:256], ACT.Copy), t_m)
            t = dve.op(lambda e: e.tensor_copy(ITF, ITI), t_it)
            TM = CH[3]["WTS"]
            yield 1
            for k in range(4):
                dst = NCB if k == 0 else TM
                t = dve.op(lambda e, k=k, dst=dst: e.tensor_tensor(dst, io4, ITF[:, :, k:k + 1].broadcast_to([128, 4, 64]), ALU.is_equal), t, t_con)
                if k:
                    t = dve.op(lambda e: e.tensor_tensor(NCB, NCB, TM, ALU.max), t)
                yield 1
            t = dve.op(lambda e: e.tensor_scalar(NCB, NCB, 1.0, 1e30, ALU.subtract, ALU.mult), t)
            t_cb = dve.op(lambda e: e.tensor_scalar(CB, PB[7][:, 0:64], QS, None, ALU.mult), t_cb)
            tk["ncb"] = dve.op(lambda e: e.tensor_tensor(NCB, NCB, CB.unsqueeze(1).broadcast_to([128, 4, 64]), ALU.add), t, t_cb)
            yield 1

        def rstd(RS, R2, var, t):
            t = dve.op(lambda e: e.tensor_scalar(R2, var, 1e-5, None, ALU.add), t)
            t = act.op(lambda e: e.activation(RS, R2, ACT.Ln), t)
            t = act.op(lambda e: e.activation(RS, RS, ACT.Exp, scale=-0.5), t)
            t = dve.op(lambda e: e.tensor_scalar(R2, R2, -0.5, None, ALU.mult), t)
            yield 1
            t = dve.op(lambda e: e.tensor_tensor(R2, R2, RS, ALU.mult), t)
            t = dve.op(lambda e: e.tensor_tensor(R2, R2, RS, ALU.mult), t)
            t = dve.op(lambda e: e.scalar_tensor_tensor(out=RS, in0=R2, scalar=1.5, in1=RS, op0=ALU.add, op1=ALU.mult), t)
            tk["rs"] = t
            yield 1

        def stats(c, xs, waits):
            n = len(xs)
            for i, x in enumerate(xs):
                dve.op(lambda e, i=i, x=x: e.bn_stats(c["ST"][:, i, :], x), *waits)
                t = dve.op(lambda e, i=i: e.bn_aggr(c["MV"][:, i, :], c["ST"][:, i, :]))
                yield 1
            yield from rstd(c["RS"][:, 0:n], c["R2"][:, 0:n], c["MV"][:, 0:n, 1], t)

        def norm(c, j, dst, x, *waits):
            return dve.op(lambda e: e.tensor_scalar(dst, x, c["MV"][:, j, 0:1], c["RS"][:, j:j + 1], ALU.subtract, ALU.mult), *waits)

        def flip(src, ps, *waits):
            def f(e):
                for k in range(4):
                    r = e.transpose(ps[:, k * 128:(k + 1) * 128], src[:, k * 128:(k + 1) * 128], ident)
                return r
            return pe.op(f, t_con, *waits)

        def evac(j, dst, ps, *waits):
            src = ps[:, :].rearrange("p (k t) -> p k t", k=4)
            d = dst[:, :, j * 128:(j + 1) * 128]
            return act.op(lambda e: e.activation(d, src, ACT.Copy), *waits)

        def back(dst_ps, w, rows, ht, tmp, p0, free0, free1, *waits):
            def f(e):
                for k in range(4):
                    r = e.matmul(p0[0:rows, :], w[:, k, :], ht[:, k, :], start=(k == 0), stop=(k == 3))
                return r
            t = pe.op(f, free0, *waits)
            t_m = t
            yield 1
            t = act.op(lambda e: e.activation(tmp[0:rows, :], p0[0:rows, :], ACT.Copy), t)
            t_c = t

            def g(e):
                for j in range(4):
                    r = e.transpose(dst_ps[:, j * rows:(j + 1) * rows], tmp[0:rows, j * 128:(j + 1) * 128], ident[0:rows, 0:rows])
                return r
            t = pe.op(g, t, free1)
            tk["back"] = (t_m, t_c, t)
            yield 1

        l_hn = [[land(f"l_hn{b}{j}") for j in range(2)] for b in range(4)]
        l_acc = [[land(f"l_as{b}{j}") for j in range(2)] for b in range(4)]
        l_sc = land("l_sc0")
        t_cc = [None] * 4
        t_end = [None] * 4
        rows0, accs0 = [], []

        def chain0(b):
            c = CH[b]
            P = [PB[2 * b], PB[2 * b + 1]]
            xs = [X[:, 4 * b + j, :] for j in range(4)]
            free = [tk["ncb"] if b == 3 else None, tk["ncb"] if b == 3 else None]
            xf = [[], []]
            yield from stats(c, xs, [(l_x[b].sem, 16)])
            t_rs = tk["rs"]
            for j in range(4):
                t_n = norm(c, j, c["XN"][j % 2], xs[j], t_rs, *xf[j % 2])
                t_f = flip(c["XN"][j % 2], P[j % 2], t_n, free[j % 2])
                xf[j % 2] = [t_f]
                yield 1
                free[j % 2] = evac(j, c["HT"], P[j % 2], t_f)
                yield 1
            yield from back(P[1], MSB, 64, c["HT"], c["TT"], P[0], free[0], free[1], tk["msb"], *free)
            t_m, t_c, t = tk["back"]
            t_sc = dve.op(lambda e: e.scalar_tensor_tensor(out=c["SC"], in0=P[1][:, 0:256].rearrange("p (a b) -> p a b", a=4), scalar=QS, in1=NCB, op0=ALU.mult, op1=ALU.add), t, tk["ncb"])
            yield 1
            t = t_sc
            for j in range(4):
                dve.op(lambda e, j=j: e.max(c["MX"][:, j, :], c["SC"][:, j, :]), t)
                t3 = dve.op(lambda e, j=j: e.max_index(c["MI"][:, j, :], c["MX"][:, j, :], c["SC"][:, j, :]))
                if j % 2:
                    yield 1
            P12, IDF, WTS, WTS2 = c["P12"], c["IDF"], c["WTS"], c["WTS2"]
            t = dve.op(lambda e: e.tensor_tensor(P12[:, :, 0:1], c["MX"][:, :, 1:2], c["MX"][:, :, 0:1], ALU.subtract), t3)
            t = act.op(lambda e: e.activation(P12[:, :, 1:2], P12[:, :, 0:1], ACT.Exp), t)
            dve.op(lambda e: e.tensor_copy(IDF, c["MI"]))
            yield 1
            for j, dst in ((0, WTS), (1, WTS2)):
                dve.op(lambda e, j=j, dst=dst: e.tensor_tensor(dst, io4, IDF[:, :, j:j + 1].broadcast_to([128, 4, 64]), ALU.is_equal))
            dve.op(lambda e: e.tensor_scalar(P12[:, :, 0:1], P12[:, :, 1:2], 1.0, None, ALU.add), t)
            dve.op(lambda e: e.reciprocal(P12[:, :, 0:1], P12[:, :, 0:1]))
            dve.op(lambda e: e.tensor_tensor(P12[:, :, 1:2], P12[:, :, 1:2], P12[:, :, 0:1], ALU.mult))
            yield 1
            for j, dst in ((0, WTS), (1, WTS2)):
                dve.op(lambda e, j=j, dst=dst: e.tensor_tensor(dst, dst, P12[:, :, j:j + 1].broadcast_to([128, 4, 64]), ALU.mult))
            t = dve.op(lambda e: e.tensor_tensor(WTS, WTS, WTS2, ALU.add))
            yield 1

            def fw(e):
                for j in range(4):
                    r = e.transpose(P[0][0:64, j * 128:(j + 1) * 128], WTS[:, j, :], ident)
                return r
            t = pe.op(fw, t, t_c)
            t_wt = act.op(lambda e: e.activation(c["WT"], P[0][0:64, :], ACT.Copy), t)
            yield 1
            free = [t_wt, t_sc]
            for j in range(4):
                t = pe.op(lambda e, j=j: e.matmul(P[j % 2][:, :], c["WT"][:, j * 128:(j + 1) * 128], CTX[0:64, b, :], start=True, stop=True),
                          t_wt, free[j % 2], t_ctx)
                yield 1
                free[j % 2] = dve.op(lambda e, j=j: e.scalar_tensor_tensor(out=xs[j], in0=P[j % 2][:, :], scalar=TG[:, 0:1], in1=xs[j], op0=ALU.mult, op1=ALU.add), t, t_tg)
                yield 1
            yield from stats(c, xs, [])
            t_rs = tk["rs"]
            xf = [[], []]
            for j in range(4):
                t_n = norm(c, j, c["XN"][j % 2], xs[j], t_rs, *xf[j % 2])
                t_f = flip(c["XN"][j % 2], P[j % 2], t_n, free[j % 2])
                i = 4 * b + j
                t_d = load(l_hn[b][j % 2], sp, HN[i * 128:(i + 1) * 128, :], c["XN"][j % 2], t_n)
                rows0.append(t_d)
                xf[j % 2] = [t_f, t_d]
                yield 1
                free[j % 2] = evac(j, c["HT"], P[j % 2], t_f)
                yield 1
            t_ht = free[1]
            t_xn = xf
            yield from back(P[1], RW0, E0, c["HT"], c["TT"], P[0], free[0], free[1], t_r0, *free)
            t_m, t_c, t = tk["back"]
            lg = P[1][:, 0:4 * E0].rearrange("p (a b) -> p a b", a=4)
            LG, EA, UU, LN_, BS, MS = (c[n] for n in ("LG", "EA", "UU", "LN", "BS", "MS"))
            tl = t
            act.op(lambda e: e.activation(EA, lg, ACT.Abs), tl)
            t = act.op(lambda e: e.activation(EA, EA, ACT.Exp, scale=-1.0))
            t_lg = t
            yield 1
            t = dve.op(lambda e: e.tensor_scalar(UU, EA, 1.0, None, ALU.add), t)
            t = act.op(lambda e: e.activation(LN_, UU, ACT.Ln), t)
            t_q = dve.op(lambda e: e.tensor_scalar(LG, lg, 0.0, None, ALU.max), tl)
            yield 1
            dve.op(lambda e: e.scalar_tensor_tensor(out=UU, in0=UU, scalar=-1.0, in1=EA, op0=ALU.add, op1=ALU.subtract), t)
            dve.op(lambda e: e.tensor_tensor(LG, LG, UU, ALU.subtract))
            t = dve.op(lambda e: e.tensor_tensor(LG, LG, LN_, ALU.add))
            yield 1
            t = dve.op(lambda e: e.tensor_scalar(UU, LG, 1e-37, None, ALU.max))
            act.op(lambda e: e.activation(LN_, UU, ACT.Ln), t)
            t = act.op(lambda e: e.activation(LN_, LN_, ACT.Exp, scale=0.5))
            yield 1
            dve.op(lambda e: e.reciprocal(EA, LN_), t)
            dve.op(lambda e: e.tensor_tensor(EA, EA, LG, ALU.mult))
            dve.op(lambda e: e.tensor_tensor(EA, EA, LN_, ALU.add))
            dve.op(lambda e: e.tensor_scalar(LG, EA, 0.5, None, ALU.mult))
            t = dve.op(lambda e: e.tensor_tensor(BS, LG, BIA.unsqueeze(1).broadcast_to([128, 4, E0]), ALU.add))
            yield 1
            yield from route(c, b, E0, K0, BS, LG, TG[:, 2:3], 1.5, [t_c, t_q, t_lg], P, CC, t_cc, 0)
            t_route = tk["cnt"]
            t_ss = tk["route"]
            free = [t_route, t_route]
            for m in range(2):
                for q in range(2):
                    def f(e, m=m, q=q):
                        base = 1024 * q
                        for k in range(4):
                            r = e.matmul(P[q][:, :], SW0[:, base + k * 256 + m * 128:base + k * 256 + (m + 1) * 128], c["HT"][:, k, :], start=(k == 0), stop=(k == 3))
                        return r
                    t = pe.op(f, t_sw, t_ht, free[q])
                    if q == 0:
                        ts = act.op(lambda e: e.activation(c["SS"], P[0][:, :], ACT.Silu), t, t_ss)
                        free[0] = ts
                    yield 1
                free[1] = dve.op(lambda e, m=m: e.tensor_tensor(c["INT"][:, m, :], c["SS"], P[1][:, :], ALU.mult), t, ts)
                t_ss = free[1]
                t_i = dve.op(lambda e, m=m: e.tensor_scalar(c["INT"][:, m, :], c["INT"][:, m, :], 10.0, -10.0, ALU.min, ALU.max))
                yield 1
            xf = t_xn
            for j in range(4):
                def f(e, j=j):
                    for k in range(2):
                        r = e.matmul(P[j % 2][:, :], c["INT"][:, k, j * 128:(j + 1) * 128], SW0[:, 2048 + k * 512:2560 + k * 512], start=(k == 0), stop=(k == 1))
                    return r
                t = pe.op(f, t_i, free[j % 2])
                yield 1
                i = 4 * b + j
                free[j % 2] = dve.op(lambda e, j=j: e.scalar_tensor_tensor(out=c["XN"][j % 2], in0=P[j % 2][:, :], scalar=TG[:, 2:3], in1=xs[j], op0=ALU.mult, op1=ALU.add), t, *xf[j % 2])
                t_d = load(l_acc[b][j % 2], sp, ACC[i * 128:(i + 1) * 128, :], c["XN"][j % 2], free[j % 2])
                accs0.append(t_d)
                xf[j % 2] = [t_d]
            t_end[b] = (t, free[1])
            yield 1

        def route(c, b, ne, kk, sel, val, wscale, factor, t_sel, P, CCx, t_ccx, layer):
            n = 4 * ne
            OHv = c["OH"].rearrange("p t (k e) -> p t k e", k=kk)
            TMv = c["TM"].rearrange("p t (k e) -> p t k e", k=kk)
            IDX, WK, DEN, ADR, VA, REC, ADI, MS = (c[x] for x in ("IDF", "WK", "DEN", "ADR", "VA", "REC", "ADI", "MS"))
            for j in range(4):
                dve.op(lambda e, j=j: e.max(c["MX"][:, j, :], sel[:, j, :]), *t_sel)
                dve.op(lambda e, j=j: e.max_index(c["MI"][:, j, :], c["MX"][:, j, :], sel[:, j, :]))
                if j % 2:
                    yield 1
            dve.op(lambda e: e.tensor_copy(IDX, c["MI"]))
            sh = [128, 4, kk, ne]
            iob = CON[:, C_IOTA:C_IOTA + ne].unsqueeze(1).unsqueeze(1).broadcast_to(sh)
            dve.op(lambda e: e.tensor_tensor(OHv, iob, IDX[:, :, 0:kk].unsqueeze(3).broadcast_to(sh), ALU.is_equal), t_con)
            t = dve.op(lambda e: e.tensor_reduce(MS, OHv.rearrange("p t k e -> p t e k"), AX.X, ALU.add))

            def cnt(e):
                e.matmul(P[0][:, 0:n], CON[:, C_U:C_U + 128], MS.rearrange("p t e -> p (t e)"), start=True, stop=True)
                return e.matmul(P[1][:, 0:n], CON[:, C_ONE:C_ONE + 128], MS.rearrange("p t e -> p (t e)"), start=True, stop=True)
            t_cnt = pe.op(cnt, t, *t_sel)
            yield 1
            dve.op(lambda e: e.tensor_tensor(TMv, OHv, val.unsqueeze(2).broadcast_to(sh), ALU.mult))
            dve.op(lambda e: e.tensor_reduce(WK, TMv, AX.X, ALU.add))
            dve.op(lambda e: e.tensor_reduce(DEN, WK, AX.X, ALU.add))
            yield 1
            dve.op(lambda e: e.reciprocal(DEN, DEN))
            dve.op(lambda e: e.tensor_scalar(DEN, DEN, wscale, factor, ALU.mult, ALU.mult), t_tg)
            dve.op(lambda e: e.tensor_tensor(REC[:, :, :, 1], WK, DEN.broadcast_to([128, 4, kk]), ALU.mult))
            t_rec = dve.op(lambda e: e.tensor_copy(REC[:, :, :, 0], CON[:, C_TOK + 4 * b:C_TOK + 4 * b + 4].unsqueeze(2).broadcast_to([128, 4, kk])))
            yield 1
            cc = CCx[:, b, :].rearrange("p (t e) -> p t e", e=ne)
            if b == 0:
                dve.op(lambda e: e.memset(cc[:, 0, :], 0.0))
            else:
                pv = CCx[:, b - 1, :].rearrange("p (t e) -> p t e", e=ne)
                dve.op(lambda e: e.tensor_copy(cc[:, 0, :], pv[:, 4, :]), t_ccx[b - 1])
            for j in range(4):
                t_ccx[b] = dve.op(lambda e, j=j: e.tensor_tensor(cc[:, j + 1, :], cc[:, j, :], P[1][:, j * ne:(j + 1) * ne], ALU.add), t_cnt)
            yield 1
            tk["cnt"] = dve.op(lambda e: e.tensor_tensor(MS, cc[:, 0:4, :], P[0][:, 0:n].rearrange("p (t e) -> p t e", e=ne), ALU.add))
            dve.op(lambda e: e.tensor_tensor(TMv, OHv, MS.unsqueeze(2).broadcast_to(sh), ALU.mult))
            t = dve.op(lambda e: e.tensor_reduce(ADR, TMv, AX.X, ALU.add))
            yield 1
            if layer == 0:
                tr = CON[:, C_TR + 4 * K0 * b:C_TR + 4 * K0 * (b + 1)].rearrange("p (t k) -> p t k", k=kk)
                dve.op(lambda e: e.tensor_scalar(VA, ADR, float(CAP), None, ALU.is_lt))
                dve.op(lambda e: e.scalar_tensor_tensor(out=ADR, in0=IDX[:, :, 0:kk], scalar=float(CAP), in1=ADR, op0=ALU.mult, op1=ALU.add))
                dve.op(lambda e: e.tensor_tensor(ADR, ADR, tr, ALU.subtract))
                dve.op(lambda e: e.tensor_tensor(ADR, ADR, VA, ALU.mult))
                dve.op(lambda e: e.tensor_tensor(ADR, ADR, tr, ALU.add))
            else:
                dve.op(lambda e: e.scalar_tensor_tensor(out=ADR, in0=IDX[:, :, 0:kk], scalar=2048.0, in1=ADR, op0=ALU.mult, op1=ALU.add))
            t = dve.op(lambda e: e.tensor_copy(ADI, ADR))
            tk["route"] = t
            lists = LIST0 if layer == 0 else LIST1
            for j in range(4):
                for k in range(kk):
                    tk[f"list{layer}"] = (l_sc if layer == 0 else l_sc1).dma(pool, lambda e, j=j, k=k: e.indirect_dma_start(
                        lists, bass.IndirectOffsetOnAxis(ap=ADI[:, j, k:k + 1], axis=0), REC[:, j, k, :], None), t, t_rec, t_init)
            yield 1

        m = matrix()
        for _ in m:
            pass
        merge(*[(10 * b, chain0(b)) for b in range(4)])
        t_sh0 = (pe.sem, pe.count)
        t_shd = (dve.sem, dve.count)
        t_list0 = tk["list0"]
        t_acc_rows, t_rows0 = accs0, rows0

        l_lb = land("l_lb")
        t_lb = load(l_lb, sp, LB.rearrange("p a b -> p (a b)"), LIST0[0:TRASH0, :].rearrange("(a b) c -> a (b c)", a=64), t_list0, t_shd, *t_acc_rows)

        def fl(e):
            e.transpose(PB[6][0:HALF, 0:64], LB[:, :, 0], ident[0:64, 0:64])
            return e.transpose(PB[6][0:HALF, 64:128], LB[:, :, 1], ident[0:64, 0:64])
        t_fl = pe.op(fl, t_lb, t_shd)
        IDI = IDS.bitcast(I32)
        t_ids = dve.op(lambda e: e.tensor_copy(IDI[0:HALF, :], PB[6][0:HALF, 0:64]), t_fl)
        t_wsl = dve.op(lambda e: e.tensor_copy(WSL[0:HALF, :], PB[6][0:HALF, 64:128]), t_fl)

        l_g = [land(f"l_g{i}") for i in range(4)]
        l_add = [land("l_add0"), land("l_add1")]
        wr_free = [None, None, t_sh0, tk["early"]]
        g_free = [t_shd] * 4
        ys_free = [t_shd] * 4
        in_free = [t_shd, t_shd]
        t_add = [None, None]
        pxt, pgu, pyy = [t_shd] * 2, [t_shd] * 2, [t_shd, t_wsl]
        xt_free = [None, None]

        def fetch_w(e_):
            st[e_] = [load(l_wr[e_ % 4], sp, WR[e_ % 4], a["we0"][e_], wr_free[e_ % 4])]

        def fetch(e_):
            tg_ = []
            for h in range(2):
                s = (2 * e_ + h) % 4
                tg_.append(l_g[s].dma(pool, lambda e, s=s, h=h: e.indirect_dma_start(
                    G[s], None, HN, bass.IndirectOffsetOnAxis(ap=IDI[0:HALF, 2 * e_ + h:2 * e_ + h + 1], axis=0)),
                    t_ids, g_free[s], *t_rows0, t_init))
            st[e_].append(tg_)

        def turn(e_):
            t_wr, tg_ = st[e_]
            tc = []
            for h in range(2):
                s = (2 * e_ + h) % 4

                def f(e, s=s, h=h):
                    for k in range(4):
                        r = e.transpose(PB[h][:, k * HALF:(k + 1) * HALF], G[s][:, k * 128:(k + 1) * 128], ident[0:HALF, 0:HALF])
                    return r
                t = pe.op(f, tg_[h], pxt[h])
                g_free[s] = t
                src = PB[h][:, 0:4 * HALF].rearrange("p (k t) -> p k t", k=4)
                dst = XT[e_ % 2][:, :, h * HALF:(h + 1) * HALF]
                if h == 0:
                    t = act.op(lambda e, src=src, dst=dst: e.activation(dst, src, ACT.Copy), t, xt_free[e_ % 2])
                else:
                    t = dve.op(lambda e, src=src, dst=dst: e.tensor_copy(dst, src), t, xt_free[e_ % 2])
                pxt[h] = t
                tc.append(t)
            st[e_].append(tc)

        def up(e_):
            t_wr, tg_, tc = st[e_]
            pg, pu = PB[2 + 2 * (e_ % 2)], PB[3 + 2 * (e_ % 2)]

            def f(e):
                for ps, base in ((pg, 0), (pu, 1024)):
                    for m in range(2):
                        for k in range(4):
                            r = e.matmul(ps[:, m * CAP:(m + 1) * CAP], WR[e_ % 4][:, base + k * 256 + m * 128:base + k * 256 + (m + 1) * 128], XT[e_ % 2][:, k, :], start=(k == 0), stop=(k == 3))
                return r
            t = pe.op(f, t_wr, *tc, pgu[e_ % 2])
            xt_free[e_ % 2] = t
            sl, inn = SL0[e_ % 2].rearrange("p a b -> p (a b)"), IN0[e_ % 2].rearrange("p a b -> p (a b)")
            ts = act.op(lambda e: e.activation(sl, pg[:, 0:2 * CAP], ACT.Silu), t, pgu[e_ % 2])
            td = dve.op(lambda e: e.tensor_tensor(inn, sl, pu[:, 0:2 * CAP], ALU.mult), ts, in_free[e_ % 2])
            pgu[e_ % 2] = td
            st[e_].append(td)

        def down(e_):
            nonlocal t_add
            td = st[e_][3]
            new = [None, None]
            for h in range(2):
                s = (2 * e_ + h) % 4

                def f(e, h=h):
                    for k in range(2):
                        r = e.matmul(PB[6 + h][0:HALF, :], IN0[e_ % 2][:, k, h * HALF:(h + 1) * HALF], WR[e_ % 4][:, 2048 + k * 512:2560 + k * 512], start=(k == 0), stop=(k == 1))
                    return r
                t = pe.op(f, td, pyy[h])
                wsc = WSL[0:HALF, 2 * e_ + h:2 * e_ + h + 1]
                if h == 0:
                    ty = act.op(lambda e, s=s, wsc=wsc: e.activation(YS[s], PB[6][0:HALF, :], ACT.Copy, scale=wsc), t, ys_free[s], t_wsl)
                else:
                    ty = dve.op(lambda e, s=s, wsc=wsc: e.tensor_scalar(YS[s], PB[7][0:HALF, :], wsc, None, ALU.mult), t, ys_free[s], t_wsl)
                pyy[h] = ty
                new[h] = l_add[h].dma(pool, lambda e, s=s, h=h: e.indirect_dma_start(
                    ACC, bass.IndirectOffsetOnAxis(ap=IDI[0:HALF, 2 * e_ + h:2 * e_ + h + 1], axis=0), YS[s], None, compute_op=ALU.add),
                    ty, *t_add, t_ids, *t_acc_rows, t_init)
                ys_free[s] = new[h]
            t_add = new
            wr_free[e_ % 4] = t
            in_free[e_ % 2] = t

        fetch_w(2)
        fetch_w(3)
        fetch(0)
        fetch(1)
        turn(0)
        for e_ in range(E0):
            up(e_)
            if e_ + 1 < E0:
                turn(e_ + 1)
            if e_ + 2 < E0:
                fetch(e_ + 2)
            down(e_)
            if e_ + 4 < E0:
                fetch_w(e_ + 4)
        t_end0 = (pe.sem, pe.count)
        t_end0d = (dve.sem, dve.count)
        t_end0a = (act.sem, act.count)

        xr = [S(8704, 4, D), S(30464, 4, D)]
        htr = [S(10752, 4, 512), S(32512, 4, 512)]
        BD, BDV = S(12800, 4, 4 * 64), S(13824, 8, 64)
        PP, PTt = S(14336, 16, 64), S(15360, 8, 128)
        HC, MN = S(16384, 4, 128), S(16896, 512)
        I1v = [S(17408, 6, D), S(27392, 6, D)]
        XC = [S(20480, D), S(20992, D)]
        SGU = S(21760, 2, 4, SI)
        late = taker(RING, 53120)
        SWD = late(6, D)
        SS1 = [late(D) for _ in range(2)]
        AC1 = [late(D) for _ in range(2)]
        RW1, SB1, CC1 = late(4, E1), late(12), late(4, 5 * E1)
        LB1 = late(256, p1=NT)
        TT1 = late(D, p1=8)
        SMX, SSM, PRM, PRS = late(16), late(16), late(4), late(4)
        c1 = []
        for b in range(2):
            c = {"OH": late(4, 2 * E1), "TM": late(4, 2 * E1), "PR": late(4, E1), "MS": late(4, E1)}
            c["ST"], c["MV"], c["RS"], c["R2"] = late(4, 6), late(4, 2), late(4), late(4)
            c["MX"], c["MI"], c["IDF"] = late(4, 8), late(4, 8).bitcast(U32), late(4, 8)
            c["WK"], c["DEN"], c["ADR"], c["VA"] = late(4, K1), late(4, 1), late(4, K1), late(4, K1)
            c1.append(c)
        recs = [(late(4, K1, 2), late(4, K1).bitcast(I32)) for _ in range(4)]
        NB, NC, NTL = late(8), late(8), late(8)
        NI = late(8).bitcast(I32)
        CMP, ETF, ETK, BLF = late(NT, 8), late(NT), late(NT).bitcast(I32), late(NT)
        BLI = late(1).bitcast(I32)
        l_w1 = land("l_w1")
        load(l_w1, sp, S(0, 2, WE1), a["we1"][0:2].rearrange("e p n -> p e n"), t_end0, t_end0d, t_end0a)
        l_s1 = land("l_s1")
        load(l_s1, act, RW1, a["rw1"], t_end0, *t_add)
        t_s1 = load(l_s1, act, SB1, a["sb1"])
        l_sgu = land("l_sgu")
        load(l_sgu, act, SGU[:, 0, :, :], a["sg1"].rearrange("(k p) n -> p k n", p=128), t_end0, t_end0d)
        t_sgu = load(l_sgu, act, SGU[:, 1, :, :], a["su1"].rearrange("(k p) n -> p k n", p=128))
        t_swd = load(land("l_swd"), act, SWD, a["sd1"].rearrange("(k p) n -> p k n", p=128))
        l_xb = [land(f"l_xb{i}") for i in range(2)]
        l_sc1 = land("l_sc1")
        mask_m = CON[:, C_CM:C_CM + 64].unsqueeze(1).broadcast_to([128, 8, 64])
        mask_a = CON[:, C_CA:C_CA + 64].unsqueeze(1).broadcast_to([128, 8, 64])
        Q = [PB[6], PB[7]]
        x_free = [[t_end0, t_end0d, t_end0a, *t_add], [t_end0, t_end0d, t_end0a, *t_add]]
        ht_free = [None, None]
        z1 = dve.op(lambda e: e.memset(BD, 0.0), *x_free[0])
        z2 = dve.op(lambda e: e.memset(BDV, 0.0))
        t_one = None
        for q in range(2):
            t_one = dve.op(lambda e, q=q: e.memset(I1v[q][64:65, 5, :], 1.0), *x_free[0])
        l_h2 = [land("l_h20"), land("l_h21")]
        rows1, accs1 = [], []
        xc_free = [[], []]
        q_free = [t_end0a, t_end0d]
        t_cc1 = [None] * 4
        tl = {}
        t_xload = {}

        def load_x(b):
            t_xload[b] = load(l_xb[b % 2], sp, xr[b % 2], ACC[b * 512:(b + 1) * 512, :].rearrange("(t p) d -> p t d", p=128), *x_free[b % 2])

        def pre1(b):
            c = c1[b % 2]
            x = xr[b % 2]
            xs = [x[:, j, :] for j in range(4)]
            if b < 2:
                load_x(b)
            def fc(e):
                for k in range(4):
                    r = e.transpose(Q[0][:, k * 64:(k + 1) * 64], CTX[0:64, b, k * 128:(k + 1) * 128], ident[0:64, 0:64])
                return r
            t = pe.op(fc, q_free[0])
            t_mean = pe.op(lambda e: e.matmul(Q[1][:, :], CON[0:64, C_INV:C_INV + 128], CTX[0:64, b, :], start=True, stop=True), q_free[1])
            t_bdv = None
            for q in range(2):
                src = CTX[64 * q:64 * q + 64, b, :].rearrange("p (a c d) -> p a c d", c=2, d=32)[:, :, q, :]
                dve.op(lambda e, q=q, src=src: e.tensor_copy(BDV[64 * q:64 * q + 64, :, 32 * q:32 * q + 32], src), tl.get("o"))
            yield 1
            for r in range(4):
                src = Q[0][32 * r:32 * r + 32, 0:256].rearrange("p (k s) -> p k s", k=4)
                dst = BD[32 * r:32 * r + 32, :, 64 * r:64 * r + 64]
                t_bd = act.op(lambda e, src=src, dst=dst: e.activation(dst, src, ACT.Copy), t, z1, tl.get("s"))
            q_free[0] = t_bd
            q_free[1] = dve.op(lambda e: e.tensor_scalar(MN, Q[1][:, :], TG[:, 1:2], None, ALU.mult), t_mean)
            yield 1
            yield from stats(c, [xs[3]], [t_xload[b]])
            t_n = norm(c, 0, XC[0], xs[3], tk["rs"], *xc_free[0])
            t_f = flip(XC[0], Q[0], t_n, q_free[0])
            xc_free[0] = [t_f]
            for j in range(2):
                dve.op(lambda e, j=j: e.tensor_tensor(xs[j], xs[j], MN, ALU.add))
            yield 1
            t_h = act.op(lambda e: e.activation(HC.rearrange("p a b -> p (a b)"), Q[0][:, :], ACT.Copy), t_f)
            t = dve.op(lambda e: e.tensor_tensor(xs[2], xs[2], MN, ALU.add))
            yield 1

            def fs(e):
                for k in range(4):
                    r = e.matmul(Q[k // 2][:, (k % 2) * 256:(k % 2 + 1) * 256], HC[:, k, :], BD[:, k, :], start=True, stop=True)
                return r
            t = pe.op(fs, t_h, t_bd, q_free[1])
            tl["s"] = t
            yield 1
            for q in range(2):
                src = Q[q][:, :].rearrange("p (g s) -> p g s", s=64)
                dve.op(lambda e, q=q, src=src: e.tensor_tensor(PP[:, 8 * q:8 * q + 8, :], src, mask_m, ALU.mult), t)
                t2 = dve.op(lambda e, q=q: e.tensor_tensor(PP[:, 8 * q:8 * q + 8, :], PP[:, 8 * q:8 * q + 8, :], mask_a, ALU.add))
                yield 1
            dve.op(lambda e: e.tensor_reduce(SMX, PP, AX.X, ALU.max))
            t = dve.op(lambda e: e.tensor_tensor(PP, PP, SMX.unsqueeze(2).broadcast_to([128, 16, 64]), ALU.subtract))
            t = act.op(lambda e: e.activation(PP.rearrange("p a b -> p (a b)"), PP.rearrange("p a b -> p (a b)"), ACT.Exp), t)
            yield 1
            for j in range(3):
                dve.op(lambda e, j=j: e.bn_stats(c["ST"][:, j, :], xs[j]))
                dve.op(lambda e, j=j: e.bn_aggr(c["MV"][:, j, :], c["ST"][:, j, :]))
                yield 1
            dve.op(lambda e: e.tensor_reduce(SSM, PP, AX.X, ALU.add), t)
            dve.op(lambda e: e.reciprocal(SSM, SSM))
            t = dve.op(lambda e: e.tensor_tensor(PP, PP, SSM.unsqueeze(2).broadcast_to([128, 16, 64]), ALU.mult))
            yield 1

            def fp(e):
                for j in range(8):
                    r = e.transpose(Q[j // 4][:, (j % 4) * 128:(j % 4 + 1) * 128], PP[:, 2 * j:2 * j + 2, :].rearrange("p a b -> p (a b)"), ident)
                return r
            t = pe.op(fp, t)
            yield 1
            for j in range(2):
                t_pt = act.op(lambda e, j=j: e.activation(PTt[:, 4 * j:4 * j + 4, :].rearrange("p a b -> p (a b)"), Q[j][:, :], ACT.Copy), t, tl.get("o"))
            yield 1

            def fo(e):
                for j in range(8):
                    r = e.matmul(Q[0][:, j * 64:(j + 1) * 64], PTt[:, j, :], BDV[:, j, :], start=True, stop=True)
                return r
            t = pe.op(fo, t_pt, z2, (dve.sem, dve.count))
            tl["o"] = t
            yield 1
            q_free[0] = dve.op(lambda e: e.scalar_tensor_tensor(out=xs[3], in0=Q[0][:, :], scalar=TG[:, 1:2], in1=xs[3], op0=ALU.mult, op1=ALU.add), t)
            q_free[1] = t_pt
            dve.op(lambda e: e.bn_stats(c["ST"][:, 3, :], xs[3]))
            t = dve.op(lambda e: e.bn_aggr(c["MV"][:, 3, :], c["ST"][:, 3, :]))
            yield 1
            yield from rstd(c["RS"], c["R2"], c["MV"][:, :, 1], t)
            t_rs = tk["rs"]
            for j in range(4):
                t_n = norm(c, j, XC[j % 2], xs[j], t_rs, *xc_free[j % 2])
                t_f = flip(XC[j % 2], Q[j % 2], t_n, q_free[j % 2])
                i = 4 * b + j
                t_d = load(l_h2[j % 2], sp, HN2[i * 128:(i + 1) * 128, :], XC[j % 2], t_n)
                rows1.append(t_d)
                xc_free[j % 2] = [t_f, t_d]
                yield 1
                q_free[j % 2] = evac(j, htr[b % 2], Q[j % 2], t_f, ht_free[b % 2])
                yield 1
            tl[("ht", b)] = q_free[1]
            yield from back(Q[1], RW1, E1, htr[b % 2], TT1, Q[0], q_free[0], q_free[1], t_s1, *q_free)
            t_m, t_c, t = tk["back"]
            PR = c["PR"]
            lgv = Q[1][:, 0:4 * E1].rearrange("p (t e) -> p t e", e=E1)
            dve.op(lambda e: e.tensor_reduce(PRM, lgv, AX.X, ALU.max), t)
            t = dve.op(lambda e: e.tensor_tensor(PR, lgv, PRM.unsqueeze(2).broadcast_to([128, 4, E1]), ALU.subtract))
            t_q = t
            t = act.op(lambda e: e.activation(PR, PR, ACT.Exp), t)
            yield 1
            dve.op(lambda e: e.tensor_reduce(PRS, PR, AX.X, ALU.add), t)
            dve.op(lambda e: e.reciprocal(PRS, PRS))
            dve.op(lambda e: e.tensor_tensor(PR, PR, PRS.unsqueeze(2).broadcast_to([128, 4, E1]), ALU.mult))
            yield 1
            cr = dict(c)
            cr["REC"], cr["ADI"] = recs[b]
            yield from route(cr, b, E1, K1, PR, PR, TG[:, 3:4], 1.0, [t_c, t_q], Q, CC1, t_cc1, 1)
            q_free[0] = q_free[1] = tk["cnt"]
            yield 1

        def slots():
            cur = CC1[:, 3, :].rearrange("p (t e) -> p t e", e=E1)[:, 4, :]
            dve.op(lambda e: e.tensor_scalar(NB, cur, 127.0, None, ALU.add))
            dve.op(lambda e: e.tensor_copy(NI, NB))
            dve.op(lambda e: e.tensor_scalar(NI, NI, 7, None, ALU.logical_shift_right))
            dve.op(lambda e: e.tensor_copy(NB, NI))
            dve.op(lambda e: e.tensor_copy(NTL, NB))
            c2, o2 = NB, NC
            for s_ in (1, 2, 4):
                dve.op(lambda e, s_=s_, c2=c2, o2=o2: e.tensor_copy(o2[:, 0:s_], c2[:, 0:s_]))
                dve.op(lambda e, s_=s_, c2=c2, o2=o2: e.tensor_tensor(o2[:, s_:8], c2[:, s_:8], c2[:, 0:8 - s_], ALU.add))
                c2, o2 = o2, c2
            yield 1
            i39 = CON[:, C_I39:C_I39 + NT * 8].rearrange("p (a b) -> p a b", b=8)
            dve.op(lambda e: e.tensor_tensor(CMP, i39, c2.unsqueeze(1).broadcast_to([128, NT, 8]), ALU.is_ge))
            dve.op(lambda e: e.tensor_reduce(ETF, CMP[:, :, 0:7], AX.X, ALU.add))
            t = dve.op(lambda e: e.tensor_scalar(ETK, ETF, float(WE1), None, ALU.mult))
            tk["et"] = t
            dve.op(lambda e: e.tensor_tensor(CMP, CMP, NTL.unsqueeze(1).broadcast_to([128, NT, 8]), ALU.mult))
            dve.op(lambda e: e.tensor_reduce(BLF, CMP, AX.X, ALU.add))
            dve.op(lambda e: e.tensor_tensor(BLF, i39[:, :, 0], BLF, ALU.subtract))
            dve.op(lambda e: e.scalar_tensor_tensor(out=BLF, in0=ETF, scalar=16.0, in1=BLF, op0=ALU.mult, op1=ALU.add))
            yield 1
            dve.op(lambda e: e.tensor_tensor(ETF, i39[:, :, 0], c2[:, 7:8].broadcast_to([128, NT]), ALU.is_ge))
            dve.op(lambda e: e.tensor_scalar(CMP[:, :, 0], BLF, -1.0, 128.0, ALU.mult, ALU.add))
            dve.op(lambda e: e.tensor_tensor(CMP[:, :, 0], CMP[:, :, 0], ETF, ALU.mult))
            dve.op(lambda e: e.tensor_tensor(BLF, BLF, CMP[:, :, 0], ALU.add))
            dve.op(lambda e: e.tensor_tensor(ETF[0:NT, :], BLF[0:NT, :], ident[0:NT, 0:NT], ALU.mult))
            dve.op(lambda e: e.tensor_reduce(BLF[0:NT, 0:1], ETF[0:NT, :], AX.X, ALU.add))
            t = dve.op(lambda e: e.tensor_copy(BLI[0:NT, :], BLF[0:NT, 0:1]))
            yield 1
            l_b = land("l_lb1")
            t = l_b.dma(pool, lambda e: e.indirect_dma_start(
                LB1, None, LIST1.rearrange("(a b) c -> a (b c)", b=128), bass.IndirectOffsetOnAxis(ap=BLI[0:NT, :], axis=0)), t, tk["list1"], t_init)
            LB1v = LB1.rearrange("p (a b) -> p a b", b=2)

            def fl1(e):
                e.transpose(Q[0][:, 0:NT], LB1v[:, :, 0], ident[0:NT, 0:NT])
                return e.transpose(Q[0][:, 64:64 + NT], LB1v[:, :, 1], ident[0:NT, 0:NT])
            tk["fl1"] = (fl1, t)
            yield 1

        NM = 6
        ups = [None, None]
        ss_free = [None, None]
        int_free = [t_one, t_one]
        ac_free = [[], []]
        py = [None, None]
        un = [0]
        l_ac1 = [land("l_ac10"), land("l_ac11")]

        def shared1(b):
            ht, inter = htr[b % 2], I1v[b % 2]
            for m in range(NM):
                w = 128 if m < 5 else 64
                u = un[0] % 2
                un[0] += 1
                pg, pu = PB[2 * u], PB[2 * u + 1]
                for q, ps in ((0, pg), (1, pu)):
                    def f(e, m=m, w=w, q=q, ps=ps):
                        for k in range(4):
                            r = e.matmul(ps[0:w, :], SGU[:, q, k, m * 128:m * 128 + w], ht[:, k, :], start=(k == 0), stop=(k == 3))
                        return r
                    t = pe.op(f, t_sgu, tl[("ht", b)], ups[u], t_end0d, t_end0a)
                    if q == 0:
                        ts = act.op(lambda e, u=u, pg=pg, w=w, m=m: e.activation(SS1[u][0:w, :], pg[0:w, :], ACT.Silu, bias=SB1[0:w, m:m + 1]), t, ss_free[u], t_s1)
                    yield 1
                td = dve.op(lambda e, u=u, pu=pu, m=m, w=w: e.scalar_tensor_tensor(out=inter[0:w, m, :], in0=pu[0:w, :], scalar=SB1[0:w, 6 + m:7 + m], in1=SS1[u][0:w, :], op0=ALU.add, op1=ALU.mult), t, ts, int_free[b % 2])
                ups[u] = td
                ss_free[u] = td
            ht_free[b % 2] = t
            tk["up_end"] = t
            for j in range(4):
                def f(e, j=j):
                    for k in range(6):
                        kp = 128 if k < 5 else 65
                        r = e.matmul(PB[4 + j % 2][:, :], inter[0:kp, k, j * 128:(j + 1) * 128], SWD[0:kp, k, :], start=(k == 0), stop=(k == 5))
                    return r
                t = pe.op(f, td, py[j % 2], t_swd, t_end0d, t_end0a)
                i = 4 * b + j
                py[j % 2] = dve.op(lambda e, j=j: e.scalar_tensor_tensor(out=AC1[j % 2], in0=PB[4 + j % 2][:, :], scalar=TG[:, 3:4], in1=xr[b % 2][:, j, :], op0=ALU.mult, op1=ALU.add), t, *ac_free[j % 2])
                t_d = load(l_ac1[j % 2], sp, ACC2[i * 128:(i + 1) * 128, :], AC1[j % 2], py[j % 2])
                accs1.append(t_d)
                ac_free[j % 2] = [t_d]
                yield 1
            int_free[b % 2] = t
            x_free[b % 2] = [py[1]]
            if b + 2 < 4:
                load_x(b + 2)
            yield 1

        def w1_part(e0, e1, *waits):
            return load(l_w1, sp, S(e0 * WE1, e1 - e0, WE1), a["we1"][e0:e1].rearrange("e p n -> p e n"), *waits)

        merge((0, pre1(0)))
        for b in range(3):
            merge((0, shared1(b)), (0, pre1(b + 1)))
        s3 = shared1(3)
        w1_part(2, 5, (pe.sem, pe.count), (dve.sem, dve.count), (act.sem, act.count), *rows1)
        merge((0, s3), (0, slots()))
        w1_part(5, 6, tk["up_end"])
        fl1, t = tk["fl1"]
        t_fl1 = pe.op(fl1, t, q_free[0])
        IDI = IDS.bitcast(I32)
        t_ids1 = dve.op(lambda e: e.tensor_copy(IDI[:, 0:NT], Q[0][:, 0:NT]), t_fl1)
        t_wsl1 = dve.op(lambda e: e.tensor_copy(WSL[:, 0:NT], Q[0][:, 64:64 + NT]), t_fl1)
        t_etk = tk["et"]
        t_sh1 = (pe.sem, pe.count)
        t_sh1d = (dve.sem, dve.count)
        t_acc2, t_rows1 = accs1, rows1
        t_w1 = w1_part(6, 8, t_sh1, t_sh1d)

        G1 = [late(512) for _ in range(2)]
        XT1 = [late(4, 128) for _ in range(2)]
        SL1 = [late(I1) for _ in range(2)]
        IN1 = [late(I1) for _ in range(2)]
        NT1 = [late(3, 128) for _ in range(2)]
        YS1 = [late(512) for _ in range(3)]
        g_free = [t_sh1] * 2
        xt_free = [t_sh1] * 2
        sl_free = [t_sh1] * 2
        inn_free = [t_sh1] * 2
        nt_free = [t_sh1] * 2
        ys_free = [t_sh1] * 3
        p_xt, p_it = t_sh1d, t_sh1d
        p_gu = [t_sh1d] * 2
        p_y = [t_sh1d] * 2
        st = {}
        t_add = None

        def fetch1(n):
            st[n] = [l_g[n % 2].dma(pool, lambda e: e.indirect_dma_start(
                G1[n % 2], None, HN2, bass.IndirectOffsetOnAxis(ap=IDI[:, n:n + 1], axis=0)), t_ids1, g_free[n % 2], *t_rows1)]

        def turn1(n):
            nonlocal p_xt

            def f(e):
                for k in range(4):
                    r = e.transpose(PB[0][:, k * 128:(k + 1) * 128], G1[n % 2][:, k * 128:(k + 1) * 128], ident)
                return r
            t = pe.op(f, st[n][0], p_xt)
            g_free[n % 2] = t
            p_xt = act.op(lambda e: e.activation(XT1[n % 2].rearrange("p a b -> p (a b)"), PB[0][:, :], ACT.Copy), t, xt_free[n % 2])
            st[n].append(p_xt)

        def up1(n, reg):
            pg, pu = PB[2 + 2 * (n % 2)], PB[3 + 2 * (n % 2)]

            def f(e):
                r0 = e.value_load(ETK[0:1, n:n + 1], min_val=0, max_val=7 * WE1)
                regs[n] = r0
                for q, ps in ((0, pg), (1, pu)):
                    for k in range(4):
                        r = e.matmul(ps[:, 0:I1], XT1[n % 2][:, k, :], W1[:, bass.ds(r0 + (q * 4 + k) * I1, I1)], start=(k == 0), stop=(k == 3))
                return r
            t = pe.op(f, st[n][1], p_gu[n % 2], t_w1, t_etk)
            xt_free[n % 2] = t
            ts = act.op(lambda e: e.activation(SL1[n % 2], pg[:, 0:I1], ACT.Silu), t, sl_free[n % 2])
            td = dve.op(lambda e: e.tensor_tensor(IN1[n % 2], SL1[n % 2], pu[:, 0:I1], ALU.mult), ts, inn_free[n % 2])
            sl_free[n % 2] = td
            p_gu[n % 2] = td
            st[n].append(td)

        def flip1(n):
            nonlocal p_it

            def f(e):
                for k in range(3):
                    w = 128 if k < 2 else 96
                    r = e.transpose(PB[1][0:w, k * 128:(k + 1) * 128], IN1[n % 2][:, k * 128:k * 128 + w], ident)
                return r
            t = pe.op(f, st[n][2], p_it)
            inn_free[n % 2] = t
            dve.op(lambda e: e.tensor_copy(NT1[n % 2][:, 0:2, :].rearrange("p a b -> p (a b)"), PB[1][:, 0:256]), t, nt_free[n % 2])
            p_it = dve.op(lambda e: e.tensor_copy(NT1[n % 2][0:96, 2, :], PB[1][0:96, 256:384]), t, nt_free[n % 2])
            st[n].append(p_it)

        def down_1(n):
            nonlocal t_add

            def f(e):
                r0 = regs[n]
                for k in range(3):
                    w = 128 if k < 2 else 96
                    r = e.matmul(PB[6 + n % 2][:, :], NT1[n % 2][0:w, k, :], W1[0:w, bass.ds(r0 + 8 * I1 + k * 512, 512)], start=(k == 0), stop=(k == 2))
                return r
            t = pe.op(f, st[n][3], p_y[n % 2])
            nt_free[n % 2] = t
            ty = act.op(lambda e: e.activation(YS1[n % 3], PB[6 + n % 2][:, :], ACT.Copy, scale=WSL[:, n:n + 1]), t, ys_free[n % 3], t_wsl1)
            p_y[n % 2] = ty
            t_add = l_add[0].dma(pool, lambda e: e.indirect_dma_start(
                ACC2, bass.IndirectOffsetOnAxis(ap=IDI[:, n:n + 1], axis=0), YS1[n % 3], None, compute_op=ALU.add), ty, t_add, *t_acc2)
            ys_free[n % 3] = t_add

        regs = {}
        fetch1(0)
        fetch1(1)
        turn1(0)
        for n in range(NT):
            up1(n, None)
            if n + 1 < NT:
                turn1(n + 1)
            if n + 2 < NT:
                fetch1(n + 2)
            if n:
                down_1(n - 1)
            flip1(n)
        down_1(NT - 1)

        l_out = land("l_out")
        t_out = load(l_out, sp, out.rearrange("b s d -> (b s) d"), ACC2[0:2048, :], t_add)
        sp.op(lambda e: e.wait_ge(l_out.sem, l_out.count) or e, sig=False)

        @block.tensor
        def _(e):
            pe.play(e)

        @block.vector
        def _(e):
            dve.play(e)

        @block.scalar
        def _(e):
            act.play(e)

        @block.gpsimd
        def _(e):
            pool.play(e)

        @block.sync
        def _(e):
            sp.play(e)


def kernel(**inp):
    import concourse.bacc as bacc
    from concourse.bass_utils import run_bass_kernel_spmd as run
    v = {k: np.asarray(x) for k, x in inp.items()}

    def cols(w):
        c, n = w.shape[-2:]
        t = -(-c // 128)
        w = np.concatenate([w, np.zeros(w.shape[:-2] + (t * 128 - c, n), w.dtype)], axis=-2)
        w = w.reshape(w.shape[:-2] + (t, 128, n))
        w = np.swapaxes(w, -3, -2)
        return w.reshape(w.shape[:-2] + (t * n,))

    sw = np.swapaxes
    we0 = np.concatenate([cols(sw(v["L0_ffn_w_gate"], 1, 2)), cols(sw(v["L0_ffn_w_up"], 1, 2)), cols(sw(v["L0_ffn_w_down"], 1, 2))], axis=-1)
    sw0 = np.concatenate([cols(v["L0_ffn_sg"].T), cols(v["L0_ffn_su"].T), cols(v["L0_ffn_sd"].T)], axis=-1)
    we1 = np.concatenate([cols(v["L1_ffn_gate_w"]), cols(v["L1_ffn_up_w"]), cols(v["L1_ffn_down_w"])], axis=-1)
    sd1 = np.zeros((768, D), np.float32)
    sd1[0:SI] = v["L1_ffn_s_down_w"]
    sd1[SI] = v["L1_ffn_s_down_b"]
    sb1 = np.zeros((2, 768), np.float32)
    sb1[0, 0:SI] = v["L1_ffn_s_gate_b"]
    sb1[1, 0:SI] = v["L1_ffn_s_up_b"]
    con, l0, l1 = constants()

    def kp(w):
        return w.reshape(4, 128, -1).transpose(1, 0, 2)
    arrays = {
        "x": v["x"], "ctx": v["ctx_2048"], "itok": v["itok_Sx4_0_63"],
        "g": np.broadcast_to(np.concatenate([v["g_xattn"], v["g_ffn"]])[None, :], (128, 4)),
        "descT": kp(v["L0_xattn_desc_router"].T), "wq": v["L0_xattn_W_q"],
        "bq": v["L0_xattn_b_q"].reshape(4, 128).T,
        "rw0": kp(v["L0_ffn_gate_w"].T), "bias": np.broadcast_to(v["L0_ffn_bias"][None, :], (128, E0)),
        "we0": we0, "sw0": sw0, "rw1": kp(v["L1_ffn_router_w"].T), "we1": we1,
        "sg1": v["L1_ffn_s_gate_w"], "su1": v["L1_ffn_s_up_w"], "sd1": sd1,
        "sb1": sb1.reshape(2, 6, 128).transpose(2, 0, 1).reshape(128, 12),
        "con": con, "l0": l0, "l1": l1, "zero": np.zeros((ROWS - 2048, D), np.float32),
    }
    nc = bacc.Bacc("TRN2", target_bir_lowering=False, num_devices=1)
    given, aps = {}, {}
    for name, x in arrays.items():
        x = np.ascontiguousarray(x)
        given[f"in_{name}"] = x
        aps[name] = nc.dram_tensor(f"in_{name}", x.shape, mybir.dt.from_np(x.dtype), kind="ExternalInput").ap()
    o = nc.dram_tensor("out_0", (4, 512, 512), F32, kind="ExternalOutput").ap()
    program(nc, aps, o)
    r = run(nc, [given], core_ids=[0])
    return r.results[0]["out_0"]
```

```python
import numpy as np
import concourse.bass as bass
from concourse import mybir
from contextlib import ExitStack

F32 = mybir.dt.float32
F32R = mybir.dt.float32r
I32 = mybir.dt.int32
U32 = mybir.dt.uint32
ALU = mybir.AluOpType
ACT = mybir.ActivationFunctionType
AX = mybir.AxisListType

T = 16
D = 512
E0, K0, I0, CAP = 32, 6, 256, 192
HALF = CAP // 2
E1, K1, I1, SI = 8, 2, 352, 704
NT = 39
CHUNK_START, MATRIX_START, SHARED0_RANK, ENTRY_RANK, GAP0, HOP0 = 15, 10, 1, 0, 0, 0.05
ATTEND_START, SHARED1_RANK, SLOTS_RANK, LIST1_WAIT, GAP1, HOP1 = 10, 3, 2, 36, 0.2, 0.1
MN0 = 10752
WE0 = 3072
WE1 = 4352
ROWS = 2048 + 192
TRASH0 = E0 * CAP

C_ID, C_U, C_ONE, C_IOTA, C_TOK, C_TR, C_CM, C_CA, C_I39 = 0, 128, 256, 384, 448, 464, 560, 624, 688
C_INV = 688 + NT * 8
C_TK1 = C_INV + 128
NCONST = C_TK1 + 16
TILES = [0, 1, 2, 4, 5, 6, 8, 9, 10, 12, 13, 14, 3, 7, 11, 15]


def constants():
    c = np.zeros((128, NCONST), np.float32)
    p = np.arange(128)
    c[:, C_ID:C_ID + 128] = np.eye(128)
    c[:, C_U:C_U + 128] = (p[:, None] < p[None, :])
    c[:, C_ONE:C_ONE + 128] = 1.0
    c[:, C_IOTA:C_IOTA + 64] = np.arange(64)
    c[:, C_TOK:C_TOK + T] = p[:, None] + 128 * np.arange(T)
    c[:, C_TR:C_TR + T * K0] = TRASH0 + p[:, None] + 128 * np.arange(T * K0)
    allowed = np.arange(64)[None, :] <= (p[:, None] - 64)
    c[:, C_CM:C_CM + 64] = allowed * (32.0 ** -0.5)
    c[:, C_CA:C_CA + 64] = np.where(allowed, 0.0, -10000.0)
    c[:, C_I39:C_I39 + NT * 8] = np.repeat(np.arange(NT), 8)
    c[:, C_INV:C_INV + 128] = 1.0 / 64
    c[:, C_TK1:C_TK1 + 16] = p[:, None] + 128 * np.array(TILES)
    l0 = np.zeros((TRASH0, 2), np.float32)
    l0[:, 0] = 2048 + np.arange(TRASH0) % CAP
    l1 = np.zeros(((E1 * 16 + 1) * 128, 2), np.float32)
    l1[:, 0] = 2048 + np.arange(len(l1)) % 128
    return c, l0, l1


class Engine:

    def __init__(self, sem, us, log, chain=False):
        self.sem, self.count, self.todo, self.chain = sem, 0, [], chain
        self.us, self.log, self.until = us, log, 0.0

    def op(self, fn, *waits, sig=True, us=None):
        self.log.append((self, us or self.us))
        if self.chain and self.count:
            waits = (*waits, (self.sem, self.count))
        if sig:
            self.count += 1
        self.todo.append((fn, waits, (self.sem, 1) if sig else None))
        return (self.sem, self.count)

    def play(self, eng):
        seen = {}
        for fn, waits, sig in self.todo:
            for w in waits:
                if w is None:
                    continue
                s, v = w
                if seen.get(s.name, 0) < v:
                    eng.wait_ge(s, v)
                    seen[s.name] = v
            ins = fn(eng)
            if sig:
                ins.then_inc(*sig)


class Landing:

    def __init__(self, sem):
        self.sem, self.count = sem, 0

    def dma(self, q, fn, *waits):
        self.count += 16
        if q.us == 1.05:
            q.log.append((q, q.us))
        q.todo.append((fn, waits, (self.sem, 16)))
        return (self.sem, self.count)


def program(nc, a, out):
    with ExitStack() as ctx:
        def second_name(name, start, end, dt):
            with nc.sbuf_tensor(f"{name}_before", [128, start], F32):
                with nc.sbuf_tensor(name, [128, end - start], dt) as t:
                    return t
        bigr = second_name("bigr", 13056, 34816, F32R)
        rawr = second_name("rawr", 17152, 34816, F32)
        big = ctx.enter_context(nc.sbuf_tensor("big", [128, 53120], F32))
        PB = [ctx.enter_context(nc.psum_tensor(f"pb{i}", [128, 512], F32)) for i in range(8)]

        def sem(name):
            return ctx.enter_context(nc.semaphore(name))

        def land(name):
            return Landing(sem(name))

        log, tk = [], {}
        pe, act, dve, pool, sp = (Engine(sem(n), us, log, n in ("s_act", "s_dve")) for n, us in (("s_pe", 0.6), ("s_act", 0.35), ("s_dve", 0.2), ("s_pool", 1.05), ("s_sp", 0.1)))
        HN = nc.dram_tensor("hn_rows", [ROWS, D], F32, kind="Internal").ap()
        HN2 = nc.dram_tensor("hn2_rows", [ROWS, D], F32, kind="Internal").ap()
        ACC = nc.dram_tensor("acc_rows", [ROWS, D], F32, kind="Internal").ap()
        OUT = out.rearrange("b s d -> (b s) d")
        LIST0 = nc.dram_tensor("list0_rows", [TRASH0 + T * K0 * 128, 2], F32, kind="Internal").ap()
        LIST1 = nc.dram_tensor("list1_rows", [(E1 * 16 + 1) * 128, 2], F32, kind="Internal").ap()

        def R(off, *shape):
            return S(off - 13056, *shape, mem=bigr)

        def RAW(off, *shape):
            return S(off - 17152, *shape, mem=rawr)

        def S(off, *shape, p0=0, p1=128, mem=big):
            n = int(np.prod(shape))
            v = mem[p0:p1, off:off + n]
            if len(shape) == 2:
                v = v.rearrange("p (a b) -> p a b", a=shape[0])
            if len(shape) == 3:
                v = v.rearrange("p (a b c) -> p a b c", a=shape[0], b=shape[1])
            return v

        REST = E1 * WE1
        W1 = S(0, REST)

        def taker(start, end):
            at = [start]

            def take(*shape, p1=128):
                o = at[0]
                at[0] += int(np.prod(shape))
                assert at[0] <= end, (at[0], end)
                return S(o, *shape, p1=p1)
            take.at = at
            return take

        keep = taker(REST, 53120)
        CON = keep(NCONST)
        CTX = keep(4, D)
        TG, GVAL, IDS, WSL = keep(4), keep(4), keep(64), keep(64)
        ident = CON[:, C_ID:C_ID + 128]
        RING = keep.at[0]
        ring = taker(RING, 53120)
        WR = [ring(WE0) for _ in range(4)]
        YS = [ring(D, p1=HALF) for _ in range(4)]
        SW0 = WR[2]
        early = taker(RING + 3 * WE0, RING + 4 * WE0)
        WQ, DT, BQB = early(4, D), early(4, 64), early(4, 128)
        one = taker(0, REST)
        X = one(T, D)
        MSB, NCB, RW0, BIA = one(4, 64), one(4, 64), one(4, E0), one(E0)
        BQ, CB, ITF, CC = one(4), ring(64), one(4, 4), one(4, 5 * E0)
        ITI = one(4, 4).bitcast(I32)
        CH = []
        for b in range(4):
            c = {"XN": [one(D), one(D)], "HT": one(4, 512), "SC": one(4, 64)}
            r = one.at[0]
            one.at[0] += 1536
            c["WTS"], c["WTS2"], c["WT"] = S(r, 4, 64), S(r + 256, 4, 64), S(r + 512, D, p1=64)
            c["TT"] = S(r + 1024, D, p1=64)
            c["OH"], c["TM"] = S(r, 4, K0 * E0), S(r + 768, 4, K0 * E0)
            c["INT"], c["SS"] = S(r, 2, D), S(r + 1024, D)
            for n in ("LG", "EA", "UU", "LN", "BS", "MS"):
                c[n] = one(4, E0)
            c["ST"], c["MV"], c["RS"], c["R2"] = one(4, 6), one(4, 2), one(4), one(4)
            c["MX"], c["MI"] = one(4, 8), one(4, 8).bitcast(U32)
            c["P12"], c["IDF"] = one(4, 2), one(4, 8)
            c["WK"], c["DEN"], c["ADR"], c["VA"] = one(4, K0), one(4, 1), one(4, K0), one(4, K0)
            c["REC"], c["ADI"] = one(4, K0, 2), one(4, K0).bitcast(I32)
            CH.append(c)
        two = taker(0, T * D)
        GF = [one(D, p1=HALF), one(D, p1=HALF)]
        G = [None, None, two(D, p1=HALF), two(D, p1=HALF)]
        XT = [two(4, CAP) for _ in range(2)]
        IN0 = [two(2, CAP) for _ in range(2)]
        SL0 = [two(2, CAP) for _ in range(2)]
        G[0], G[1] = two(D, p1=HALF), two(D, p1=HALF)
        LB = ring(HALF, 2, p1=64)

        block = ctx.enter_context(nc.Block())
        l_con, l_w, l_x = land("l_con"), land("l_w"), [land(f"l_x{i}") for i in range(4)]
        l_init = land("l_init")

        def load(l, q, dst, src, *waits):
            return l.dma(q, lambda e: e.dma_start(dst, src), *waits)


        def merge(busy, gap, hop, *chains):
            live, free = [[t, rank, ch] for t, rank, ch in chains], {}
            log.clear()
            while live:
                now = free.get(busy, 0.0)
                c = min(live, key=lambda c: (max(c[0], now), c[1]))
                more = next(c[2], None)
                t = c[0] + 0.05 if log else max(c[0], now) + 0.5
                for eng, us in log:
                    if eng is pool:
                        free[pool] = max(t, free.get(pool, 0.0)) + 1.05
                        continue
                    t = max(t, free.get(eng, 0.0)) + us
                    free[eng] = t + gap
                    t += hop
                t = max(t, free.get(pool, 0.0) + tk.pop("lands", 0.0) if "lands" in tk else 0.0)
                log.clear()
                c[0] = t
                if more is None:
                    live.remove(c)

        l_it = land("l_it")
        t_gv = load(land("l_gv"), act, GVAL, a["g"])
        t_id = load(land("l_id"), act, CON[:, 0:128], a["con"][:, 0:128])
        load(l_w, act, DT, a["descT"])
        t_bqd = load(land("l_bq"), act, BQ, a["bq"])
        t_con = load(land("l_con0"), act, CON[:, 128:NCONST], a["con"][:, 128:NCONST])
        for b in range(4):
            load(l_x[b], sp, X[:, 4 * b:4 * b + 4, :], a["x"][b].rearrange("(t p) d -> p t d", p=128))
            if b == 0:
                t_w = load(l_w, sp, WQ, a["wq"].rearrange("(k p) d -> p k d", p=128))
        t_it = load(l_it, act, ITI, a["itok"].rearrange("(t p) k -> p t k", p=128))
        load(l_con, act, CTX[0:64], a["ctx"].rearrange("b s d -> s b d"))
        t_ctx = load(l_con, act, CTX[64:128], a["ctx"].rearrange("b s d -> s b d"))
        l_r0 = land("l_r0")
        load(l_r0, act, RW0, a["rw0"])
        t_r0 = load(l_r0, act, BIA, a["bias"])
        t_sw = load(land("l_sw0"), sp, SW0, a["sw0"])
        load(l_init, sp, LIST0[0:TRASH0, :].rearrange("(a b) c -> a (b c)", a=64), a["l0"].rearrange("(a b) c -> a (b c)", a=64))
        load(l_init, sp, LIST1.rearrange("(a b) c -> a (b c)", a=E1 * 16 + 1), a["l1"].rearrange("(a b) c -> a (b c)", a=E1 * 16 + 1))
        for tab in (HN, HN2, ACC):
            t_init = load(l_init, sp, tab[2048:ROWS, :], a["zero"])
        l_wr = [land(f"l_wr{i}") for i in range(4)]
        st = {}
        for e_ in range(2):
            st[e_] = [load(l_wr[e_], sp, WR[e_][:, 0:2048], a["we0"][e_][:, 0:2048])]

        t_tg = act.op(lambda e: e.activation(TG, GVAL, ACT.Tanh), t_gv)
        QS = float(D) ** -0.5
        io4 = CON[:, C_IOTA:C_IOTA + 64].unsqueeze(1).broadcast_to([128, 4, 64])

        def matrix():
            def mrows(e):
                for m in range(4):
                    for k in range(4):
                        i = e.matmul(PB[6][:, m * 64:(m + 1) * 64], WQ[:, k, m * 128:(m + 1) * 128], DT[:, k, :],
                                     start=(k == 0), stop=(k == 3))
                return i
            t_m = pe.op(mrows, t_w)
            t_bq = dve.op(lambda e: e.tensor_copy(BQB, BQ.unsqueeze(2).broadcast_to([128, 4, 128])), t_bqd)

            def cbrow(e):
                for k in range(4):
                    i = e.matmul(PB[7][:, 0:64], BQB[:, k, :], DT[:, k, :], start=(k == 0), stop=(k == 3))
                return i
            t_cb = pe.op(cbrow, t_bq, t_w)
            tk["early"] = t_cb
            yield 1
            tk["msb"] = act.op(lambda e: e.activation(MSB.rearrange("p a b -> p (a b)"), PB[6][:, 0:256], ACT.Copy), t_m)
            t = dve.op(lambda e: e.tensor_copy(ITF, ITI), t_it)
            TM = CH[3]["WTS"]
            yield 1
            for k in range(4):
                dst = NCB if k == 0 else TM
                t = dve.op(lambda e, k=k, dst=dst: e.tensor_tensor(dst, io4, ITF[:, :, k:k + 1].broadcast_to([128, 4, 64]), ALU.is_equal), t, t_con)
                if k:
                    t = dve.op(lambda e: e.tensor_tensor(NCB, NCB, TM, ALU.max), t)
                yield 1
            t = dve.op(lambda e: e.tensor_scalar(NCB, NCB, 1.0, 1e30, ALU.subtract, ALU.mult), t)
            t_cb = dve.op(lambda e: e.tensor_scalar(CB, PB[7][:, 0:64], QS, None, ALU.mult), t_cb)
            tk["ncb"] = dve.op(lambda e: e.tensor_tensor(NCB, NCB, CB.unsqueeze(1).broadcast_to([128, 4, 64]), ALU.add), t, t_cb)
            yield 1

        def table(name):
            if tk.get("table") != name:
                tk["table"] = name
                act.todo.append((lambda e: e.preload_act_table_set(name), (), None))

        LNEXP, SILU = "natural_log_exp_and_others", "silu_and_others"

        def rstd(RS, R2, var, t):
            t = dve.op(lambda e: e.tensor_scalar(R2, var, 1e-5, None, ALU.add), t)
            table(LNEXP)
            t = act.op(lambda e: e.activation(RS, R2, ACT.Ln), t)
            table(LNEXP)
            t = act.op(lambda e: e.activation(RS, RS, ACT.Exp, scale=-0.5), t)
            t = dve.op(lambda e: e.tensor_scalar(R2, R2, -0.5, None, ALU.mult), t)
            yield 1
            t = dve.op(lambda e: e.tensor_tensor(R2, R2, RS, ALU.mult), t)
            t = dve.op(lambda e: e.tensor_tensor(R2, R2, RS, ALU.mult), t)
            return dve.op(lambda e: e.scalar_tensor_tensor(out=RS, in0=R2, scalar=1.5, in1=RS, op0=ALU.add, op1=ALU.mult), t)

        def stats(c, xs, waits, steps=False):
            n = len(xs)
            for i, x in enumerate(xs):
                dve.op(lambda e, i=i, x=x: e.bn_stats(c["ST"][:, i, :], x), *waits, us=0.6)
                t = dve.op(lambda e, i=i: e.bn_aggr(c["MV"][:, i, :], c["ST"][:, i, :]))
                yield 1
            if steps:
                RS, R2, V = c["RS"][:, 0:n], c["R2"][:, 0:n], c["MV"][:, 0:n, 1]
                dve.op(lambda e: e.tensor_scalar(V, V, 1e-5, None, ALU.add))
                dve.op(lambda e: e.tensor_scalar(RS.bitcast(I32), V.bitcast(I32), 1, None, ALU.logical_shift_right))
                dve.op(lambda e: e.tensor_scalar(RS.bitcast(I32), RS.bitcast(I32), -1.0, float(0x5F3759DF), ALU.mult, ALU.add))
                dve.op(lambda e: e.tensor_scalar(V, V, -0.5, None, ALU.mult))
                for _ in range(3):
                    dve.op(lambda e: e.tensor_tensor(R2, RS, RS, ALU.mult))
                    dve.op(lambda e: e.tensor_tensor(R2, R2, V, ALU.mult))
                    t = dve.op(lambda e: e.scalar_tensor_tensor(out=RS, in0=R2, scalar=1.5, in1=RS, op0=ALU.add, op1=ALU.mult))
                yield 1
            else:
                t = yield from rstd(c["RS"][:, 0:n], c["R2"][:, 0:n], c["MV"][:, 0:n, 1], t)
            return dve.op(lambda e: e.scalar_tensor_tensor(out=c["R2"][:, 0:n], in0=c["MV"][:, 0:n, 0], scalar=-1.0, in1=c["RS"][:, 0:n], op0=ALU.mult, op1=ALU.mult), t)

        def norm(c, j, dst, x, *waits):
            return act.op(lambda e: e.activation(dst, x, ACT.Identity, scale=c["RS"][:, j:j + 1], bias=c["R2"][:, j:j + 1]), *waits, us=0.7)

        def flip(src, ps, *waits):
            def f(e):
                for k in range(4):
                    r = e.transpose(ps[:, k * 128:(k + 1) * 128], src[:, k * 128:(k + 1) * 128], ident)
                return r
            return pe.op(f, t_id, *waits)

        def evac(j, dst, ps, *waits):
            src = ps[:, :].rearrange("p (k t) -> p k t", k=4)
            d = dst[:, :, j * 128:(j + 1) * 128]
            return act.op(lambda e: e.activation(d, src, ACT.Copy), *waits, us=0.5)

        def back(dst_ps, w, rows, ht, tmp, p0, free0, free1, *waits):
            def f(e):
                for k in range(4):
                    r = e.matmul(p0[0:rows, :], w[:, k, :], ht[:, k, :], start=(k == 0), stop=(k == 3))
                return r
            t = pe.op(f, free0, *waits, us=3.5)
            t_m = t
            yield 1
            t = act.op(lambda e: e.activation(tmp[0:rows, :], p0[0:rows, :], ACT.Copy), t, us=0.5)
            t_c = t

            def g(e):
                for j in range(4):
                    r = e.transpose(dst_ps[:, j * rows:(j + 1) * rows], tmp[0:rows, j * 128:(j + 1) * 128], ident[0:rows, 0:rows])
                return r
            t = pe.op(g, t, free1)
            yield 1
            return t_m, t_c, t

        l_hn = [[land(f"l_hn{b}{j}") for j in range(2)] for b in range(4)]
        l_acc = [[land(f"l_as{b}{j}") for j in range(2)] for b in range(4)]
        l_sc = land("l_sc0")
        t_cc = [None] * 4
        t_end = [None] * 4
        rows0, accs0, done = [], [], {}

        def chain0(b):
            c = CH[b]
            P = [PB[2 * b], PB[2 * b + 1]]
            xs = [X[:, 4 * b + j, :] for j in range(4)]
            free = [tk["ncb"], tk["ncb"]] if b == 3 else [None, None]
            xf = [[], []]
            t_rs = yield from stats(c, xs, [(l_x[b].sem, 16)])
            for j in range(5):
                if j < 4:
                    t_n = norm(c, j, c["XN"][j % 2], xs[j], t_rs, *xf[j % 2])
                    t_f = flip(c["XN"][j % 2], P[j % 2], t_n, free[j % 2])
                    xf[j % 2] = [t_f]
                    yield 1
                if j:
                    q = (j - 1) % 2
                    free[q] = evac(j - 1, c["HT"], P[q], xf[q][0])
                    yield 1
            t_m, t_c, t = yield from back(P[1], MSB, 64, c["HT"], c["TT"], P[0], free[0], free[1], tk["msb"], *free)
            t_sc = dve.op(lambda e: e.scalar_tensor_tensor(out=c["SC"], in0=P[1][:, 0:256].rearrange("p (a b) -> p a b", a=4), scalar=QS, in1=NCB, op0=ALU.mult, op1=ALU.add), t, tk["ncb"])
            yield 1
            t = t_sc
            for j in range(4):
                dve.op(lambda e, j=j: e.max(c["MX"][:, j, :], c["SC"][:, j, :]), t)
                t3 = dve.op(lambda e, j=j: e.max_index(c["MI"][:, j, :], c["MX"][:, j, :], c["SC"][:, j, :]))
                if j % 2:
                    yield 1
            P12, IDF, WTS, WTS2 = c["P12"], c["IDF"], c["WTS"], c["WTS2"]
            t = dve.op(lambda e: e.tensor_tensor(P12[:, :, 0:1], c["MX"][:, :, 1:2], c["MX"][:, :, 0:1], ALU.subtract), t3)
            table(LNEXP)
            t = act.op(lambda e: e.activation(P12[:, :, 1:2], P12[:, :, 0:1], ACT.Exp), t)
            dve.op(lambda e: e.tensor_copy(IDF, c["MI"]))
            yield 1
            for j, dst in ((0, WTS), (1, WTS2)):
                dve.op(lambda e, j=j, dst=dst: e.tensor_tensor(dst, io4, IDF[:, :, j:j + 1].broadcast_to([128, 4, 64]), ALU.is_equal))
            dve.op(lambda e: e.tensor_scalar(P12[:, :, 0:1], P12[:, :, 1:2], 1.0, None, ALU.add), t)
            dve.op(lambda e: e.reciprocal(P12[:, :, 0:1], P12[:, :, 0:1]))
            dve.op(lambda e: e.tensor_tensor(P12[:, :, 1:2], P12[:, :, 1:2], P12[:, :, 0:1], ALU.mult))
            yield 1
            for j, dst in ((0, WTS), (1, WTS2)):
                dve.op(lambda e, j=j, dst=dst: e.tensor_tensor(dst, dst, P12[:, :, j:j + 1].broadcast_to([128, 4, 64]), ALU.mult))
            t = dve.op(lambda e: e.tensor_tensor(WTS, WTS, WTS2, ALU.add))
            yield 1

            def fw(e):
                for j in range(4):
                    r = e.transpose(P[0][0:64, j * 128:(j + 1) * 128], WTS[:, j, :], ident)
                return r
            t = pe.op(fw, t, t_c)
            t_wt = act.op(lambda e: e.activation(c["WT"], P[0][0:64, :], ACT.Copy), t)
            yield 1
            free = [t_wt, t_sc]
            for j in range(4):
                t = pe.op(lambda e, j=j: e.matmul(P[j % 2][:, :], c["WT"][:, j * 128:(j + 1) * 128], CTX[0:64, b, :], start=True, stop=True),
                          t_wt, free[j % 2], t_ctx, us=0.9)
                yield 1
                free[j % 2] = dve.op(lambda e, j=j: e.scalar_tensor_tensor(out=xs[j], in0=P[j % 2][:, :], scalar=TG[:, 0:1], in1=xs[j], op0=ALU.mult, op1=ALU.add), t, t_tg, us=0.6)
                yield 1
            t_rs = yield from stats(c, xs, [])
            xf = [[], []]
            for j in range(5):
                if j < 4:
                    t_n = norm(c, j, c["XN"][j % 2], xs[j], t_rs, *xf[j % 2])
                    t_f = flip(c["XN"][j % 2], P[j % 2], t_n, free[j % 2])
                    i = 4 * b + j
                    t_d = load(l_hn[b][j % 2], sp, HN[i * 128:(i + 1) * 128, :], c["XN"][j % 2], t_n)
                    rows0.append(t_d)
                    xf[j % 2] = [t_f, t_d]
                    yield 1
                if j:
                    q = (j - 1) % 2
                    free[q] = evac(j - 1, c["HT"], P[q], xf[q][0])
                    yield 1
            t_ht = free[1]
            t_xn = xf
            t_m, t_c, t = yield from back(P[1], RW0, E0, c["HT"], c["TT"], P[0], free[0], free[1], t_r0, *free)
            lg = P[1][:, 0:4 * E0].rearrange("p (a b) -> p a b", a=4)
            LG, EA, UU, LN_, BS, MS = (c[n] for n in ("LG", "EA", "UU", "LN", "BS", "MS"))
            tl = t
            act.op(lambda e: e.activation(EA, lg, ACT.Abs), tl)
            table(LNEXP)
            t = act.op(lambda e: e.activation(EA, EA, ACT.Exp, scale=-1.0))
            t_lg = t
            yield 1
            t = dve.op(lambda e: e.tensor_scalar(UU, EA, 1.0, None, ALU.add), t)
            table(LNEXP)
            t = act.op(lambda e: e.activation(LN_, UU, ACT.Ln), t)
            t_q = dve.op(lambda e: e.tensor_scalar(LG, lg, 0.0, None, ALU.max), tl)
            yield 1
            dve.op(lambda e: e.scalar_tensor_tensor(out=UU, in0=UU, scalar=-1.0, in1=EA, op0=ALU.add, op1=ALU.subtract), t)
            dve.op(lambda e: e.tensor_tensor(LG, LG, UU, ALU.subtract))
            t = dve.op(lambda e: e.tensor_tensor(LG, LG, LN_, ALU.add))
            yield 1
            t = dve.op(lambda e: e.tensor_scalar(UU, LG, 1e-37, None, ALU.max))
            table(LNEXP)
            act.op(lambda e: e.activation(LN_, UU, ACT.Ln), t)
            table(LNEXP)
            t = act.op(lambda e: e.activation(LN_, LN_, ACT.Exp, scale=0.5))
            yield 1
            dve.op(lambda e: e.reciprocal(EA, LN_), t)
            dve.op(lambda e: e.tensor_tensor(EA, EA, LG, ALU.mult))
            dve.op(lambda e: e.tensor_tensor(EA, EA, LN_, ALU.add))
            dve.op(lambda e: e.tensor_scalar(LG, EA, 0.5, None, ALU.mult))
            t = dve.op(lambda e: e.tensor_tensor(BS, LG, BIA.unsqueeze(1).broadcast_to([128, 4, E0]), ALU.add))
            yield 1
            t_read, t_adr = yield from route(c, b, E0, K0, BS, LG, TG[:, 2:3], 1.5, [t_c, t_q, t_lg], P, CC, t_cc, 0)
            done[b] = (t_read, t_adr, t_ht, t_xn)
            yield 1

        def shared0(b):
            c = CH[b]
            P = [PB[2 * b], PB[2 * b + 1]]
            xs = [X[:, 4 * b + j, :] for j in range(4)]
            t_route, t_ss, t_ht, t_xn = done[b]
            free = [t_route, t_route]
            for m in range(2):
                for q in range(2):
                    def f(e, m=m, q=q):
                        base = 1024 * q
                        for k in range(4):
                            r = e.matmul(P[q][:, :], SW0[:, base + k * 256 + m * 128:base + k * 256 + (m + 1) * 128], c["HT"][:, k, :], start=(k == 0), stop=(k == 3))
                        return r
                    t = pe.op(f, t_sw, t_ht, free[q], us=3.5)
                    if q == 0:
                        table(SILU)
                        ts = act.op(lambda e: e.activation(c["SS"], P[0][:, :], ACT.Silu), t, t_ss, us=0.6)
                        free[0] = ts
                    yield 1
                free[1] = dve.op(lambda e, m=m: e.tensor_tensor(c["INT"][:, m, :], c["SS"], P[1][:, :], ALU.mult), t, ts, us=0.6)
                t_ss = free[1]
                t_i = dve.op(lambda e, m=m: e.tensor_scalar(c["INT"][:, m, :], c["INT"][:, m, :], 10.0, -10.0, ALU.min, ALU.max), us=0.4)
                yield 1
            xf = t_xn
            for j in range(4):
                def f(e, j=j):
                    for k in range(2):
                        r = e.matmul(P[j % 2][:, :], c["INT"][:, k, j * 128:(j + 1) * 128], SW0[:, 2048 + k * 512:2560 + k * 512], start=(k == 0), stop=(k == 1))
                    return r
                t = pe.op(f, t_i, free[j % 2], us=1.8)
                yield 1
                i = 4 * b + j
                free[j % 2] = dve.op(lambda e, j=j: e.scalar_tensor_tensor(out=c["XN"][j % 2], in0=P[j % 2][:, :], scalar=TG[:, 2:3], in1=xs[j], op0=ALU.mult, op1=ALU.add), t, *xf[j % 2], us=0.6)
                t_d = load(l_acc[b][j % 2], sp, ACC[i * 128:(i + 1) * 128, :], c["XN"][j % 2], free[j % 2])
                accs0.append(t_d)
                xf[j % 2] = [t_d]
            t_end[b] = (t, free[1])
            yield 1

        def route(c, b, ne, kk, sel, val, wscale, factor, t_sel, P, CCx, t_ccx, layer):
            big_ = 0.9 if layer == 0 else 0.2
            n, tok = 4 * ne, C_TOK if layer == 0 else C_TK1
            OHv = c["OH"].rearrange("p t (k e) -> p t k e", k=kk)
            TMv = c["TM"].rearrange("p t (k e) -> p t k e", k=kk)
            IDX, WK, DEN, ADR, VA, REC, ADI, MS = (c[x] for x in ("IDF", "WK", "DEN", "ADR", "VA", "REC", "ADI", "MS"))
            for j in range(4):
                dve.op(lambda e, j=j: e.max(c["MX"][:, j, :], sel[:, j, :]), *t_sel)
                dve.op(lambda e, j=j: e.max_index(c["MI"][:, j, :], c["MX"][:, j, :], sel[:, j, :]))
                if j % 2:
                    yield 1
            dve.op(lambda e: e.tensor_copy(IDX, c["MI"]))
            sh = [128, 4, kk, ne]
            iob = CON[:, C_IOTA:C_IOTA + ne].unsqueeze(1).unsqueeze(1).broadcast_to(sh)
            dve.op(lambda e: e.tensor_tensor(OHv, iob, IDX[:, :, 0:kk].unsqueeze(3).broadcast_to(sh), ALU.is_equal), t_con, us=big_)
            t = dve.op(lambda e: e.tensor_reduce(MS, OHv.rearrange("p t k e -> p t e k"), AX.X, ALU.add), us=big_)

            def cnt(e):
                e.matmul(P[0][:, 0:n], CON[:, C_U:C_U + 128], MS.rearrange("p t e -> p (t e)"), start=True, stop=True)
                return e.matmul(P[1][:, 0:n], CON[:, C_ONE:C_ONE + 128], MS.rearrange("p t e -> p (t e)"), start=True, stop=True)
            t_cnt = pe.op(cnt, t, *t_sel)
            yield 1
            dve.op(lambda e: e.tensor_tensor(TMv, OHv, val.unsqueeze(2).broadcast_to(sh), ALU.mult), us=big_)
            dve.op(lambda e: e.tensor_reduce(WK, TMv, AX.X, ALU.add), us=big_)
            dve.op(lambda e: e.tensor_reduce(DEN, WK, AX.X, ALU.add))
            yield 1
            dve.op(lambda e: e.reciprocal(DEN, DEN))
            dve.op(lambda e: e.tensor_scalar(DEN, DEN, wscale, factor, ALU.mult, ALU.mult), t_tg)
            dve.op(lambda e: e.tensor_tensor(REC[:, :, :, 1], WK, DEN.broadcast_to([128, 4, kk]), ALU.mult))
            t_rec = dve.op(lambda e: e.tensor_copy(REC[:, :, :, 0], CON[:, tok + 4 * b:tok + 4 * b + 4].unsqueeze(2).broadcast_to([128, 4, kk])))
            yield 1
            cc = CCx[:, b, :].rearrange("p (t e) -> p t e", e=ne)
            if b == 0:
                dve.op(lambda e: e.memset(cc[:, 0, :], 0.0))
            else:
                pv = CCx[:, b - 1, :].rearrange("p (t e) -> p t e", e=ne)
                dve.op(lambda e: e.tensor_copy(cc[:, 0, :], pv[:, 4, :]), t_ccx[b - 1])
            for j in range(4):
                t_ccx[b] = dve.op(lambda e, j=j: e.tensor_tensor(cc[:, j + 1, :], cc[:, j, :], P[1][:, j * ne:(j + 1) * ne], ALU.add), t_cnt)
            yield 1
            t_read = dve.op(lambda e: e.tensor_tensor(MS, cc[:, 0:4, :], P[0][:, 0:n].rearrange("p (t e) -> p t e", e=ne), ALU.add))
            dve.op(lambda e: e.tensor_tensor(TMv, OHv, MS.unsqueeze(2).broadcast_to(sh), ALU.mult), us=big_)
            t = dve.op(lambda e: e.tensor_reduce(ADR, TMv, AX.X, ALU.add), us=big_)
            yield 1
            if layer == 0:
                tr = CON[:, C_TR + 4 * K0 * b:C_TR + 4 * K0 * (b + 1)].rearrange("p (t k) -> p t k", k=kk)
                dve.op(lambda e: e.tensor_scalar(VA, ADR, float(CAP), None, ALU.is_lt))
                dve.op(lambda e: e.scalar_tensor_tensor(out=ADR, in0=IDX[:, :, 0:kk], scalar=float(CAP), in1=ADR, op0=ALU.mult, op1=ALU.add))
                dve.op(lambda e: e.tensor_tensor(ADR, ADR, tr, ALU.subtract))
                dve.op(lambda e: e.tensor_tensor(ADR, ADR, VA, ALU.mult))
                dve.op(lambda e: e.tensor_tensor(ADR, ADR, tr, ALU.add))
            else:
                dve.op(lambda e: e.scalar_tensor_tensor(out=ADR, in0=IDX[:, :, 0:kk], scalar=2048.0, in1=ADR, op0=ALU.mult, op1=ALU.add))
            t = dve.op(lambda e: e.tensor_copy(ADI, ADR))
            t_adr = t
            lists = LIST0 if layer == 0 else LIST1
            for j in range(4):
                for k in range(kk):
                    tk[f"list{layer}"] = (l_sc if layer == 0 else l_sc1).dma(pool, lambda e, j=j, k=k: e.indirect_dma_start(
                        lists, bass.IndirectOffsetOnAxis(ap=ADI[:, j, k:k + 1], axis=0), REC[:, j, k, :], None), t, t_rec, t_init)
            yield 1
            return t_read, t_adr

        def three(e, dst, ops):
            for n, (wh, wl, xh, xl) in enumerate(ops):
                e.matmul(dst, wh, xl, start=(n == 0), stop=False)
                e.matmul(dst, wl, xh, start=False, stop=False)
                r = e.matmul(dst, wh, xh, start=False, stop=(n == len(ops) - 1))
            return r

        l_lb = land("l_lb")
        l_g = [land(f"l_g{i}") for i in range(4)]
        IDI = IDS.bitcast(I32)
        MN = [S(MN0 + 512 * i, D) for i in range(4)]

        def fetch(e_):
            tg_ = []
            for h in range(2):
                s = (2 * e_ + h) % 4
                tg_.append(l_g[s].dma(pool, lambda e, s=s, h=h: e.indirect_dma_start(
                    (G if e_ else GF)[s], None, HN, bass.IndirectOffsetOnAxis(ap=IDI[0:HALF, 2 * e_ + h:2 * e_ + h + 1], axis=0)),
                    tk["ids"], g_free[s], tk.get("shd"), *rows0, t_init))
            st[e_].append(tg_)

        def turn(e_):
            t_wr, tg_ = st[e_]
            tc = []
            for h in range(2):
                s = (2 * e_ + h) % 4

                def f(e, s=s, h=h):
                    for k in range(4):
                        r = e.transpose(PB[h][:, k * HALF:(k + 1) * HALF], (G if e_ else GF)[s][:, k * 128:(k + 1) * 128], ident[0:HALF, 0:HALF])
                    return r
                t = pe.op(f, tg_[h], pxt[h])
                g_free[s] = t
                src = PB[h][:, 0:4 * HALF].rearrange("p (k t) -> p k t", k=4)
                dst = XT[e_ % 2][:, :, h * HALF:(h + 1) * HALF]
                if h == 0:
                    t = act.op(lambda e, src=src, dst=dst: e.activation(dst, src, ACT.Copy), t, xt_free[e_ % 2])
                else:
                    t = dve.op(lambda e, src=src, dst=dst: e.tensor_copy(dst, src), t, xt_free[e_ % 2])
                pxt[h] = t
                tc.append(t)
            st[e_].append(tc)

        def shareds():
            for b in range(4):
                while b not in done:
                    yield 1
                yield from shared0(b)

        g_free, pxt, xt_free = [None] * 4, [None, None], [None, None]

        def means():
            while t_end[1] is None:
                yield 1
            t = t_end[1][1]
            for i in range(4):
                t = pe.op(lambda e, i=i: e.matmul(PB[1][:, :], CON[0:64, C_INV:C_INV + 128], CTX[0:64, i, :], start=True, stop=True), t_ctx, t)
                yield 1
                t = dve.op(lambda e, i=i: e.tensor_scalar(MN[i], PB[1][:, :], TG[:, 1:2], None, ALU.mult), t, *accs0)
                yield 1
            tk["means"] = t

        def entry():
            while len(done) < 4:
                yield 1
            t_lb = l_lb.dma(pool, lambda e: e.dma_start(
                LB.rearrange("p a b -> p (a b)"), LIST0[0:TRASH0, :].rearrange("(a b) c -> a (b c)", a=64)), tk["list0"], t_init)
            tk["lands"] = 4.0
            yield 1
            while "means" not in tk:
                yield 1
            t = tk["means"]

            def fl(e):
                e.transpose(PB[0][0:HALF, 0:64], LB[:, :, 0], ident[0:64, 0:64])
                return e.transpose(PB[0][0:HALF, 64:128], LB[:, :, 1], ident[0:64, 0:64])
            t_fl = pe.op(fl, t_lb, t)
            yield 1
            tk["ids"] = dve.op(lambda e: e.tensor_copy(IDI[0:HALF, :], PB[0][0:HALF, 0:64]), t_fl)
            tk["wsl"] = dve.op(lambda e: e.tensor_copy(WSL[0:HALF, :], PB[0][0:HALF, 64:128]), t_fl)
            pxt[0] = pxt[1] = tk["wsl"]
            xt_free[0] = xt_free[1] = g_free[2] = g_free[3] = t_end[1][1]
            fetch(0)
            fetch(1)
            yield 1
            turn(0)
            yield 1

        merge(None, GAP0, HOP0, (MATRIX_START, -1, matrix()), *[(5 + CHUNK_START * b, 0, chain0(b)) for b in range(4)], (0, SHARED0_RANK, shareds()), (0, ENTRY_RANK, entry()), (0, ENTRY_RANK, means()))
        t_sh0 = (pe.sem, pe.count)
        t_shd = (dve.sem, dve.count)
        t_acc_rows, t_rows0 = accs0, rows0
        tk["shd"] = t_shd
        t_ids, t_wsl = tk["ids"], tk["wsl"]

        l_add = [land("l_add0"), land("l_add1")]
        wr_free = [None, None, t_sh0, tk["early"]]
        ys_free = [t_shd] * 4
        in_free = [t_shd, t_shd]
        t_add = [None, None]
        pgu, pyy = [t_shd] * 2, [t_shd, t_shd]

        def fetch_w(e_):
            st[e_] = [load(l_wr[e_ % 4], sp, WR[e_ % 4][:, 0:2048], a["we0"][e_][:, 0:2048], wr_free[e_ % 4])]

        WDH, WDL = [R(13056, 1024), R(14080, 1024)], [R(15104, 1024), R(16128, 1024)]
        INH, INL = [R(17152, 2 * CAP), R(17536, 2 * CAP)], [R(17920, 2 * CAP), R(18304, 2 * CAP)]
        RD = [RAW(18688 + 1024 * i, 1024) for i in range(3)]
        SLR, INR = [RAW(21760, 2 * CAP), RAW(22144, 2 * CAP)], [RAW(22528, 2 * CAP), RAW(22912, 2 * CAP)]
        l_rd = [land(f"l_rd{i}") for i in range(3)]
        rd_free, wd_free, rd, wd, ins = [None] * 3, [None] * 2, {}, {}, {}

        def fetch_d(e_):
            rd[e_] = load(l_rd[e_ % 3], sp, RD[e_ % 3], a["we0"][e_][:, 2048:3072], t_sh0, t_shd, rd_free[e_ % 3], *t_acc_rows)

        def split_d(e_):
            q = e_ % 2
            t = act.op(lambda e: e.activation(WDH[q], RD[e_ % 3], ACT.Copy), rd[e_], wd_free[q])
            wd[e_] = rd_free[e_ % 3] = dve.op(lambda e: e.tensor_tensor(WDL[q], RD[e_ % 3], WDH[q].bitcast(F32), ALU.subtract), t)

        def split_i(e_):
            q = e_ % 2
            t = act.op(lambda e: e.activation(INH[q], INR[q], ACT.Copy), st[e_][3], in_free[q])
            ins[e_] = dve.op(lambda e: e.tensor_tensor(INL[q], INR[q], INH[q].bitcast(F32), ALU.subtract), t)

        def up(e_):
            t_wr, tg_, tc = st[e_]
            pg, pu = PB[2 + 2 * (e_ % 2)], PB[3 + 2 * (e_ % 2)]

            def f(e):
                for ps, base in ((pg, 0), (pu, 1024)):
                    for m in range(2):
                        for k in range(4):
                            r = e.matmul(ps[:, m * CAP:(m + 1) * CAP], WR[e_ % 4][:, base + k * 256 + m * 128:base + k * 256 + (m + 1) * 128], XT[e_ % 2][:, k, :], start=(k == 0), stop=(k == 3))
                return r
            t = pe.op(f, t_wr, *tc, pgu[e_ % 2])
            xt_free[e_ % 2] = t
            wr_free[e_ % 4] = t
            sl, inn = SLR[e_ % 2], INR[e_ % 2]
            table(SILU)
            ts = act.op(lambda e: e.activation(sl, pg[:, 0:2 * CAP], ACT.Silu), t, pgu[e_ % 2])
            td = dve.op(lambda e: e.tensor_tensor(inn, sl, pu[:, 0:2 * CAP], ALU.mult), ts)
            pgu[e_ % 2] = td
            st[e_].append(td)

        def down(e_):
            nonlocal t_add
            new = [None, None]
            for h in range(2):
                s = (2 * e_ + h) % 4

                def f(e, h=h):
                    q = e_ % 2
                    tok = [slice(k * CAP + h * HALF, k * CAP + (h + 1) * HALF) for k in range(2)]
                    return three(e, PB[6 + h][0:HALF, :], [(INH[q][:, tok[k]], INL[q][:, tok[k]], WDH[q][:, k * 512:(k + 1) * 512], WDL[q][:, k * 512:(k + 1) * 512]) for k in range(2)])
                t = pe.op(f, ins[e_], wd[e_], pyy[h])
                wsc = WSL[0:HALF, 2 * e_ + h:2 * e_ + h + 1]
                if h == 0:
                    ty = act.op(lambda e, s=s, wsc=wsc: e.activation(YS[s], PB[6][0:HALF, :], ACT.Copy, scale=wsc), t, ys_free[s], t_wsl)
                else:
                    ty = dve.op(lambda e, s=s, wsc=wsc: e.tensor_scalar(YS[s], PB[7][0:HALF, :], wsc, None, ALU.mult), t, ys_free[s], t_wsl)
                pyy[h] = ty
                new[h] = l_add[h].dma(pool, lambda e, s=s, h=h: e.indirect_dma_start(
                    ACC, bass.IndirectOffsetOnAxis(ap=IDI[0:HALF, 2 * e_ + h:2 * e_ + h + 1], axis=0), YS[s], None, compute_op=ALU.add),
                    ty, *t_add, t_ids, *t_acc_rows, t_init)
                ys_free[s] = new[h]
            t_add = new
            wd_free[e_ % 2] = t
            in_free[e_ % 2] = t

        SRAW, SHI, SLO = RAW(29184, 4, 2 * SI), R(23552, 4, 2 * SI), R(29184, 4, 2 * SI)
        l_sgu, l_w1 = land("l_sgu"), land("l_w1")

        def w1_part(e0, e1, *waits, q=act):
            return load(l_w1, q, S(e0 * WE1, e1 - e0, WE1), a["we1"][e0:e1].rearrange("e p n -> p e n"), *waits)

        def w1_columns(ex, c0, c1, *waits):
            return load(l_w1, act, S(ex * WE1 + c0, c1 - c0), a["we1"][ex][:, c0:c1], *waits)

        fetch_d(0)
        fetch_d(1)
        fetch_w(2)
        fetch_d(2)
        fetch_w(3)
        split_d(0)
        for e_ in range(E0):
            up(e_)
            if e_ == 8:
                t_raw = load(l_sgu, act, SRAW, a["sgu1"].rearrange("(k p) n -> p k n", p=128), t_sh0, t_shd, *t_acc_rows)
            if 14 <= e_ < 22:
                k, h = (e_ - 14) // 2, slice((e_ % 2) * SI, (e_ % 2) * SI + SI)
                t = act.op(lambda e, k=k, h=h: e.activation(SHI[:, k, h], SRAW[:, k, h], ACT.Copy), t_raw, t_sh0, t_shd)
                t_sgu = dve.op(lambda e, k=k, h=h: e.tensor_tensor(SLO[:, k, h], SRAW[:, k, h], SHI[:, k, h].bitcast(F32), ALU.subtract), t)
            if e_ + 1 < E0:
                turn(e_ + 1)
            if e_ + 2 < E0:
                fetch(e_ + 2)
            split_i(e_)
            if e_:
                down(e_ - 1)
            if e_ + 1 < E0:
                split_d(e_ + 1)
            if e_ + 3 < E0:
                fetch_d(e_ + 3)
            if e_ + 4 < E0:
                fetch_w(e_ + 4)
        down(E0 - 1)
        t_end0 = (pe.sem, pe.count)
        t_end0d = (dve.sem, dve.count)
        t_end0a = (act.sem, act.count)

        htr = [(R(o, 4, 512), R(o + 2048, 4, 512)) for o in (13056, 19456)]
        BD, BDV = S(4352, 4, 4 * 64), S(5376, 8, 64)
        PP, PTt, HC = S(5888, 16, 64), S(6912, 8, 128), S(7936, 4, 128)
        XC = [S(2048, D), S(2560, D)]
        TT1 = S(3072, D, p1=8)
        late = taker(RING, 53120)
        xr = [S(8704, 4, D), S(17408, 4, D), S(8704, 4, D), late(4, D)]
        SWD = late(6, D)
        SS1 = [late(D) for _ in range(2)]
        AC1 = [late(D) for _ in range(2)]
        SB1, CC1 = late(12), late(4, 5 * E1)
        LB1 = late(256, p1=NT)
        SMX, SSM, PRM, PRS = late(16), late(16), late(4), late(4)
        c1 = []
        for b in range(2):
            c = {"OH": late(4, 2 * E1), "TM": late(4, 2 * E1), "PR": late(4, E1), "MS": late(4, E1)}
            c["ST"], c["MV"], c["RS"], c["R2"] = late(4, 6), late(4, 2), late(4), late(4)
            c["MX"], c["MI"], c["IDF"] = late(4, 8), late(4, 8).bitcast(U32), late(4, 8)
            c["WK"], c["DEN"], c["ADR"], c["VA"] = late(4, K1), late(4, 1), late(4, K1), late(4, K1)
            c1.append(c)
        ca = {"ST": late(4, 6), "MV": late(4, 2), "RS": late(4), "R2": late(4)}
        recs = [(late(4, K1, 2), late(4, K1).bitcast(I32)) for _ in range(4)]
        NB, NC, NTL = late(8), late(8), late(8)
        NI = late(8).bitcast(I32)
        CMP, ETF, ETK, BLF = late(NT, 8), late(NT), late(NT).bitcast(I32), late(NT)
        BLI = late(1).bitcast(I32)
        G1 = [late(512) for _ in range(2)]
        XT1 = [late(4, 128) for _ in range(2)]
        inter = S(late.at[0], 6, D)
        SL1 = [late(I1) for _ in range(2)]
        IN1 = [late(I1) for _ in range(2)]
        NT1 = [late(3, 128) for _ in range(2)]
        YS1 = [late(512) for _ in range(3)]
        l_xb = [land(f"l_xb{i}") for i in range(4)]
        l_sc1 = land("l_sc1")
        mask_m = CON[:, C_CM:C_CM + 64].unsqueeze(1).broadcast_to([128, 8, 64])
        mask_a = CON[:, C_CA:C_CA + 64].unsqueeze(1).broadcast_to([128, 8, 64])
        Q = [PB[6], PB[7]]
        t_xload = {}

        def load_x(b, *waits):
            for j in range(4):
                i = TILES[4 * b + j]
                t_xload[b] = load(l_xb[b], sp, xr[b][:, j, :], ACC[i * 128:(i + 1) * 128, :], *waits)

        end0 = [t_end0, t_end0d, t_end0a, *t_add]
        load_x(0, *end0)
        l_s1 = land("l_s1")
        RW1, RWH, RWL = RAW(17152, 4, E1), R(17184, 4, E1), R(17216, 4, E1)
        load(l_s1, sp, RW1, a["rw1"])
        t_s1 = load(l_s1, sp, SB1, a["sb1"])
        t_rh = act.op(lambda e: e.activation(RWH, RW1, ACT.Copy), t_s1)
        load_x(1)
        load_x(3)
        t_swd = load(land("l_swd"), sp, SWD, a["sd1"].rearrange("(k p) n -> p k n", p=128))
        ht_free = [None, None]
        z1 = dve.op(lambda e: e.memset(BD, 0.0), *end0)
        z2 = dve.op(lambda e: e.memset(BDV, 0.0))
        t_one = dve.op(lambda e: e.memset(inter[0:64, 5, :], 1.0))
        t_rl = dve.op(lambda e: e.tensor_tensor(RWL, RW1, RWH.bitcast(F32), ALU.subtract), t_rh)
        l_h2 = [land("l_h20"), land("l_h21")]
        rows1, accs1 = [], []
        xc_free = [[], []]
        q_free = [t_end0a, t_end0d]
        qa_free = [t_end0d, t_end0d]
        t_cc1 = [None] * 4
        tl = {}

        def attend(b):
            x, c, Q, q_free = xr[3][:, b, :], ca, [PB[4], PB[5]], qa_free

            def fc(e):
                for k in range(4):
                    r = e.transpose(Q[0][:, k * 64:(k + 1) * 64], CTX[0:64, b, k * 128:(k + 1) * 128], ident[0:64, 0:64])
                return r
            t = pe.op(fc, q_free[0])
            for q in range(2):
                src = CTX[64 * q:64 * q + 64, b, :].rearrange("p (a c d) -> p a c d", c=2, d=32)[:, :, q, :]
                t_bdv = dve.op(lambda e, q=q, src=src: e.tensor_copy(BDV[64 * q:64 * q + 64, :, 32 * q:32 * q + 32], src), tl.get("o"))
            yield 1
            for r in range(4):
                src = Q[0][32 * r:32 * r + 32, 0:256].rearrange("p (k s) -> p k s", k=4)
                dst = BD[32 * r:32 * r + 32, :, 64 * r:64 * r + 64]
                t_bd = act.op(lambda e, src=src, dst=dst: e.activation(dst, src, ACT.Copy), t, z1, tl.get("s"))
            q_free[0] = t_bd
            yield 1
            t_rs = tk["rs3"]
            XA = PP[:, 0:8, :].rearrange("p a b -> p (a b)")
            t_n = norm(c, b, XA, x, t_rs, tl.get("pp"), tl.get("sum"))
            t_f = flip(XA, Q[0], t_n, q_free[0])
            yield 1
            t_h = act.op(lambda e: e.activation(HC.rearrange("p a b -> p (a b)"), Q[0][:, :], ACT.Copy), t_f, tl.get("o2"), us=0.5)
            yield 1

            def fs(e):
                for k in range(4):
                    r = e.matmul(Q[k // 2][:, (k % 2) * 256:(k % 2 + 1) * 256], HC[:, k, :], BD[:, k, :], start=True, stop=True)
                return r
            t = pe.op(fs, t_h, t_bd, q_free[1], us=1.8)
            tl["s"] = t
            yield 1
            for q in range(2):
                src = Q[q][:, :].rearrange("p (g s) -> p g s", s=64)
                dve.op(lambda e, q=q, src=src: e.tensor_tensor(PP[:, 8 * q:8 * q + 8, :], src, mask_m, ALU.mult), t, us=0.65)
                t2 = dve.op(lambda e, q=q: e.tensor_tensor(PP[:, 8 * q:8 * q + 8, :], PP[:, 8 * q:8 * q + 8, :], mask_a, ALU.add), us=0.65)
                yield 1
            dve.op(lambda e: e.tensor_reduce(SMX, PP, AX.X, ALU.max), us=1.15)
            t = dve.op(lambda e: e.tensor_tensor(PP, PP, SMX.unsqueeze(2).broadcast_to([128, 16, 64]), ALU.subtract), us=1.15)
            table(LNEXP)
            t = act.op(lambda e: e.activation(PP.rearrange("p a b -> p (a b)"), PP.rearrange("p a b -> p (a b)"), ACT.Exp), t, us=0.95)
            yield 1

            def fp(e):
                for j in range(8):
                    r = e.transpose(Q[j // 4][:, (j % 4) * 128:(j % 4 + 1) * 128], PP[:, 2 * j:2 * j + 2, :].rearrange("p a b -> p (a b)"), ident)
                return r
            t_p = t
            t = pe.op(fp, t, us=1.0)
            dve.op(lambda e: e.tensor_reduce(SSM, PP, AX.X, ALU.add), t_p, us=1.15)
            tl["sum"] = dve.op(lambda e: e.reciprocal(SSM, SSM))
            tl["pp"] = t
            yield 1
            for j in range(2):
                t_pt = act.op(lambda e, j=j: e.activation(PTt[:, 4 * j:4 * j + 4, :].rearrange("p a b -> p (a b)"), Q[j][:, :], ACT.Copy), t, tl.get("o"), us=0.5)
            yield 1

            def fo(e):
                for j in range(8):
                    r = e.matmul(Q[0][:, j * 64:(j + 1) * 64], PTt[:, j, :], BDV[:, j, :], start=True, stop=True)
                return r
            t = pe.op(fo, t_pt, z2, t_bdv, us=3.5)
            tl["o"] = t
            yield 1
            o = HC.rearrange("p a (b d) -> p (a b) d", d=32)
            q_free[0] = dve.op(lambda e: e.scalar_tensor_tensor(out=o, in0=Q[0][:, :].rearrange("p (h d) -> p h d", d=32), scalar=TG[:, 1:2], in1=SSM.unsqueeze(2).broadcast_to([128, 16, 32]), op0=ALU.mult, op1=ALU.mult), t, us=0.7)
            tl["o2"] = dve.op(lambda e: e.tensor_tensor(x, x, HC.rearrange("p a b -> p (a b)"), ALU.add), us=0.6)
            q_free[1] = t_pt
            tl["att"] = b
            yield 1

        def pre1(b):
            while b not in t_xload or (b >= 2 and ("up", b - 2) not in tl) or (b == 3 and tl.get("att") != 3):
                yield 1
            c = c1[b % 2]
            ids = TILES[4 * b:4 * b + 4]
            xs = [xr[b][:, j, :] for j in range(4)]
            if b < 3:
                for j in range(4):
                    dve.op(lambda e, j=j: e.tensor_tensor(xs[j], xs[j], MN[ids[j] // 4], ALU.add), t_xload[b], us=0.6)
                    if j % 2:
                        yield 1
            t_rs = yield from stats(c, xs, [], True)
            for j in range(5):
                if j < 4:
                    t_n = norm(c, j, XC[j % 2], xs[j], t_rs, *xc_free[j % 2])
                    t_f = flip(XC[j % 2], Q[j % 2], t_n, q_free[j % 2])
                    i = ids[j]
                    t_d = load(l_h2[j % 2], sp, HN2[i * 128:(i + 1) * 128, :], XC[j % 2], t_n)
                    rows1.append(t_d)
                    xc_free[j % 2] = [t_f, t_d]
                    yield 1
                if j:
                    q, t_f = (j - 1) % 2, xc_free[(j - 1) % 2][0]
                    hi, lo = (h[:, :, (j - 1) * 128:j * 128] for h in htr[b % 2])
                    src = Q[q][:, :].rearrange("p (k t) -> p k t", k=4)
                    t_e = act.op(lambda e, hi=hi, src=src: e.activation(hi, src, ACT.Copy), t_f, ht_free[b % 2], us=0.5)
                    q_free[q] = dve.op(lambda e, hi=hi, lo=lo, src=src: e.tensor_tensor(lo, src, hi.bitcast(F32), ALU.subtract), t_e, t_f, ht_free[b % 2], us=0.6)
                    yield 1
            tl[("ht", b)] = q_free[1]

            def fr(e):
                return three(e, Q[0][0:E1, :], [(RWH[:, k, :], RWL[:, k, :], htr[b % 2][0][:, k, :], htr[b % 2][1][:, k, :]) for k in range(4)])
            t = pe.op(fr, t_rl, *q_free, us=2.7)
            yield 1
            t_c = act.op(lambda e: e.activation(TT1, Q[0][0:E1, :], ACT.Copy), t, us=0.5)

            def fb(e):
                for j in range(4):
                    r = e.transpose(Q[1][:, j * E1:(j + 1) * E1], TT1[:, j * 128:(j + 1) * 128], ident[0:E1, 0:E1])
                return r
            t = pe.op(fb, t_c)
            yield 1
            PR = c["PR"]
            lgv = Q[1][:, 0:4 * E1].rearrange("p (t e) -> p t e", e=E1)
            dve.op(lambda e: e.tensor_reduce(PRM, lgv, AX.X, ALU.max), t)
            t = dve.op(lambda e: e.tensor_tensor(PR, lgv, PRM.unsqueeze(2).broadcast_to([128, 4, E1]), ALU.subtract))
            t_q = t
            table(LNEXP)
            t = act.op(lambda e: e.activation(PR, PR, ACT.Exp), t)
            yield 1
            dve.op(lambda e: e.tensor_reduce(PRS, PR, AX.X, ALU.add), t)
            dve.op(lambda e: e.reciprocal(PRS, PRS))
            dve.op(lambda e: e.tensor_tensor(PR, PR, PRS.unsqueeze(2).broadcast_to([128, 4, E1]), ALU.mult))
            yield 1
            cr = dict(c)
            cr["REC"], cr["ADI"] = recs[b]
            t_read, t_adr = yield from route(cr, b, E1, K1, PR, PR, TG[:, 3:4], 1.0, [t_c, t_q], Q, CC1, t_cc1, 1)
            q_free[0] = q_free[1] = t_read
            tl["routed"] = b
            yield 1

        def slots():
            while tl.get("routed") != 3:
                yield 1
            cur = CC1[:, 3, :].rearrange("p (t e) -> p t e", e=E1)[:, 4, :]
            dve.op(lambda e: e.tensor_scalar(NB, cur, 127.0, None, ALU.add))
            dve.op(lambda e: e.tensor_copy(NI, NB))
            dve.op(lambda e: e.tensor_scalar(NI, NI, 7, None, ALU.logical_shift_right))
            dve.op(lambda e: e.tensor_copy(NB, NI))
            dve.op(lambda e: e.tensor_copy(NTL, NB))
            c2, o2 = NB, NC
            for s_ in (1, 2, 4):
                dve.op(lambda e, s_=s_, c2=c2, o2=o2: e.tensor_copy(o2[:, 0:s_], c2[:, 0:s_]))
                dve.op(lambda e, s_=s_, c2=c2, o2=o2: e.tensor_tensor(o2[:, s_:8], c2[:, s_:8], c2[:, 0:8 - s_], ALU.add))
                c2, o2 = o2, c2
            yield 1
            i39 = CON[:, C_I39:C_I39 + NT * 8].rearrange("p (a b) -> p a b", b=8)
            dve.op(lambda e: e.tensor_tensor(CMP, i39, c2.unsqueeze(1).broadcast_to([128, NT, 8]), ALU.is_ge))
            dve.op(lambda e: e.tensor_reduce(ETF, CMP[:, :, 0:7], AX.X, ALU.add))
            t = dve.op(lambda e: e.tensor_scalar(ETK, ETF, float(WE1), None, ALU.mult))
            tk["et"] = t
            dve.op(lambda e: e.tensor_tensor(CMP, CMP, NTL.unsqueeze(1).broadcast_to([128, NT, 8]), ALU.mult))
            dve.op(lambda e: e.tensor_reduce(BLF, CMP, AX.X, ALU.add))
            dve.op(lambda e: e.tensor_tensor(BLF, i39[:, :, 0], BLF, ALU.subtract))
            dve.op(lambda e: e.scalar_tensor_tensor(out=BLF, in0=ETF, scalar=16.0, in1=BLF, op0=ALU.mult, op1=ALU.add))
            yield 1
            dve.op(lambda e: e.tensor_tensor(ETF, i39[:, :, 0], c2[:, 7:8].broadcast_to([128, NT]), ALU.is_ge))
            dve.op(lambda e: e.tensor_scalar(CMP[:, :, 0], BLF, -1.0, 128.0, ALU.mult, ALU.add))
            dve.op(lambda e: e.tensor_tensor(CMP[:, :, 0], CMP[:, :, 0], ETF, ALU.mult))
            dve.op(lambda e: e.tensor_tensor(BLF, BLF, CMP[:, :, 0], ALU.add))
            dve.op(lambda e: e.tensor_tensor(ETF[0:NT, :], BLF[0:NT, :], ident[0:NT, 0:NT], ALU.mult))
            dve.op(lambda e: e.tensor_reduce(BLF[0:NT, 0:1], ETF[0:NT, :], AX.X, ALU.add))
            t = dve.op(lambda e: e.tensor_copy(BLI[0:NT, :], BLF[0:NT, 0:1]))
            yield 1
            l_b = land("l_lb1")
            t = l_b.dma(pool, lambda e: e.indirect_dma_start(
                LB1, None, LIST1.rearrange("(a b) c -> a (b c)", b=128), bass.IndirectOffsetOnAxis(ap=BLI[0:NT, :], axis=0)), t, tk["list1"], t_init)
            tk["lands"] = LIST1_WAIT
            LB1v = LB1.rearrange("p (a b) -> p a b", b=2)

            def fl1(e):
                e.transpose(Q[0][:, 0:NT], LB1v[:, :, 0], ident[0:NT, 0:NT])
                return e.transpose(Q[0][:, 64:64 + NT], LB1v[:, :, 1], ident[0:NT, 0:NT])
            yield 1
            t = pe.op(fl1, t, q_free[0])
            yield 1
            tk["ids1"] = dve.op(lambda e: e.tensor_copy(IDI[:, 0:NT], Q[0][:, 0:NT]), t)
            tk["wsl1"] = dve.op(lambda e: e.tensor_copy(WSL[:, 0:NT], Q[0][:, 64:64 + NT]), t)
            fetch1(0)
            fetch1(1)
            yield 1

        NM = 6
        ups = [None, None]
        ss_free = [None, None]
        int_free = [t_one]
        ac_free = [[], []]
        py = [None, None]
        un = [0]
        l_ac1 = [land("l_ac10"), land("l_ac11")]

        def shared1(b):
            hi, lo = htr[b % 2]
            for m in range(NM):
                u = un[0] % 2
                un[0] += 1
                pg, pu = PB[2 * u], PB[2 * u + 1]

                def up_(ps, c):
                    return pe.op(lambda e: three(e, ps[:, :], [(SHI[:, k, c:c + 128], SLO[:, k, c:c + 128], hi[:, k, :], lo[:, k, :]) for k in range(4)]),
                                 t_sgu, tl[("ht", b)], ups[u], t_end0d, t_end0a, us=2.7)
                if m < 5:
                    t = up_(pg, m * 128)
                    ts = act.op(lambda e, u=u, pg=pg, m=m: e.activation(SS1[u], pg[:, :], ACT.Silu, bias=SB1[:, m:m + 1]), t, ss_free[u], t_s1, us=0.6)
                    yield 1
                    t = up_(pu, 640 + m * 128)
                    r0, ps = 0, pu
                else:
                    t = up_(pg, 1280)
                    ts = act.op(lambda e, u=u, pg=pg, m=m: e.activation(SS1[u][64:128, :], pg[0:64, :], ACT.Silu, bias=SB1[0:64, m:m + 1]), t, ss_free[u], t_s1, us=0.6)
                    r0, ps = 64, pg
                td = dve.op(lambda e, u=u, ps=ps, m=m, r0=r0: e.scalar_tensor_tensor(out=inter[r0:128, m, :], in0=ps[r0:128, :], scalar=SB1[r0:128, 6 + m:7 + m], in1=SS1[u][r0:128, :], op0=ALU.add, op1=ALU.mult), t, ts, int_free[0], us=0.7)
                ups[u] = td
                ss_free[u] = td
                yield 1
            ht_free[b % 2] = t
            tl[("up", b)] = t
            if b == 3:
                w1_columns(4, 2048, WE1, t, *rows1)
                tk["w1"] = w1_part(5, 8, t, *rows1)
            for j in range(4):
                def f(e, j=j):
                    for k in range(6):
                        kp = 128
                        r = e.matmul(PB[j][:, :], inter[0:kp, k, j * 128:(j + 1) * 128], SWD[0:kp, k, :], start=(k == 0), stop=(k == 5))
                    return r
                t = pe.op(f, td, t_swd, t_end0d, t_end0a, us=5.2)
                i = TILES[4 * b + j]
                py[j % 2] = dve.op(lambda e, j=j: e.scalar_tensor_tensor(out=AC1[j % 2], in0=PB[j][:, :], scalar=TG[:, 3:4], in1=xr[b][:, j, :], op0=ALU.mult, op1=ALU.add), t, *ac_free[j % 2], us=0.7)
                ups[j // 2] = py[j % 2]
                t_d = load(l_ac1[j % 2], sp, OUT[i * 128:(i + 1) * 128, :], AC1[j % 2], py[j % 2])
                accs1.append(t_d)
                ac_free[j % 2] = [t_d]
                yield 1
            int_free[0] = t
            if b == 0:
                load_x(2, py[1])
            yield 1

        g1_free = [None, None]
        st1 = {}

        def fetch1(n):
            st1[n] = [l_g[n % 2].dma(pool, lambda e: e.indirect_dma_start(
                G1[n % 2], None, HN2, bass.IndirectOffsetOnAxis(ap=IDI[:, n:n + 1], axis=0)), tk["ids1"], g1_free[n % 2], *rows1)]

        def norms():
            for b in range(4):
                yield from pre1(b)

        def attends():
            tk["rs3"] = yield from stats(ca, [xr[3][:, j, :] for j in range(4)], [t_xload[3]], True)
            for b in range(4):
                yield from attend(b)

        def shareds1():
            for b in range(4):
                while ("ht", b) not in tl:
                    yield 1
                if b == 3:
                    w1_columns(4, 0, 2048, (pe.sem, pe.count), (dve.sem, dve.count), (act.sem, act.count), *rows1)
                    w1_part(0, 4, (pe.sem, pe.count), (dve.sem, dve.count), (act.sem, act.count), *rows1)
                yield from shared1(b)

        merge(pe, GAP1, HOP1, (0, 0, norms()), (ATTEND_START, 1, attends()), (0, SHARED1_RANK, shareds1()), (0, SLOTS_RANK, slots()))
        t_ids1, t_wsl1, t_etk = tk["ids1"], tk["wsl1"], tk["et"]
        t_sh1 = (pe.sem, pe.count)
        t_sh1d = (dve.sem, dve.count)
        t_acc2, t_rows1 = accs1, rows1
        t_w1 = tk["w1"]

        xt_free = [t_sh1] * 2
        sl_free = [t_sh1] * 2
        inn_free = [t_sh1] * 2
        nt_free = [t_sh1] * 2
        ys_free = [t_sh1] * 3
        p_xt, p_it = t_sh1d, t_sh1d
        p_gu = [t_sh1d] * 2
        p_y = [t_sh1d] * 2
        st = st1
        t_add = None

        def turn1(n):
            nonlocal p_xt

            def f(e):
                for k in range(4):
                    r = e.transpose(PB[0][:, k * 128:(k + 1) * 128], G1[n % 2][:, k * 128:(k + 1) * 128], ident)
                return r
            t = pe.op(f, st[n][0], p_xt)
            g1_free[n % 2] = t
            p_xt = act.op(lambda e: e.activation(XT1[n % 2].rearrange("p a b -> p (a b)"), PB[0][:, :], ACT.Copy), t, xt_free[n % 2])
            st[n].append(p_xt)

        def up1(n, reg):
            pg, pu = PB[2 + 2 * (n % 2)], PB[3 + 2 * (n % 2)]

            def f(e):
                r0 = e.value_load(ETK[0:1, n:n + 1], min_val=0, max_val=7 * WE1)
                regs[n] = r0
                for q, ps in ((0, pg), (1, pu)):
                    for k in range(4):
                        r = e.matmul(ps[:, 0:I1], XT1[n % 2][:, k, :], W1[:, bass.ds(r0 + (q * 4 + k) * I1, I1)], start=(k == 0), stop=(k == 3))
                return r
            t = pe.op(f, st[n][1], p_gu[n % 2], t_w1, t_etk)
            xt_free[n % 2] = t
            table(SILU)
            ts = act.op(lambda e: e.activation(SL1[n % 2], pg[:, 0:I1], ACT.Silu), t, sl_free[n % 2])
            td = dve.op(lambda e: e.tensor_tensor(IN1[n % 2], SL1[n % 2], pu[:, 0:I1], ALU.mult), ts, inn_free[n % 2])
            sl_free[n % 2] = td
            p_gu[n % 2] = td
            st[n].append(td)

        def flip1(n):
            nonlocal p_it

            def f(e):
                for k in range(3):
                    w = 128 if k < 2 else 96
                    r = e.transpose(PB[1][0:w, k * 128:(k + 1) * 128], IN1[n % 2][:, k * 128:k * 128 + w], ident)
                return r
            t = pe.op(f, st[n][2], p_it)
            inn_free[n % 2] = t
            dve.op(lambda e: e.tensor_copy(NT1[n % 2][:, 0:2, :].rearrange("p a b -> p (a b)"), PB[1][:, 0:256]), t, nt_free[n % 2])
            p_it = dve.op(lambda e: e.tensor_copy(NT1[n % 2][0:96, 2, :], PB[1][0:96, 256:384]), t, nt_free[n % 2])
            st[n].append(p_it)

        def down_1(n):
            nonlocal t_add

            def f(e):
                r0 = regs[n]
                for k in range(3):
                    w = 128 if k < 2 else 96
                    r = e.matmul(PB[6 + n % 2][:, :], NT1[n % 2][0:w, k, :], W1[0:w, bass.ds(r0 + 8 * I1 + k * 512, 512)], start=(k == 0), stop=(k == 2))
                return r
            t = pe.op(f, st[n][3], p_y[n % 2])
            nt_free[n % 2] = t
            ty = act.op(lambda e: e.activation(YS1[n % 3], PB[6 + n % 2][:, :], ACT.Copy, scale=WSL[:, n:n + 1]), t, ys_free[n % 3], t_wsl1)
            p_y[n % 2] = ty
            t_add = l_add[0].dma(pool, lambda e: e.indirect_dma_start(
                OUT, bass.IndirectOffsetOnAxis(ap=IDI[:, n:n + 1], axis=0), YS1[n % 3], None, compute_op=ALU.add, bounds_check=2047, oob_is_err=False), ty, t_add, *t_acc2)
            ys_free[n % 3] = t_add

        regs = {}
        turn1(0)
        for n in range(NT):
            up1(n, None)
            if n + 1 < NT:
                turn1(n + 1)
            if n + 2 < NT:
                fetch1(n + 2)
            if n:
                down_1(n - 1)
            flip1(n)
        down_1(NT - 1)

        sp.op(lambda e: e.wait_ge(l_add[0].sem, l_add[0].count) or e, sig=False)

        @block.tensor
        def _(e):
            pe.play(e)

        @block.vector
        def _(e):
            dve.play(e)

        @block.scalar
        def _(e):
            act.play(e)

        @block.gpsimd
        def _(e):
            pool.play(e)

        @block.sync
        def _(e):
            sp.play(e)


def kernel(**inp):
    import concourse.bacc as bacc
    from concourse.bass_utils import run_bass_kernel_spmd as run
    v = {k: np.asarray(x) for k, x in inp.items()}

    def cols(w):
        c, n = w.shape[-2:]
        t = -(-c // 128)
        w = np.concatenate([w, np.zeros(w.shape[:-2] + (t * 128 - c, n), w.dtype)], axis=-2)
        w = w.reshape(w.shape[:-2] + (t, 128, n))
        w = np.swapaxes(w, -3, -2)
        return w.reshape(w.shape[:-2] + (t * n,))

    sw = np.swapaxes
    we0 = np.concatenate([cols(sw(v["L0_ffn_w_gate"], 1, 2)), cols(sw(v["L0_ffn_w_up"], 1, 2)), cols(sw(v["L0_ffn_w_down"], 1, 2))], axis=-1)
    sw0 = np.concatenate([cols(v["L0_ffn_sg"].T), cols(v["L0_ffn_su"].T), cols(v["L0_ffn_sd"].T)], axis=-1)
    we1 = np.concatenate([cols(v["L1_ffn_gate_w"]), cols(v["L1_ffn_up_w"]), cols(v["L1_ffn_down_w"])], axis=-1)
    sd1 = np.zeros((768, D), np.float32)
    m5 = 5 * 128
    sd1[0:m5] = v["L1_ffn_s_down_w"][0:m5]
    sd1[m5] = v["L1_ffn_s_down_b"]
    sd1[m5 + 64:] = v["L1_ffn_s_down_w"][m5:]
    sb1 = np.zeros((2, 768), np.float32)
    sb1[0, 0:SI] = v["L1_ffn_s_gate_b"]
    sb1[1, 0:m5] = v["L1_ffn_s_up_b"][0:m5]
    sb1[1, m5 + 64:] = v["L1_ffn_s_up_b"][m5:]
    sg, su = v["L1_ffn_s_gate_w"], v["L1_ffn_s_up_w"]
    sgu1 = np.concatenate([sg[:, 0:m5], su[:, 0:m5], sg[:, m5:], su[:, m5:]], axis=1)
    con, l0, l1 = constants()

    def kp(w):
        return w.reshape(4, 128, -1).transpose(1, 0, 2)
    arrays = {
        "x": v["x"], "ctx": v["ctx_2048"], "itok": v["itok_Sx4_0_63"],
        "g": np.broadcast_to(np.concatenate([v["g_xattn"], v["g_ffn"]])[None, :], (128, 4)),
        "descT": kp(v["L0_xattn_desc_router"].T), "wq": v["L0_xattn_W_q"],
        "bq": v["L0_xattn_b_q"].reshape(4, 128).T,
        "rw0": kp(v["L0_ffn_gate_w"].T), "bias": np.broadcast_to(v["L0_ffn_bias"][None, :], (128, E0)),
        "we0": we0, "sw0": sw0, "rw1": kp(v["L1_ffn_router_w"].T), "we1": we1,
        "sgu1": sgu1, "sd1": sd1,
        "sb1": sb1.reshape(2, 6, 128).transpose(2, 0, 1).reshape(128, 12),
        "con": con, "l0": l0, "l1": l1, "zero": np.zeros((ROWS - 2048, D), np.float32),
    }
    nc = bacc.Bacc("TRN2", target_bir_lowering=False, num_devices=1)
    given, aps = {}, {}
    for name, x in arrays.items():
        x = np.ascontiguousarray(x)
        given[f"in_{name}"] = x
        aps[name] = nc.dram_tensor(f"in_{name}", x.shape, mybir.dt.from_np(x.dtype), kind="ExternalInput").ap()
    o = nc.dram_tensor("out_0", (4, 512, 512), F32, kind="ExternalOutput").ap()
    program(nc, aps, o)
    r = run(nc, [given], core_ids=[0])
    return r.results[0]["out_0"]
```
